# Optimizing a Trainium2 kernel written in Bass

```python
import numpy as np
import jax
import jax.numpy as jnp

def _softmax(x, axis=-1):
    return jax.nn.softmax(x, axis=axis)

def _gelu(x):
    return jax.nn.gelu(x, approximate=True)

def _silu(x):
    return jax.nn.silu(x)

def _sigmoid(x):
    return jax.nn.sigmoid(x)

def _layernorm(x, axis=-1, eps=1e-05):
    m = jnp.mean(x, axis=axis, keepdims=True)
    v = jnp.var(x, axis=axis, keepdims=True)
    return (x - m) / jnp.sqrt(v + eps)

def _scatter_add(tgt, idx, src, axis=0):
    return tgt.at[idx].add(src)

def _segment_sum(src, seg, n):
    return jax.ops.segment_sum(src, seg, n)
kernel_name = 'mk_adaln_d1_jaxref_r8_604416'

def setup_inputs(seed: int=0):
    np.random.seed(seed)
    _w = jnp.asarray

    def _L0_attn_setup():
        import jax, jax.numpy as jnp
        import numpy as np
        _J6 = jnp.array([[0, 0, 0, 0, 0, 1], [0, 0, 0, 0, -1, 0], [0, 0, 0, 1, 0, 0], [0, 0, 1, 0, 0, 0], [0, -1, 0, 0, 0, 0], [1, 0, 0, 0, 0, 0]], dtype=jnp.float32)
        _PI = jnp.array([0, 0, 0, 1, 1, 2])
        _PJ = jnp.array([1, 2, 3, 2, 3, 3])

        def exterior(p1, p2):
            L = p1[..., _PI] * p2[..., _PJ] - p1[..., _PJ] * p2[..., _PI]
            n = jnp.clip(jnp.linalg.norm(L, axis=-1, keepdims=True), 1e-12)
            return L / n
        key = jax.random.key(seed)
        ks = jax.random.split(key, 8)
        B, T, D, H = (2, 256, 128, 16)
        pd = 4
        s = 0.02
        return {'x': jax.random.normal(ks[0], (B, T, D), jnp.float32), 'w_qkv': jax.random.normal(ks[1], (3 * D, D), jnp.float32) * s, 'b_qkv': jnp.zeros((3 * D,), jnp.float32), 'w1_write': jax.random.normal(ks[2], (pd * H, D), jnp.float32) * s, 'w2_write': jax.random.normal(ks[3], (pd * H, D), jnp.float32) * s, 'w1_read': jax.random.normal(ks[4], (pd * H, D), jnp.float32) * s, 'w2_read': jax.random.normal(ks[5], (pd * H, D), jnp.float32) * s, 'w_out': jax.random.normal(ks[6], (D, D), jnp.float32) * s, 'b_out': jnp.zeros((D,), jnp.float32), 'decay_logits': jnp.full((H,), 4.6, jnp.float32), 'bias_scale': jnp.full((H,), 0.1, jnp.float32)}
    _L0_attn_in = _L0_attn_setup()

    def _L0_ffn_setup():
        import jax, jax.numpy as jnp
        import numpy as np
        E = 8
        TOP_K = 2
        D = 128
        H = 2 * D
        key = jax.random.key(seed)
        k0, k1, k2, k3, k4 = jax.random.split(key, 5)
        scale = 0.02
        x = jax.random.normal(k0, (4, 256, D), dtype=jnp.float32)
        Wg = jax.random.normal(k1, (D, E), dtype=jnp.float32) * scale
        W1 = jax.random.normal(k2, (E, D, H), dtype=jnp.float32) * scale
        W2 = jax.random.normal(k3, (E, D, H), dtype=jnp.float32) * scale
        W3 = jax.random.normal(k4, (E, H, D), dtype=jnp.float32) * scale
        return {'x': x, 'Wg': Wg, 'W1': W1, 'W2': W2, 'W3': W3}
    _L0_ffn_in = _L0_ffn_setup()
    _L0_c = _w((lambda *s: np.random.randn(*s).astype(np.float32) * 0.05)(32, 128))
    _L0_wmod = _w((lambda *s: np.random.randn(*s).astype(np.float32) * 0.05)(128, 6 * 128) * 128 ** (-0.5))
    _d = {'L0_attn_x': _L0_attn_in['x'], 'L0_attn_w_qkv': _L0_attn_in['w_qkv'], 'L0_attn_b_qkv': _L0_attn_in['b_qkv'], 'L0_attn_w1_write': _L0_attn_in['w1_write'], 'L0_attn_w2_write': _L0_attn_in['w2_write'], 'L0_attn_w1_read': _L0_attn_in['w1_read'], 'L0_attn_w2_read': _L0_attn_in['w2_read'], 'L0_attn_w_out': _L0_attn_in['w_out'], 'L0_attn_b_out': _L0_attn_in['b_out'], 'L0_attn_decay_logits': _L0_attn_in['decay_logits'], 'L0_attn_bias_scale': _L0_attn_in['bias_scale'], 'L0_ffn_Wg': _L0_ffn_in['Wg'], 'L0_ffn_W1': _L0_ffn_in['W1'], 'L0_ffn_W2': _L0_ffn_in['W2'], 'L0_ffn_W3': _L0_ffn_in['W3'], 'L0_c': _L0_c, 'L0_wmod': _L0_wmod}
    _x0 = _d['L0_attn_x']
    _d['L0_attn_x'] = jax.random.normal(jax.random.fold_in(jax.random.key(seed), 1), (32, 256, 128), dtype=_x0.dtype)
    del _x0
    return _d

def reference(L0_attn_x, L0_attn_w_qkv, L0_attn_b_qkv, L0_attn_w1_write, L0_attn_w2_write, L0_attn_w1_read, L0_attn_w2_read, L0_attn_w_out, L0_attn_b_out, L0_attn_decay_logits, L0_attn_bias_scale, L0_ffn_Wg, L0_ffn_W1, L0_ffn_W2, L0_ffn_W3, L0_c, L0_wmod):

    def _L0_attn_ref(x, w_qkv, b_qkv, w1_write, w2_write, w1_read, w2_read, w_out, b_out, decay_logits, bias_scale):
        import jax, jax.numpy as jnp
        import numpy as np
        _J6 = jnp.array([[0, 0, 0, 0, 0, 1], [0, 0, 0, 0, -1, 0], [0, 0, 0, 1, 0, 0], [0, 0, 1, 0, 0, 0], [0, -1, 0, 0, 0, 0], [1, 0, 0, 0, 0, 0]], dtype=jnp.float32)
        _PI = jnp.array([0, 0, 0, 1, 1, 2])
        _PJ = jnp.array([1, 2, 3, 2, 3, 3])

        def exterior(p1, p2):
            L = p1[..., _PI] * p2[..., _PJ] - p1[..., _PJ] * p2[..., _PI]
            n = jnp.clip(jnp.linalg.norm(L, axis=-1, keepdims=True), 1e-12)
            return L / n
        B, T, D = x.shape
        H = decay_logits.shape[0]
        dh = D // H
        pd = w1_write.shape[0] // H
        scale = dh ** (-0.5)
        qkv = (x @ w_qkv.T + b_qkv).reshape(B, T, 3, H, dh)
        qkv = jnp.transpose(qkv, (2, 0, 3, 1, 4))
        q, k, v = (qkv[0], qkv[1], qkv[2])
        std_logits = jnp.einsum('bhqd,bhkd->bhqk', q, k) * scale
        x_prev = jnp.concatenate([jnp.zeros((B, 1, D), x.dtype), x[:, :-1]], axis=1)
        w1 = (x_prev @ w1_write.T).reshape(B, T, H, pd)
        w2 = (x @ w2_write.T).reshape(B, T, H, pd)
        write_lines = exterior(w1, w2)
        r1 = (x @ w1_read.T).reshape(B, T, H, pd)
        r2 = (x @ w2_read.T).reshape(B, T, H, pd)
        read_lines = exterior(r1, r2)
        J_write = jnp.einsum('bthi,ij->bthj', write_lines, _J6)
        incidence = jnp.einsum('bqhp,bkhp->bhqk', read_lines, J_write)
        decays = jax.nn.sigmoid(decay_logits)
        pos = jnp.arange(T, dtype=x.dtype)
        diffs = pos[:, None] - pos[None, :]
        past = diffs > 0
        diffs_pos = jnp.where(past, diffs, 0.0)
        weights = decays[:, None, None] ** diffs_pos[None] * past[None].astype(x.dtype)
        bias = incidence * weights[None] * bias_scale[None, :, None, None]
        logits = std_logits + bias
        causal_mask = diffs < 0
        logits = jnp.where(causal_mask[None, None], -jnp.inf, logits)
        attn = jax.nn.softmax(logits, axis=-1)
        out = jnp.einsum('bhqk,bhkd->bqhd', attn, v).reshape(B, T, D)
        return out @ w_out.T + b_out

    def _L0_ffn_ref(x, Wg, W1, W2, W3):
        import jax, jax.numpy as jnp
        import numpy as np
        E = 8
        TOP_K = 2
        D = 128
        H = 2 * D
        logits = jnp.einsum('bsd,de->bse', x, Wg)
        top_vals, top_idx = jax.lax.top_k(logits, TOP_K)
        probs = jax.nn.softmax(top_vals, axis=-1)
        onehot = jax.nn.one_hot(top_idx, E, dtype=x.dtype)
        weights = jnp.einsum('bsk,bske->bse', probs, onehot)
        out = jnp.zeros_like(x)
        for e in range(E):
            u = jnp.einsum('bsd,dh->bsh', x, W1[e])
            v = jnp.einsum('bsd,dh->bsh', x, W2[e])
            h = u * jax.nn.sigmoid(u) * v
            y = jnp.einsum('bsh,hd->bsd', h, W3[e])
            out = out + y * weights[..., e][..., None]
        return out
    x = L0_attn_x
    mod = (_silu(L0_c) @ L0_wmod).reshape(L0_c.shape[0], 6, 1, -1)
    sa, ca, ga, sb, cb, gb = (mod[:, 0], mod[:, 1], mod[:, 2], mod[:, 3], mod[:, 4], mod[:, 5])
    ga = (2 * (ga >= 0) - 1) * jnp.maximum(jnp.abs(ga), 0.25)
    gb = (2 * (gb >= 0) - 1) * jnp.maximum(jnp.abs(gb), 0.25)
    h = _layernorm(x, axis=-1) * (1 + ca) + sa
    x = x + ga * _L0_attn_ref(h, L0_attn_w_qkv, L0_attn_b_qkv, L0_attn_w1_write, L0_attn_w2_write, L0_attn_w1_read, L0_attn_w2_read, L0_attn_w_out, L0_attn_b_out, L0_attn_decay_logits, L0_attn_bias_scale)
    h = _layernorm(x, axis=-1) * (1 + cb) + sb
    x = x + gb * _L0_ffn_ref(h, L0_ffn_Wg, L0_ffn_W1, L0_ffn_W2, L0_ffn_W3)
    return x

_drawn_inputs = setup_inputs


def setup_inputs(seed=0):
    import zlib

    import numpy as np

    out = dict(_drawn_inputs(seed))
    spreads = {'L0_attn_b_qkv': (0.0, 0.8),
     'L0_attn_b_out': (0.0, 0.341),
     'L0_attn_decay_logits': (4.599999904632568, 0.6),
     'L0_attn_bias_scale': (0.10000000149011612, 0.6)}
    factors = {'L0_attn_w_qkv': 8.0,
     'L0_attn_w1_write': 8.0,
     'L0_attn_w2_write': 8.0,
     'L0_attn_w1_read': 8.0,
     'L0_attn_w2_read': 8.0,
     'L0_attn_w_out': 7.887,
     'L0_ffn_Wg': 8.0,
     'L0_ffn_W1': 8.0,
     'L0_ffn_W2': 8.0,
     'L0_ffn_W3': 8.0}
    for name, (base, spread) in spreads.items():
        noise = np.random.default_rng([zlib.crc32(name.encode()), seed]).standard_normal(out[name].shape)
        drawn = base * np.exp(spread * noise) if base else spread * noise
        out[name] = jnp.asarray(drawn.astype(out[name].dtype))
    for name, factor in factors.items():
        out[name] = (out[name] * factor).astype(out[name].dtype)
    return out
```

```python
import concourse.bass as bass
from concourse import mybir
from contextlib import ExitStack

fp32 = mybir.dt.float32
f32r = mybir.dt.float32r
bf16 = mybir.dt.bfloat16
i32 = mybir.dt.int32
u32 = mybir.dt.uint32
ALU = mybir.AluOpType
ACT = mybir.ActivationFunctionType
AX = mybir.AxisListType

P = 128
NB, T, D = 32, 256, 128
H, DH, PD = 16, 8, 4
NT = T // P
E, HF = 8, 256
NF = 4
NV = DH + 6 + 6
GR = 64
SCALE = float(DH) ** -0.5
EPS = 1e-5
MASK = -1e30


class Signal:

    def __init__(self, sem, per):
        self.sem, self.per = sem, per


def wait(eng, signal, batch, k=None):
    value = batch * signal.per + (signal.per if k is None else k)
    if not isinstance(value, int) or value > 0:
        eng.wait_ge(signal.sem, value)


def settle(eng, settled):
    eng.sem_inc(settled, 1)


JOBS = [
    (0, "route", -2, 1),
    (1, "k0", 1, 0), (1, "q0", 1, 1), (1, "head1", -1, 0),
    (2, "norm", 2, 1), (2, "k1", 1, 0), (2, "q1", 1, 1), (2, "attnT", -1, 0),
    (3, "max1", 0, 1), (3, "qkv0", 2, 0), (3, "line0", 2, 1),
    (4, "out", -1, 0), (4, "qkv1", 2, 1), (4, "line1", 2, 0),
    (5, "k2", 1, 1), (5, "q2", 1, 0), (5, "head0", 0, 1), (5, "res", -1, 0),
    (6, "k3", 1, 1), (6, "q3", 1, 0),
    (7, "norm2", -1, 1), (7, "max0", 1, 0),
]
BANK = {name: bank for _, name, _, bank in JOBS}


def span(start, count):
    return slice(start, start + count) if isinstance(start, int) else bass.ds(start, count)


def one(batch):
    return span(batch, 1)


def live(batch):
    return not isinstance(batch, int) or 0 <= batch < NB


def before(n, b):
    bank, m = JOBS[n][3], n
    while True:
        m -= 1
        if m < 0:
            m, b = len(JOBS) - 1, b - 1
        if JOBS[m][3] == bank and live(b + JOBS[m][2]):
            return JOBS[m][1], b + JOBS[m][2]
        if isinstance(b, int) and b < -3:
            return None


def iterations(engine, body):
    for b in (-2, -1, 0, 1):
        body(b, b % 2)
    with engine.Fori(1, NB // 2 - 1) as i:
        body(i * 2, 0)
        body(i * 2 + 1, 1)
    for b in (NB - 2, NB - 1, NB, NB + 1):
        body(b, b % 2)


def pair_heads(p):
    g = p % 2
    return g, [(4 * (p // 2) + g + 2 * n, 2 * (p // 2) + n) for n in range(2)]


def build(nc, x, w_qkv, b_qkv, w1_write, w2_write, w1_read, w2_read, w_out, b_out,
          decay_logits, bias_scale, Wg, W1, W2, W3, c, wmod, out):
    with ExitStack() as whole:
        def sb(stack, name, shape, dt=fp32):
            return stack.enter_context(nc.sbuf_tensor(name, shape, dt))

        def sem(name):
            return whole.enter_context(nc.semaphore(name))

        def signal(name, per=1):
            return Signal(sem(name), per)

        x_all = sb(whole, "x_all", [P, NB * NT * D])
        h2_all = sb(whole, "h2_all", [P, NB * T])
        route_w = sb(whole, "route_w", [P, NB * NT * E])
        mod = sb(whole, "mod", [P, 6, NB])
        ident = sb(whole, "ident", [P, P])
        ones = sb(whole, "ones", [P, P])

        attention = whole.enter_context(ExitStack())
        a = lambda name, shape, dt=fp32: sb(attention, name, shape, dt)
        w_proj = a("w_proj", [P, 640])
        w_outT = a("w_outT", [P, P])
        bias_qkv = a("bias_qkv", [P, 3 * D])
        gate_bias = a("gate_bias", [P, NB])
        wg_sb = a("wg_sb", [P, E])
        identb = a("identb", [P, P], bf16)
        causal = a("causal", [P, 3 * P], bf16)
        decay = a("decay", [P, H, P])
        decay_q = a("decay_q", [P, H])
        decay_k = a("decay_k", [P, H])
        bscale = a("bscale", [P, H])
        pick = a("pick", [P, 8, P], f32r)
        keep_f = a("keep_f", [P, 1])
        keep_i = a("keep_i", [P, 1])
        iota8 = a("iota8", [P, E])
        neg_half = a("neg_half", [P, 2 * NT * H])

        setup(nc, ExitStack(), sem, sb, locals())
        attend(nc, whole, attention, sb, sem, signal, locals())
        attention.close()
        experts(nc, whole, sb, sem, signal, locals())


def setup(nc, stack, sem, sb, v):
    x, mod, ident, ones = v["x"], v["mod"], v["ident"], v["ones"]
    w_proj, decay = v["w_proj"], v["decay"]
    with stack:
        s = lambda name, shape, dt=fp32: sb(stack, name, shape, dt)
        wq_raw = s("wq_raw", [P, 3, D])
        wl_raw = s("wl_raw", [PD * H, 4, D])
        wo_raw = s("wo_raw", [P, D])
        c_raw = s("c_raw", [NB, D])
        wmod_sb = s("wmod_sb", [P, 6 * D])
        bout = s("bout", [P, 1])
        logit = s("logit", [P, H])
        az = s("az", [P, H]); ez = s("ez", [P, H]); lz = s("lz", [P, H]); lam = s("lam", [P, H]); lam2 = s("lam2", [P, H])
        silu_c = s("silu_c", [P, NB])
        dist_i = s("dist_i", [P, P], i32); dist = s("dist", [P, P])
        col_i = s("col_i", [P, 1], i32); col = s("col", [P, 1]); rcol = s("rcol", [P, 1])
        e_i = s("e_i", [P, E], i32)
        mask0 = s("mask0", [P, 3 * P]); mask1 = s("mask1", [P, 3 * P])
        pick0 = s("pick0", [P, 8, P]); pick1 = s("pick1", [P, 8, P])
        kf = [s(f"kf{n}", [P, 1]) for n in range(7)]
        ga_abs = s("ga_abs", [P, 2, NB]); ga_sign = s("ga_sign", [P, 2, NB]); ga_two = s("ga_two", [P, 2, NB])
        tA = stack.enter_context(nc.psum_tensor("tA", [P, 512], fp32))
        tB = stack.enter_context(nc.psum_tensor("tB", [P, 512], fp32))
        tC = stack.enter_context(nc.psum_tensor("tC", [P, 512], fp32))

        ld_w, ld_c, ld_v, ld_x, ld_d = (sem(n) for n in ("ld_w", "ld_c", "ld_v", "ld_x", "ld_d"))
        pool_step, ident_ok, dist_ok, cols_ok = (sem(n) for n in ("pool_step", "ident_ok", "dist_ok", "cols_ok"))
        wT_ok, cT_ok, silu_ok, mod_ok, modded = (sem(n) for n in ("wT_ok", "cT_ok", "silu_ok", "mod_ok", "modded"))
        az_ok, ln_ok, lam_ok, arg_ok, exp_ok = (sem(n) for n in ("az_ok", "ln_ok", "lam_ok", "arg_ok", "exp_ok"))
        dve_step, act_step, setup_done = sem("dve_step"), sem("act_step"), sem("setup_done")
        xd = x.rearrange("b (t p) d -> p (b t) d", p=P)

        with nc.Block() as block:
            @block.sync
            def _(sp):
                sp.dma_start(wq_raw[:], v["w_qkv"].rearrange("(m p) d -> p m d", p=P)).then_inc(ld_w, 16)
                for n, w in enumerate(("w2_write", "w1_read", "w2_read", "w1_write")):
                    sp.dma_start(wl_raw[:, n, :], v[w]).then_inc(ld_w, 16)
                sp.dma_start(wo_raw[:], v["w_out"]).then_inc(ld_w, 16)
                for n in range(8):
                    k = NB * NT // 8
                    sp.dma_start(v["x_all"][:, n * k * D:(n + 1) * k * D].rearrange("p (n d) -> p n d", d=D), xd[:, n * k:(n + 1) * k, :]).then_inc(ld_x, 16)
                sp.wait_ge(ld_x, 128)

            @block.gpsimd
            def _(pool):
                n = [0]

                def step(ins):
                    ins.then_inc(pool_step, 1)
                    n[0] += 1
                    pool.wait_ge(pool_step, n[0])

                step(nc.gpsimd.memset(ident[:], 0.0))
                nc.gpsimd.affine_select(out=ident[:], in_=ident[:], compare_op=ALU.not_equal, fill=1.0, base=0,
                                        pattern=[[-1, P]], channel_multiplier=1).then_inc(ident_ok, 1)
                step(nc.gpsimd.iota(dist_i[:], pattern=[[1, P]], base=0, channel_multiplier=-1))
                nc.gpsimd.tensor_scalar(dist[:], dist_i[:], 0.0, None, ALU.max).then_inc(dist_ok, 1)
                step(nc.gpsimd.iota(col_i[:], pattern=[[0, 1]], base=0, channel_multiplier=1))
                step(nc.gpsimd.tensor_copy(col[:], col_i[:]))
                nc.gpsimd.tensor_scalar(rcol[:], col[:], -1.0, float(P), ALU.mult, ALU.add).then_inc(cols_ok, 1)
                step(nc.gpsimd.iota(e_i[:], pattern=[[1, E]], base=0, channel_multiplier=0))
                nc.gpsimd.tensor_copy(v["iota8"][:], e_i[:])
                nc.gpsimd.memset(v["neg_half"][:], -0.5)
                nc.gpsimd.memset(ones[:], 1.0)
                step(nc.gpsimd.memset(mask0[:], 0.0))
                step(nc.gpsimd.tensor_copy(mask1[:], mask0[:]))
                for k in (0, 2):
                    step(nc.gpsimd.affine_select(out=mask1[:, k * P:(k + 1) * P], in_=mask0[:, 0:P],
                                                 compare_op=ALU.is_ge, fill=MASK, base=0,
                                                 pattern=[[-1, P]], channel_multiplier=1))
                nc.gpsimd.tensor_copy(v["causal"][:], mask1[:])
                step(nc.gpsimd.memset(pick0[:], 0.0))
                step(nc.gpsimd.affine_select(out=pick1[:], in_=pick0[:], compare_op=ALU.not_equal, fill=1.0, base=0,
                                             pattern=[[-1, 8], [0, P]], channel_multiplier=1))
                step(nc.gpsimd.affine_select(out=pick0[:], in_=pick1[:], compare_op=ALU.not_equal, fill=1.0, base=-GR,
                                             pattern=[[-1, 8], [0, P]], channel_multiplier=1))
                nc.gpsimd.tensor_copy(v["pick"][:], pick0[:])
                step(nc.gpsimd.tensor_scalar(kf[0][:], col[:], float(GR), float(-GR), ALU.is_ge, ALU.mult))
                step(nc.gpsimd.tensor_tensor(kf[1][:], col[:], kf[0][:], ALU.add))
                for k in range(3):
                    src = kf[1 + k]
                    step(nc.gpsimd.tensor_scalar(kf[5][:], src[:], float(NV), float(-NV), ALU.is_ge, ALU.mult))
                    step(nc.gpsimd.tensor_tensor(kf[2 + k][:], src[:], kf[5][:], ALU.add))
                nc.gpsimd.tensor_scalar(v["keep_f"][:], kf[4][:], float(DH + 6), None, ALU.is_lt)
                nc.gpsimd.tensor_scalar(v["keep_i"][:], kf[4][:], float(DH + 6), None, ALU.is_ge)
                nc.gpsimd.wait_ge(ident_ok, 1)
                nc.gpsimd.tensor_copy(v["identb"][:], ident[:]).then_inc(pool_step, 1)
                pool.wait_ge(exp_ok, 1)
                nc.gpsimd.affine_select(out=decay[:], in_=decay[:], compare_op=ALU.is_gt, fill=0.0, base=0,
                                        pattern=[[0, H], [1, P]], channel_multiplier=-1).then_inc(setup_done, 1)
                pool.wait_ge(setup_done, 1)

            @block.tensor
            def _(pe):
                pe.wait_ge(ident_ok, 1)
                pe.wait_ge(ld_c, 16 * 2)
                nc.tensor.transpose(tC[:, 256:256 + NB], c_raw[:], ident[0:NB, 0:NB]).then_inc(cT_ok, 1)
                pe.wait_ge(ld_w, 16 * 6)
                for m in range(3):
                    nc.tensor.transpose(tA[:, m * P:(m + 1) * P], wq_raw[:, m, :], ident[:])
                nc.tensor.transpose(tA[:, 3 * P:4 * P], wo_raw[:], ident[:])
                for n in range(4):
                    last = nc.tensor.transpose(tB[:, n * 64:(n + 1) * 64], wl_raw[:, n, :], ident[0:64, 0:64])
                last.then_inc(wT_ok, 1)
                pe.wait_ge(silu_ok, 1)
                for m in range(6):
                    last = nc.tensor.matmul(tC[:, m * NB:(m + 1) * NB], wmod_sb[:, m * D:(m + 1) * D], silu_c[:],
                                            start=True, stop=True)
                last.then_inc(mod_ok, 1)

            @block.scalar
            def _(act):
                act.dma_start(c_raw[:], v["c"]).then_inc(ld_c, 16)
                act.dma_start(wmod_sb[:], v["wmod"]).then_inc(ld_c, 16)
                act.dma_start(logit[:], v["decay_logits"].rearrange("(a n) -> a n", a=1).broadcast_to([P, H])).then_inc(ld_d, 16)
                act.dma_start(v["bscale"][:], v["bias_scale"].rearrange("(a n) -> a n", a=1).broadcast_to([P, H])).then_inc(ld_v, 16)
                act.dma_start(v["bias_qkv"][:], v["b_qkv"].rearrange("(a n) -> a n", a=1).broadcast_to([P, 3 * D])).then_inc(ld_v, 16)
                act.dma_start(bout[:], v["b_out"].rearrange("(p a) -> p a", a=1)).then_inc(ld_v, 16)
                act.dma_start(v["wg_sb"][:], v["Wg"]).then_inc(ld_v, 16)
                act.wait_ge(cT_ok, 1)
                nc.scalar.activation(silu_c[:], tC[:, 256:256 + NB], ACT.Silu).then_inc(silu_ok, 1)
                act.wait_ge(az_ok, 1)
                nc.scalar.activation(ez[:], az[:], ACT.Exp, scale=-1.0).then_inc(act_step, 1)
                act.wait_ge(act_step, 1)
                nc.scalar.activation(lz[:], ez[:], ACT.Ln, bias=1.0).then_inc(ln_ok, 1)
                act.wait_ge(arg_ok, 1)
                nc.scalar.activation(v["decay_q"][:], v["decay_q"][:], ACT.Exp).then_inc(act_step, 1)
                nc.scalar.activation(v["decay_k"][:], v["decay_k"][:], ACT.Exp).then_inc(act_step, 1)
                nc.scalar.activation(decay[:], decay[:], ACT.Exp).then_inc(exp_ok, 1)
                act.wait_ge(ld_v, 64)

            @block.vector
            def _(dve):
                n = [0]

                def step(ins):
                    ins.then_inc(dve_step, 1)
                    n[0] += 1
                    dve.wait_ge(dve_step, n[0])

                dve.wait_ge(ld_d, 16)
                step(nc.vector.tensor_scalar(lam2[:], logit[:], -1.0, None, ALU.mult))
                nc.vector.tensor_tensor(az[:], logit[:], lam2[:], ALU.max).then_inc(az_ok, 1)
                dve.wait_ge(wT_ok, 1)
                nc.vector.tensor_scalar(w_proj[:, 0:P], tA[:, 0:P], SCALE, None, ALU.mult)
                nc.vector.tensor_copy(w_proj[:, P:3 * P], tA[:, P:3 * P])
                nc.vector.tensor_copy(v["w_outT"][:], tA[:, 3 * P:4 * P])
                for n4, rev in enumerate((True, False, False, True)):
                    dst = w_proj[:, 384 + 64 * n4:448 + 64 * n4].rearrange("p (h i) -> p h i", i=PD)
                    src = tB[:, 64 * n4:64 * n4 + 64].rearrange("p (h i) -> p h i", i=PD)
                    for i in range(PD):
                        nc.vector.tensor_copy(dst[:, :, i], src[:, :, PD - 1 - i if rev else i])
                dve.wait_ge(ld_v, 64)
                nc.vector.tensor_scalar(v["bias_qkv"][:, 0:D], v["bias_qkv"][:, 0:D], SCALE, None, ALU.mult)
                dve.wait_ge(ln_ok, 1)
                step(nc.vector.scalar_tensor_tensor(out=lam[:], in0=lam2[:], scalar=0.0, in1=lz[:], op0=ALU.max, op1=ALU.add))
                step(nc.vector.tensor_scalar(ez[:], lam[:], -1.0, None, ALU.mult))
                dve.wait_ge(dist_ok, 1)
                dve.wait_ge(cols_ok, 1)
                nc.vector.tensor_scalar(v["decay_q"][:], ez[:], col[:], None, ALU.mult)
                nc.vector.tensor_scalar(v["decay_k"][:], ez[:], rcol[:], None, ALU.mult)
                for h in range(H):
                    last = nc.vector.tensor_scalar(decay[:, h, :], dist[:], ez[:, h:h + 1], None, ALU.mult)
                last.then_inc(arg_ok, 1)
                dve.wait_ge(mod_ok, 1)
                step(nc.vector.tensor_copy(mod[:], tC[:, 0:6 * NB].rearrange("p (m b) -> p m b", b=NB)))
                for m in (1, 4):
                    nc.vector.tensor_scalar(mod[:, m, :], mod[:, m, :], 1.0, None, ALU.add)
                gates = mod[:, 2:6:3, :]
                nc.vector.tensor_scalar(ga_sign[:], gates, 0.0, 2.0, ALU.is_ge, ALU.mult)
                step(nc.vector.tensor_scalar(ga_two[:], gates, -1.0, None, ALU.mult))
                step(nc.vector.tensor_tensor(ga_abs[:], ga_two[:], gates, ALU.max))
                step(nc.vector.tensor_scalar(ga_two[:], ga_abs[:], 0.25, None, ALU.max))
                step(nc.vector.tensor_scalar(ga_abs[:], ga_sign[:], 1.0, None, ALU.subtract))
                step(nc.vector.tensor_tensor(gates, ga_abs[:], ga_two[:], ALU.mult))
                step(nc.vector.tensor_scalar(v["gate_bias"][:], mod[:, 2, :], bout[:], None, ALU.mult))


def attend(nc, whole, stack, sb, sem, signal, v):
    x_all, h2_all, mod, ident = v["x_all"], v["h2_all"], v["mod"], v["ident"]
    w_proj, w_outT, bias_qkv, decay = v["w_proj"], v["w_outT"], v["bias_qkv"], v["decay"]
    pick, causal, identb, route_w = v["pick"], v["causal"], v["identb"], v["route_w"]
    with stack.enter_context(ExitStack()):
        a = lambda name, shape, dt=fp32: sb(stack, name, shape, dt)
        KT = [a(f"KT{n}", [P, 8, T], f32r) for n in range(2)]
        QF = [a(f"QF{n}", [P, 8, T], f32r) for n in range(2)]
        QI = [a(f"QI{n}", [P, 8, T], f32r) for n in range(2)]
        VP = [a(f"VP{n}", [P, NT, H, 32]) for n in range(2)]
        packs = {k: a("pack_" + k, [P, NF, NT, 4, GR], f32r) for k in "kq"}
        vals = {k: [a(f"val_{k}{n}", [P, NF, NT, 4, NV]) for n in range(2)] for k in "kq"}
        v_stage = a("v_stage", [P, NT, D])
        lines = a("lines", [P, NT, 256])
        prod = [a(f"prod{n}", [P, 2, NT * H, 6]) for n in range(2)]
        cross = a("cross", [P, 2, NT * H, 6])
        square = a("square", [P, 2, NT * H, 6])
        norm_sq = a("norm_sq", [P, 2 * NT * H])
        norm_cl = a("norm_cl", [P, 2 * NT * H])
        rnorm = a("rnorm", [P, 2, NT, H])
        rscale = a("rscale", [P, NT, H])
        st1 = a("st1", [P, NT, 6]); mv1 = a("mv1", [P, NT, 2]); ve1 = a("ve1", [P, NT]); rs1 = a("rs1", [P, NT])
        st2 = a("st2", [P, NT, 6]); mv2 = a("mv2", [P, NT, 2]); ve2 = a("ve2", [P, NT]); rs2 = a("rs2", [P, NT])
        xhat = a("xhat", [P, NT, D])
        xhat2 = a("xhat2", [P, NT, D])
        hT = a("hT", [P, T + 1])
        h2T = a("h2T", [P, T])
        mtok = [a(f"mtok{n}", [P, NT, P]) for n in range(2)]
        MT = [a(f"MT{n}", [P, T], f32r) for n in range(2)]
        tt = [a(f"tt{n}", [P, 2, NT, P]) for n in range(2)]
        PT = [a(f"PT{n}", [P, 2, 3 * P]) for n in range(2)]
        headT = a("headT", [P, 2 * T])
        rden = a("rden", [P, NT, 8])
        attn = a("attn", [P, NT, D])
        attnT = a("attnT", [P, T])
        yT = a("yT", [P, T])
        lg = a("lg", [P, NT, E]); top = a("top", [P, NT, 8]); topi = a("topi", [P, NT, 8], u32)
        topf = a("topf", [P, NT, 8]); gap = a("gap", [P, NT]); egap = a("egap", [P, NT]); eg1 = a("eg1", [P, NT])
        p12 = a("p12", [P, NT, 2]); hot = a("hot", [P, 2, NT, E])
        ps = lambda name, shape: stack.enter_context(nc.psum_tensor(name, shape, fp32))
        pre = ps("pre", [P, 2, 512])
        sc = ps("sc", [P, 2, 512])
        inc = ps("inc", [P, 2, NT, P])
        pv = ps("pv", [P, 2, T])
        bank = [ps(f"bank{n}", [P, 512]) for n in range(2)]

        ready = {j: signal("ready_" + j) for _, j, _, _ in JOBS}
        used = {j: signal("used_" + j) for _, j, _, _ in JOBS}
        zeroed, dve_settled, pool_settled = sem("zeroed"), sem("dve_settled"), sem("pool_settled")
        init = sem("init")
        stats, var, rstd, normed = signal("stats", 2), signal("var"), signal("rstd"), signal("normed")
        stats2, var2, rstd2, normed2 = signal("stats2", 2), signal("var2"), signal("rstd2"), signal("normed2")
        eps1, eps2 = signal("eps1"), signal("eps2")
        prods, crossed, squares, sums = signal("prods"), signal("crossed"), signal("squares"), signal("sums")
        clamped, inverted, rscaled = signal("clamped"), signal("inverted"), signal("rscaled")
        values, decayed = signal("values"), signal("decayed")
        packed = signal("packed", 2 * NF)
        v_done = signal("v_done")
        hi_done = signal("hi_done", 2 * NF)
        pre_ready, maxed = signal("pre_ready", 8), signal("maxed", 8)
        inc_ready, weighed, masked = signal("inc_ready", 8), signal("weighed", 8), signal("masked", 8)
        sc_ready, added, exped, pv_ready = (signal(n, 8) for n in ("sc_ready", "added", "exped", "pv_ready"))
        head_out = signal("head_out", 2)
        recip = signal("recip", 2)
        route_step, hot_done = signal("route_step", 3), signal("hot_done")
        gapped, gap_exp, probs, chosen, routed = (signal(n) for n in ("gapped", "gap_exp", "probs", "chosen", "routed"))

        with nc.Block() as block:
            @block.tensor
            def _(pe):
                def scores(b, par, p):
                    g, heads = pair_heads(p)
                    rows = slice(GR * g, GR * g + GR)
                    if p == 0:
                        wait(pe, used["q3"], b)
                    wait(pe, weighed, b, p)
                    for n, (h, j) in enumerate(heads):
                        for t in range(NT):
                            blk = slice(t * P, (t + 1) * P)
                            last = nc.tensor.matmul(inc[:, n, t, :], KT[par][rows, j, blk], QI[par][rows, j, blk],
                                                    start=True, stop=True)
                    last.then_inc(inc_ready.sem, 1)
                    wait(pe, exped, b, p)
                    wait(pe, used["max0" if p < 4 else "max1"], b)
                    for n, (h, j) in enumerate(heads):
                        for keys, cols, queries in ((slice(0, P), slice(0, T), slice(0, T)),
                                                    (slice(P, T), slice(T, T + P), slice(P, T))):
                            nc.tensor.matmul(sc[:, n, cols], KT[par][rows, j, keys], QF[par][rows, j, queries],
                                             start=True, stop=False)
                            last = nc.tensor.matmul(sc[:, n, cols], pick[rows, h % 8, :], MT[p // 4][rows, queries],
                                                    start=False, stop=True)
                    last.then_inc(sc_ready.sem, 1)

                def prescores(b, par, p):
                    g, heads = pair_heads(p)
                    rows = slice(GR * g, GR * g + GR)
                    if p % 2 == 0:
                        wait(pe, used[f"k{p // 2}"], b)
                        wait(pe, used[f"q{p // 2}"], b)
                    wait(pe, maxed, b, p)
                    for n, (h, j) in enumerate(heads):
                        nc.tensor.matmul(pre[:, n, 0:3 * P], identb[:], causal[:], start=True, stop=False)
                        nc.tensor.matmul(pre[:, n, 0:P], QF[par][rows, j, 0:P], KT[par][rows, j, 0:P],
                                         start=False, stop=False)
                        last = nc.tensor.matmul(pre[:, n, P:3 * P], QF[par][rows, j, P:T], KT[par][rows, j, :],
                                                start=False, stop=True)
                    last.then_inc(pre_ready.sem, 1)

                def values_out(b, par, p):
                    g, heads = pair_heads(p)
                    if p == 0:
                        wait(pe, v_done, b)
                    if p % 4 == 0:
                        wait(pe, head_out, b, p // 4)
                    wait(pe, exped, b, p + 1)
                    for n, (h, j) in enumerate(heads):
                        rows = slice(32 * (h % 4), 32 * (h % 4) + 32)
                        quad = (p % 4) // 2
                        nc.tensor.matmul(pv[rows, quad, :], VP[par][:, 0, h, :], PT[p % 2][:, n, 0:T],
                                         start=True, stop=False)
                        last = nc.tensor.matmul(pv[rows, quad, P:T], VP[par][:, 1, h, :], PT[p % 2][:, n, T:T + P],
                                                start=False, stop=True)
                    last.then_inc(pv_ready.sem, 1)

                def job(n, b, par):
                    _, name, off, bk = JOBS[n]
                    jb = b + off
                    if (was := before(n, b)) is not None:
                        wait(pe, used[was[0]], was[1])
                    B = bank[bk]
                    if name == "norm":
                        wait(pe, normed, jb)
                        for t in range(NT):
                            last = nc.tensor.transpose(B[:, t * P:(t + 1) * P], xhat[:, t, :], ident[:])
                    elif name[:-1] == "qkv":
                        t = int(name[-1])
                        wait(pe, used["norm"], jb)
                        last = nc.tensor.matmul(B[:, 0:384], hT[:, 1 + t * P:1 + (t + 1) * P], w_proj[:, 0:384],
                                                start=True, stop=True)
                    elif name[:-1] == "line":
                        t = int(name[-1])
                        nc.tensor.matmul(B[:, 0:192], hT[:, 1 + t * P:1 + (t + 1) * P], w_proj[:, 384:576],
                                         start=True, stop=True)
                        last = nc.tensor.matmul(B[:, 192:256], hT[:, t * P:(t + 1) * P], w_proj[:, 576:640],
                                                start=True, stop=True)
                    elif name[:-1] in ("k", "q"):
                        f = int(name[-1])
                        wait(pe, packed, jb, 2 * f + (1 if name[0] == "k" else 2))
                        for j in range(2):
                            for t in range(NT):
                                src = packs[name[0]][:, f, t, 2 * j:2 * j + 2, :].rearrange("p h r -> p (h r)").bitcast(fp32)
                                last = nc.tensor.transpose(B[:, (2 * j + t) * P:(2 * j + t + 1) * P], src, ident[:])
                    elif name[:-1] == "max":
                        half = int(name[-1])
                        wait(pe, maxed, jb, 4 * half + 4)
                        for t in range(NT):
                            last = nc.tensor.transpose(B[:, t * P:(t + 1) * P], mtok[half][:, t, :], ident[:])
                    elif name[:-1] == "head":
                        wait(pe, head_out, jb, int(name[-1]) + 1)
                        for t in range(NT):
                            for quad in range(2):
                                last = nc.tensor.transpose(B[:, (2 * t + quad) * P:(2 * t + quad + 1) * P],
                                                           headT[:, quad * T + t * P:quad * T + (t + 1) * P], ident[:])
                    elif name == "attnT":
                        wait(pe, used["head1"], jb)
                        for t in range(NT):
                            last = nc.tensor.transpose(B[:, t * P:(t + 1) * P], attn[:, t, :], ident[:])
                    elif name == "out":
                        wait(pe, used["attnT"], jb)
                        last = nc.tensor.matmul(B[:, 0:T], w_outT[:], attnT[:], start=True, stop=True)
                    elif name == "res":
                        wait(pe, used["out"], jb)
                        for t in range(NT):
                            last = nc.tensor.transpose(B[:, t * P:(t + 1) * P], yT[:, t * P:(t + 1) * P], ident[:])
                    elif name == "norm2":
                        wait(pe, normed2, jb)
                        for t in range(NT):
                            last = nc.tensor.transpose(B[:, t * P:(t + 1) * P], xhat2[:, t, :], ident[:])
                    elif name == "route":
                        wait(pe, used["norm2"], jb)
                        for t in range(NT):
                            last = nc.tensor.matmul(B[:, t * E:(t + 1) * E], h2T[:, t * P:(t + 1) * P], v["wg_sb"][:],
                                                    start=True, stop=True)
                    last.then_inc(ready[name].sem, 1)

                def body(b, par):
                    for p in range(8):
                        if live(b):
                            scores(b, par, p)
                        if p < 3 and live(b):
                            prescores(b, par, p + 5)
                        if p >= 3 and live(b + 1):
                            prescores(b + 1, 1 - par, p - 3)
                        if p > 0 and live(b):
                            values_out(b, par, p - 1)
                        if p == 0 and live(b - 1):
                            values_out(b - 1, 1 - par, 7)
                        for n, (slot, name, off, bk) in enumerate(JOBS):
                            if slot == p and live(b + off):
                                job(n, b, par)

                pe.wait_ge(init, 1)
                iterations(pe, body)

            @block.vector
            def _(dve):
                def body(b, par):
                    for p in range(8):
                        if live(b):
                            g, heads = pair_heads(p)
                            h0 = heads[0][0]
                            wait(dve, inc_ready, b, p + 1)
                            wait(dve, added, b, p - 1)
                            nc.vector.tensor_tensor(
                                tt[p % 2][:], inc[:], decay[:, h0:h0 + 3:2, :].unsqueeze(2).broadcast_to([P, 2, NT, P]),
                                ALU.mult).then_inc(weighed.sem, 1)
                        pb, pp = (b, p + 5) if p < 3 else (b + 1, p - 3)
                        if live(pb):
                            half, i = pp // 4, 4 * ((pp % 4) // 2) + pp % 2
                            g = pp % 2
                            wait(dve, pre_ready, pb, pp + 1)
                            if pp % 4 == 0:
                                wait(dve, ready[f"max{half}"], pb - 1)
                            at = GR * g + i
                            nc.vector.reduce_max(mtok[half][:, 0, at:at + 3:2], pre[:, :, 0:P], AX.X)
                            nc.vector.reduce_max(mtok[half][:, 1, at:at + 3:2], pre[:, :, P:3 * P], AX.X)\
                              .then_inc(maxed.sem, 1)
                        if live(b):
                            wait(dve, sc_ready, b, p + 1)
                            wait(dve, masked, b, p + 1)
                            diag = sc[:, :, 0:512].rearrange("p n (t k) -> p n t k", t=2)[:, :, :, 0:P]
                            nc.vector.tensor_tensor(diag, diag, tt[p % 2][:], ALU.add).then_inc(added.sem, 1)
                        extras(b, par, p)

                def extras(b, par, p):
                    if p == 0 and live(b + 2):
                        jb = b + 2
                        wait(dve, normed, jb - 1)
                        settle(dve, dve_settled)
                        for t in range(NT):
                            nc.vector.bn_stats(st1[:, t, :], x_all[:, span(jb * T + t * D, D)]).then_inc(stats.sem, 1)
                        wait(dve, stats, jb, 2)
                        wait(dve, rstd, jb - 1)
                        settle(dve, dve_settled)
                        for t in range(NT):
                            last = nc.vector.bn_aggr(mv1[:, t, :], st1[:, t, :])
                        last.then_inc(var.sem, 1)
                    if p == 1 and live(b + 2):
                        jb = b + 2
                        wait(dve, rstd, jb)
                        wait(dve, ready["norm"], jb - 1)
                        for t in range(NT):
                            last = nc.vector.tensor_scalar(xhat[:, t, :], x_all[:, span(jb * T + t * D, D)], mv1[:, t, 0:1],
                                                           rs1[:, t:t + 1], ALU.subtract, ALU.mult)
                        last.then_inc(normed.sem, 1)
                    if p == 1 and live(b - 1):
                        heads_norm(b - 1, 1)
                    if p in (3, 4) and live(b + 2):
                        jb, t = b + 2, p - 3
                        wait(dve, ready[f"qkv{t}"], jb)
                        if t == 0:
                            wait(dve, packed, jb - 2)
                            wait(dve, v_done, jb - 1)
                        B = bank[BANK[f"qkv{t}"]]
                        for n, k in enumerate("qk"):
                            nc.vector.tensor_tensor(
                                vals[k][par][:, :, t, :, 0:DH],
                                B[:, n * D:(n + 1) * D].rearrange("p (f h d) -> p f h d", f=NF, d=DH),
                                bias_qkv[:, n * D:(n + 1) * D].rearrange("p (f h d) -> p f h d", f=NF, d=DH), ALU.add)
                        nc.vector.tensor_tensor(v_stage[:, t, :], B[:, 2 * D:3 * D], bias_qkv[:, 2 * D:3 * D],
                                                ALU.add).then_inc(used[f"qkv{t}"].sem, 1)
                    if p == 5 and live(b):
                        heads_norm(b, 0)
                    if p == 5 and live(b - 1):
                        jb = b - 1
                        wait(dve, ready["res"], jb)
                        xs = x_all[:, span(jb * T, T)]
                        B = bank[BANK["res"]]
                        nc.vector.tensor_tensor(xs, B[:, 0:T], xs,
                                                ALU.add).then_inc(used["res"].sem, 1)
                        wait(dve, used["res"], jb)
                        wait(dve, normed2, jb - 1)
                        settle(dve, dve_settled)
                        for t in range(NT):
                            nc.vector.bn_stats(st2[:, t, :], x_all[:, span(jb * T + t * D, D)]).then_inc(stats2.sem, 1)
                        wait(dve, stats2, jb, 2)
                        wait(dve, rstd2, jb - 1)
                        settle(dve, dve_settled)
                        for t in range(NT):
                            last = nc.vector.bn_aggr(mv2[:, t, :], st2[:, t, :])
                        last.then_inc(var2.sem, 1)
                    if p == 6 and live(b - 1):
                        jb = b - 1
                        wait(dve, rstd2, jb)
                        wait(dve, ready["norm2"], jb - 1)
                        for t in range(NT):
                            last = nc.vector.tensor_scalar(xhat2[:, t, :], x_all[:, span(jb * T + t * D, D)], mv2[:, t, 0:1],
                                                           rs2[:, t:t + 1], ALU.subtract, ALU.mult)
                        last.then_inc(normed2.sem, 1)
                    if p == 6 and live(b + 2):
                        wait(dve, squares, b + 2)
                        wait(dve, clamped, b + 1)
                        nc.vector.reduce_sum(norm_sq[:], square[:].rearrange("p k n c -> p (k n) c"), AX.X)\
                          .then_inc(sums.sem, 1)
                    if p == 0 and live(b - 2):
                        jb = b - 2
                        wait(dve, ready["route"], jb)
                        wait(dve, routed, jb - 1)
                        B = bank[BANK["route"]]
                        nc.vector.tensor_copy(lg[:], B[:, 0:NT * E].rearrange("p (t e) -> p t e", t=NT))\
                          .then_inc(used["route"].sem, 1)
                        wait(dve, used["route"], jb)
                        settle(dve, dve_settled)
                        for t in range(NT):
                            last = nc.vector.max(top[:, t, :], lg[:, t, :])
                        last.then_inc(route_step.sem, 1)
                        wait(dve, route_step, jb, 1)
                        settle(dve, dve_settled)
                        for t in range(NT):
                            nc.vector.max_index(topi[:, t, :], top[:, t, :], lg[:, t, :])
                        wait(dve, gap_exp, jb - 1)
                        nc.vector.tensor_tensor(gap[:], top[:, :, 1], top[:, :, 0], ALU.subtract).then_inc(gapped.sem, 1)
                        wait(dve, gapped, jb)
                    if p == 2 and live(b - 2):
                        jb = b - 2
                        nc.vector.tensor_copy(topf[:], topi[:]).then_inc(chosen.sem, 1)
                        wait(dve, gap_exp, jb)
                        nc.vector.tensor_scalar(eg1[:], egap[:], 1.0, None, ALU.add).then_inc(route_step.sem, 1)
                        wait(dve, route_step, jb, 2)
                        nc.vector.reciprocal(p12[:, :, 0], eg1[:]).then_inc(route_step.sem, 1)
                        wait(dve, route_step, jb, 3)
                        nc.vector.tensor_tensor(p12[:, :, 1], p12[:, :, 0], egap[:], ALU.mult).then_inc(probs.sem, 1)

                def heads_norm(jb, half):
                    wait(dve, ready[f"head{half}"], jb)
                    wait(dve, used[f"head{1 - half}"], jb if half else jb - 1)
                    B = bank[BANK[f"head{half}"]][:, :].rearrange("p (t q r) -> p t q r", t=NT, r=32)
                    nc.vector.reciprocal(rden[:], B[:, :, :, DH]).then_inc(recip.sem, 1)
                    wait(dve, recip, jb, half + 1)
                    if half == 0:
                        wait(dve, ready["attnT"], jb - 1)
                    nc.vector.tensor_tensor(
                        attn[:, :, 64 * half:64 * half + 64].rearrange("p t (q d) -> p t q d", d=DH), B[:, :, :, 0:DH],
                        rden[:].unsqueeze(3).broadcast_to([P, NT, 8, DH]), ALU.mult).then_inc(used[f"head{half}"].sem, 1)

                for n in range(2):
                    nc.vector.memset(mtok[n][:], 0.0)
                    nc.vector.memset(VP[n][:], 0.0)
                    nc.vector.memset(vals["k"][n][:, :, 1, :, DH:DH + 6], 0.0)
                    nc.vector.memset(vals["q"][n][:, :, 0, :, DH:DH + 6], 0.0)
                for k in "kq":
                    nc.vector.memset(packs[k][:, :, :, :, 3 * NV:GR].bitcast(fp32), 0.0)
                nc.vector.memset(hT[:, 0:1], 0.0).then_inc(zeroed, 1)
                dve.wait_ge(zeroed, 1)
                for n in range(2):
                    last = nc.vector.memset(VP[n][:, :, :, DH:DH + 1], 1.0)
                last.then_inc(init, 1)
                dve.wait_ge(init, 1)
                iterations(dve, body)

            @block.scalar
            def _(act):
                def evacuate(name, b, par):
                    B = bank[BANK[name]]
                    wait(act, ready[name], b)
                    done = used[name].sem
                    if name == "norm":
                        nc.scalar.activation(hT[:, 1:T + 1], B[:, 0:T], ACT.Identity, bias=mod[:, 0, one(b)],
                                             scale=mod[:, 1, one(b)]).then_inc(done, 1)
                    elif name[:-1] == "line":
                        t = int(name[-1])
                        if t == 0:
                            wait(act, prods, b - 1)
                        nc.scalar.activation(lines[:, t, :], B[:, 0:256], ACT.Copy).then_inc(done, 1)
                    elif name[:-1] == "k":
                        f = int(name[-1])
                        nc.scalar.activation(KT[par][:, 2 * f:2 * f + 2, :],
                                             B[:, :].rearrange("p (j t) -> p j t", j=2), ACT.Copy).then_inc(done, 1)
                    elif name[:-1] == "q":
                        f = int(name[-1])
                        src = B[:, :].rearrange("p (j t) -> p j t", j=2)
                        nc.scalar.activation(QF[par][:, 2 * f:2 * f + 2, :], src, ACT.Copy, scale=v["keep_f"][:])
                        nc.scalar.activation(QI[par][:, 2 * f:2 * f + 2, :], src, ACT.Copy,
                                             scale=v["keep_i"][:]).then_inc(done, 1)
                    elif name[:-1] == "max":
                        half = int(name[-1])
                        wait(act, sc_ready, b - 1, 4 * half + 4)
                        nc.scalar.activation(MT[half][:], B[:, 0:T], ACT.Copy, scale=-1.0).then_inc(done, 1)
                    elif name == "attnT":
                        nc.scalar.activation(attnT[:], B[:, 0:T], ACT.Copy).then_inc(done, 1)
                    elif name == "out":
                        wait(act, ready["res"], b - 1)
                        nc.scalar.activation(yT[:], B[:, 0:T], ACT.Identity, bias=v["gate_bias"][:, one(b)],
                                             scale=mod[:, 2, one(b)]).then_inc(done, 1)
                    elif name == "norm2":
                        wait(act, ready["route"], b - 1)
                        nc.scalar.activation(h2T[:], B[:, 0:T], ACT.Identity, bias=mod[:, 3, one(b)],
                                             scale=mod[:, 4, one(b)])
                        nc.scalar.activation(h2_all[:, span(b * T, T)], B[:, 0:T], ACT.Identity, bias=mod[:, 3, one(b)],
                                             scale=mod[:, 4, one(b)]).then_inc(done, 1)

                def body(b, par):
                    for p in range(8):
                        for n, (slot, name, off, bk) in enumerate(JOBS):
                            if slot == p and live(b + off) and name[:-1] not in ("qkv", "head") and name not in ("res", "route"):
                                evacuate(name, b + off, (par + off) % 2)
                            if p in (0, 4) and n == 0 and live(b if p else b - 1):
                                jb, half = (b, 0) if p else (b - 1, 1)
                                wait(act, pv_ready, jb, 4 * half + 4)
                                wait(act, ready[f"head{1 - half}"], jb if half else jb - 1)
                                nc.scalar.activation(headT[:], pv[:, :, :].rearrange("p q t -> p (q t)"),
                                                     ACT.Copy).then_inc(head_out.sem, 1)
                        if p == 1 and live(b - 2):
                            wait(act, gapped, b - 2)
                            wait(act, probs, b - 3)
                            nc.scalar.activation(egap[:], gap[:], ACT.Exp).then_inc(gap_exp.sem, 1)
                        if live(b):
                            wait(act, added, b, p + 1)
                            wait(act, pv_ready, b, p - 1)
                            nc.scalar.activation(PT[p % 2][:], sc[:, :, 0:3 * P], ACT.Exp).then_inc(exped.sem, 1)

                act.wait_ge(init, 1)
                iterations(act, body)

            @block.gpsimd
            def _(pool):
                def body(b, par):
                    for p in range(8):
                        if live(b):
                            wait(pool, weighed, b, p + 1)
                            settle(pool, pool_settled)
                            nc.gpsimd.affine_select(out=tt[p % 2][:], in_=tt[p % 2][:], compare_op=ALU.is_ge, fill=fill,
                                                    base=0, pattern=[[0, 2 * NT], [1, P]],
                                                    channel_multiplier=-1).then_inc(masked.sem, 1)
                        if p == 0 and live(b + 2):
                            inverse_std(b + 2, var, mv1, ve1, eps1, rs1, rstd)
                        if p == 5 and live(b - 1):
                            inverse_std(b - 1, var2, mv2, ve2, eps2, rs2, rstd2)
                        if p in (0, 3, 4) and live(b + 1):
                            pack(b + 1, 1 - par, {0: 1, 3: 2, 4: 3}[p])
                        if p == 1 and live(b + 1):
                            place_v(b + 1, 1 - par)
                        if p == 2 and live(b - 2):
                            route(b - 2)
                        if p == 5 and live(b + 2):
                            cross_products(b + 2)
                        if p == 7 and live(b + 2):
                            line_values(b + 2, par)
                            pack(b + 2, par, 0)

                def inverse_std(jb, var, mv, ve, eps_done, rs, done):
                    wait(pool, var, jb)
                    settle(pool, pool_settled)
                    nc.gpsimd.tensor_scalar(ve[:], mv[:, :, 1], EPS, None, ALU.add).then_inc(eps_done.sem, 1)
                    wait(pool, eps_done, jb)
                    wait(pool, normed if done is rstd else normed2, jb - 1)
                    nc.gpsimd.tensor_tensor(rs[:], ve[:], v["neg_half"][:, 0:NT], ALU.pow).then_inc(done.sem, 1)

                def place_v(jb, par):
                    wait(pool, used["qkv1"], jb)
                    wait(pool, pv_ready, jb - 2)
                    settle(pool, pool_settled)
                    nc.gpsimd.tensor_copy(VP[par][:, :, :, 0:DH], v_stage[:].rearrange("p t (h d) -> p t h d", d=DH))\
                      .then_inc(v_done.sem, 1)

                def cross_products(jb):
                    wait(pool, used["line1"], jb)
                    wait(pool, squares, jb - 1)
                    col = {k: lines[:, :, 64 * k:64 * k + 64].rearrange("p t (h i) -> p t h i", i=PD) for k in range(4)}
                    for kind, p1, p2 in ((0, col[3], col[0]), (1, col[1], col[2])):
                        runs = [(0, 1, 3, slice(0, 2)), (0, 3, 4, slice(3, 4)), (1, 2, 4, slice(2, 5, 2)), (2, 3, 4, slice(5, 6))] \
                            if kind == 0 else [(0, 1, 4, slice(0, 3)), (1, 2, 4, slice(3, 5)), (2, 3, 4, slice(5, 6))]
                        for i, j0, j1, to in runs:
                            for n, (one_p, many_p) in enumerate(((p1, p2), (p2, p1))):
                                dst = prod[n][:, kind, :, :].rearrange("p (t h) c -> p t h c", t=NT)[:, :, :, to]
                                last = nc.gpsimd.tensor_tensor(
                                    dst, many_p[:, :, :, j0:j1],
                                    one_p[:, :, :, i:i + 1].broadcast_to([P, NT, H, j1 - j0]), ALU.mult)
                    last.then_inc(prods.sem, 1)
                    wait(pool, prods, jb)
                    wait(pool, values, jb - 1)
                    nc.gpsimd.tensor_tensor(cross[:, 0], prod[0][:, 0], prod[1][:, 0], ALU.subtract)
                    parts = [t[:, 1, :, :].rearrange("p n (a c) -> p n a c", a=2) for t in (*prod, cross)]
                    nc.gpsimd.tensor_tensor(parts[2][:, :, :, 0:3:2], parts[1][:, :, :, 0:3:2], parts[0][:, :, :, 0:3:2],
                                            ALU.subtract)
                    nc.gpsimd.tensor_tensor(parts[2][:, :, :, 1], parts[0][:, :, :, 1], parts[1][:, :, :, 1],
                                            ALU.subtract).then_inc(crossed.sem, 1)
                    wait(pool, crossed, jb)
                    wait(pool, sums, jb - 1)
                    nc.gpsimd.tensor_tensor(square[:], cross[:], cross[:], ALU.mult).then_inc(squares.sem, 1)

                def line_values(jb, par):
                    wait(pool, sums, jb)
                    settle(pool, pool_settled)
                    nc.gpsimd.tensor_scalar(norm_cl[:], norm_sq[:], 1e-24, None, ALU.max).then_inc(clamped.sem, 1)
                    wait(pool, clamped, jb)
                    nc.gpsimd.tensor_tensor(rnorm[:].rearrange("p k t h -> p (k t h)"), norm_cl[:], v["neg_half"][:],
                                            ALU.pow).then_inc(inverted.sem, 1)
                    wait(pool, inverted, jb)
                    nc.gpsimd.tensor_tensor(rscale[:], rnorm[:, 1], v["bscale"][:].unsqueeze(1).broadcast_to([P, NT, H]),
                                            ALU.mult).then_inc(rscaled.sem, 1)
                    wait(pool, rscaled, jb)
                    wait(pool, packed, jb - 2)
                    for n, (k, by) in enumerate((("k", rnorm[:, 0]), ("q", rscale[:]))):
                        for t in range(NT):
                            last = nc.gpsimd.tensor_tensor(
                                vals[k][par][:, :, t, :, DH + 6:NV],
                                cross[:, n, t * H:(t + 1) * H, :].rearrange("p (f h) c -> p f h c", f=NF),
                                by[:, t, :].rearrange("p (f h) -> p f h", f=NF).unsqueeze(3).broadcast_to([P, NF, 4, 6]),
                                ALU.mult)
                    last.then_inc(values.sem, 1)
                    wait(pool, values, jb)
                    for k, t, by in (("k", 0, v["decay_k"]), ("q", 1, v["decay_q"])):
                        last = nc.gpsimd.tensor_tensor(
                            vals[k][par][:, :, t, :, DH:DH + 6], vals[k][par][:, :, t, :, DH + 6:NV],
                            by[:].rearrange("p (f h) -> p f h", f=NF).unsqueeze(3).broadcast_to([P, NF, 4, 6]), ALU.mult)
                    last.then_inc(decayed.sem, 1)

                def pack(jb, par, f):
                    if f == 0:
                        wait(pool, decayed, jb)
                        wait(pool, used["qkv1"], jb)
                    for n, k in enumerate("kq"):
                        wait(pool, ready[f"{k}{f}"], jb - 1)
                        settle(pool, pool_settled)
                        src = vals[k][par][:, f, :, :, :].rearrange("p t h c -> p (t h) c")
                        dst = packs[k][:, f, :, :, 0:3 * NV].rearrange("p t h (c v) -> p (t h) c v", c=3)
                        high = slice(0, 2) if k == "k" else slice(0, 3, 2)
                        nc.gpsimd.tensor_copy(dst[:, :, high, :], src.unsqueeze(2).broadcast_to([P, NT * 4, 2, NV]))\
                          .then_inc(hi_done.sem, 1)
                        wait(pool, hi_done, jb, 2 * f + n + 1)
                        nc.gpsimd.tensor_tensor(dst[:, :, 2 if k == "k" else 1, :], src, dst[:, :, 0, :].bitcast(fp32),
                                                ALU.subtract).then_inc(packed.sem, 1)

                def route(jb):
                    wait(pool, chosen, jb)
                    wait(pool, probs, jb)
                    wait(pool, routed, jb - 1)
                    settle(pool, pool_settled)
                    for n in range(2):
                        for t in range(NT):
                            last = nc.gpsimd.tensor_scalar(hot[:, n, t, :], v["iota8"][:], topf[:, t, n:n + 1],
                                                           p12[:, t, n:n + 1], ALU.is_equal, ALU.mult)
                    last.then_inc(hot_done.sem, 1)
                    wait(pool, hot_done, jb)
                    nc.gpsimd.tensor_tensor(route_w[:, span(jb * (NT * E), NT * E)],
                                            hot[:, 0].rearrange("p t e -> p (t e)"), hot[:, 1].rearrange("p t e -> p (t e)"),
                                            ALU.add).then_inc(routed.sem, 1)

                pool.wait_ge(init, 1)
                fill = nc.gpsimd.to_reg(MASK)
                iterations(pool, body)


def experts(nc, whole, sb, sem, signal, v):
    C, NC, TC = 512, NB * T // 512, 4
    x_all, h2_all, route_w, mod, ident = v["x_all"], v["h2_all"], v["route_w"], v["mod"], v["ident"]
    with whole.enter_context(ExitStack()) as stack:
        a = lambda name, shape, dt=fp32: sb(stack, name, shape, dt)
        raw = [a(f"raw{n}", [P, E * HF]) for n in range(2)]
        w_hi = [a(f"w_hi{n}", [P, E * HF], f32r) for n in range(2)]
        w_lo = [a(f"w_lo{n}", [P, E * HF], f32r) for n in range(2)]
        w3 = a("w3", [P, E * 2, D])
        x_hi = [a(f"x_hi{n}", [P, C], f32r) for n in range(2)]
        x_lo = [a(f"x_lo{n}", [P, C], f32r) for n in range(2)]
        act_u = [a(f"act_u{n}", [P, C]) for n in range(2)]
        hid = [[a(f"hid{n}{m}", [P, C]) for m in range(2)] for n in range(2)]
        acc = [a(f"acc{n}", [P, TC, D]) for n in range(2)]
        gated = a("gated", [P, C])
        result = [a(f"result{n}", [P, C]) for n in range(2)]
        diag = [a(f"diag{n}", [P, 2, D]) for n in range(2)]
        gate = [a(f"gate{n}", [P, 2, D]) for n in range(2)]
        ps = lambda name, shape: stack.enter_context(nc.psum_tensor(name, shape, fp32))
        up = [[ps(f"up{n}{m}", [P, C]) for m in range(2)] for n in range(2)]
        y = [ps(f"y{n}", [P, TC, D]) for n in range(2)]
        gate_ps = ps("gate_ps", [P, C])

        w_loaded, w3_loaded = sem("w_loaded"), sem("w3_loaded")
        w_high, w_low = sem("w_high"), sem("w_low")
        x_high, x_low = signal("x_high"), signal("x_low")
        up_ready, silued, hidden = signal("up_ready", 2 * E), signal("silued", 2 * E), signal("hidden", 2 * E)
        y_ready, y_added = signal("y_ready", E), signal("y_added", E)
        diag_ready, gate_ready, gate_done = signal("diag_ready"), signal("gate_ready"), signal("gate_done")
        scaled, summed, stored = signal("scaled"), signal("summed"), signal("stored", 16)

        def chunks(engine, body):
            for n in (0, 1):
                body(n, n)
            with engine.Fori(1, NC // 2 - 1) as i:
                body(i * 2, 0)
                body(i * 2 + 1, 1)
            for n in (NC - 2, NC - 1):
                body(n, n % 2)

        def last_chunk(ch):
            return isinstance(ch, int) and ch == NC - 1

        def first_chunk(ch):
            return isinstance(ch, int) and ch == 0

        outd = v["out"].rearrange("b (t p) d -> p (b t) d", p=P)

        with nc.Block() as block:
            @block.sync
            def _(sp):
                for n, w in enumerate(("W1", "W2")):
                    sp.dma_start(raw[n][:].rearrange("p (e h) -> p e h", e=E), v[w].rearrange("e d h -> d e h"))\
                      .then_inc(w_loaded, 16)
                sp.dma_start(w3[:], v["W3"].rearrange("e (m p) d -> p (e m) d", p=P)).then_inc(w3_loaded, 16)

                def body(ch, par):
                    wait(sp, summed, ch)
                    wait(sp, stored, ch - 1)
                    sp.dma_start(outd[:, span(ch * TC, TC), :], result[par][:].rearrange("p (t d) -> p t d", t=TC))\
                      .then_inc(stored.sem, 16)

                chunks(sp, body)
                wait(sp, stored, NC - 1)

            @block.tensor
            def _(pe):
                def down(ch, e):
                    wait(pe, hidden, ch, 2 * e + 2)
                    wait(pe, y_added, ch, e - 1)
                    for t in range(TC):
                        for m in range(2):
                            last = nc.tensor.matmul(y[e % 2][:, t, :], hid[e % 2][m][:, t * P:(t + 1) * P],
                                                    w3[:, 2 * e + m, :], start=(m == 0), stop=(m == 1))
                    last.then_inc(y_ready.sem, 1)

                def body(ch, par):
                    wait(pe, x_low, ch)
                    for e in range(E):
                        for m in range(2):
                            n = 2 * e + m
                            wait(pe, hidden, ch, n - 1)
                            cols = slice(n * P, (n + 1) * P)
                            for k in range(2):
                                for q, (w, xx) in enumerate(((w_hi, x_hi), (w_hi, x_lo), (w_lo, x_hi))):
                                    last = nc.tensor.matmul(up[m][k][:], w[k][:, cols], xx[par][:],
                                                            start=(q == 0), stop=(q == 2))
                            last.then_inc(up_ready.sem, 1)
                            if m == 0:
                                if e > 0:
                                    down(ch, e - 1)
                                elif not first_chunk(ch):
                                    down(ch - 1, E - 1)
                        if e == 2:
                            wait(pe, diag_ready, ch)
                            wait(pe, gate_done, ch - 1)
                            nc.tensor.matmul(gate_ps[:, 0:2 * D], v["ones"][:],
                                             diag[par][:].rearrange("p b d -> p (b d)"), start=True, stop=True)\
                              .then_inc(gate_ready.sem, 1)

                pe.wait_ge(w_low, 2)
                pe.wait_ge(w3_loaded, 16)
                chunks(pe, body)
                down(NC - 1, E - 1)

            @block.scalar
            def _(act):
                def split(ch, par):
                    wait(act, up_ready, ch - 2)
                    nc.scalar.activation(x_hi[par][:], h2_all[:, span(ch * C, C)], ACT.Copy).then_inc(x_high.sem, 1)

                def body(ch, par):
                    for e in range(E):
                        for m in range(2):
                            n = 2 * e + m
                            wait(act, up_ready, ch, n + 1)
                            wait(act, hidden, ch, n - 1)
                            nc.scalar.activation(act_u[m][:], up[m][0][:], ACT.Silu).then_inc(silued.sem, 1)
                        if e == 2:
                            wait(act, gate_ready, ch)
                            wait(act, scaled, ch - 2)
                            nc.scalar.activation(gate[par][:].rearrange("p b d -> p (b d)"), gate_ps[:, 0:2 * D],
                                                 ACT.Copy).then_inc(gate_done.sem, 1)
                        if e == 3 and not last_chunk(ch):
                            split(ch + 1, 1 - par)

                act.wait_ge(w_loaded, 32)
                for n in range(2):
                    nc.scalar.activation(w_hi[n][:], raw[n][:], ACT.Copy).then_inc(w_high, 1)
                split(0, 0)
                chunks(act, body)

            @block.vector
            def _(dve):
                def split(ch, par):
                    wait(dve, x_high, ch)
                    nc.vector.tensor_tensor(x_lo[par][:], h2_all[:, span(ch * C, C)], x_hi[par][:].bitcast(fp32),
                                            ALU.subtract).then_inc(x_low.sem, 1)

                def accumulate(ch, par, e):
                    wait(dve, y_ready, ch, e + 1)
                    if e == 0:
                        wait(dve, scaled, ch - 2)
                    else:
                        wait(dve, y_added, ch, e)
                    for t in range(TC):
                        weight = route_w[:, span(ch * (TC * E) + (t * E + e), 1)]
                        if e == 0:
                            last = nc.vector.tensor_scalar(acc[par][:, t, :], y[e % 2][:, t, :], weight, None, ALU.mult)
                        else:
                            last = nc.vector.scalar_tensor_tensor(
                                out=acc[par][:, t, :], in0=y[e % 2][:, t, :], scalar=weight, in1=acc[par][:, t, :],
                                op0=ALU.mult, op1=ALU.add)
                    last.then_inc(y_added.sem, 1)

                def body(ch, par):
                    for e in range(E):
                        for m in range(2):
                            n = 2 * e + m
                            wait(dve, silued, ch, n + 1)
                            wait(dve, y_ready, ch, e - 1)
                            nc.vector.tensor_tensor(hid[e % 2][m][:], act_u[m][:], up[m][1][:], ALU.mult)\
                              .then_inc(hidden.sem, 1)
                        if e > 0:
                            accumulate(ch, par, e - 1)
                        elif not first_chunk(ch):
                            accumulate(ch - 1, 1 - par, E - 1)
                        if e == 3 and not last_chunk(ch):
                            split(ch + 1, 1 - par)

                for n in range(2):
                    dve.wait_ge(w_high, n + 1)
                    nc.vector.tensor_tensor(w_lo[n][:], raw[n][:], w_hi[n][:].bitcast(fp32), ALU.subtract)\
                      .then_inc(w_low, 1)
                split(0, 0)
                chunks(dve, body)
                accumulate(NC - 1, (NC - 1) % 2, E - 1)

            @block.gpsimd
            def _(pool):
                def finish(ch, par):
                    wait(pool, y_added, ch)
                    wait(pool, gate_done, ch)
                    wait(pool, summed, ch - 1)
                    nc.gpsimd.tensor_tensor(
                        gated[:].rearrange("p (b t d) -> p b t d", b=2, t=NT),
                        acc[par][:].rearrange("p (b t) d -> p b t d", b=2),
                        gate[par][:].unsqueeze(2).broadcast_to([P, 2, NT, D]), ALU.mult).then_inc(scaled.sem, 1)
                    wait(pool, scaled, ch)
                    wait(pool, stored, ch - 2)
                    nc.gpsimd.tensor_tensor(result[par][:], gated[:], x_all[:, span(ch * C, C)], ALU.add)\
                      .then_inc(summed.sem, 1)

                def body(ch, par):
                    wait(pool, gate_ready, ch - 2)
                    for n in range(2):
                        last = nc.gpsimd.tensor_tensor(diag[par][:, n, :], ident[:], mod[:, 5, one(ch * 2 + n)].broadcast_to([P, D]), ALU.mult)
                    last.then_inc(diag_ready.sem, 1)
                    if not first_chunk(ch):
                        finish(ch - 1, 1 - par)

                chunks(pool, body)
                finish(NC - 1, (NC - 1) % 2)


_INS = ["x", "w_qkv", "b_qkv", "w1_write", "w2_write", "w1_read", "w2_read", "w_out", "b_out", "decay_logits", "bias_scale"]
_INS = ["L0_attn_" + n for n in _INS] + ["L0_ffn_Wg", "L0_ffn_W1", "L0_ffn_W2", "L0_ffn_W3", "L0_c", "L0_wmod"]


def kernel(**inputs):
    import numpy as _np
    import concourse.bacc as _bacc
    from concourse import mybir as _mybir
    from concourse.bass_utils import run_bass_kernel_spmd as _run

    nc = _bacc.Bacc("TRN2", target_bir_lowering=False, num_devices=1)
    arrays, args = {}, []
    for name in _INS:
        arr = _np.ascontiguousarray(inputs[name])
        arrays[f"in_{name}"] = arr
        args.append(nc.dram_tensor(f"in_{name}", arr.shape, _mybir.dt.from_np(arr.dtype), kind="ExternalInput").ap())
    out = nc.dram_tensor("out", (NB, T, D), _mybir.dt.float32, kind="ExternalOutput").ap()
    build(nc, *args, out)
    return _run(nc, [arrays], core_ids=[0]).results[0]["out"]
```

```python
import concourse.bass as bass
from concourse import mybir
from contextlib import ExitStack

fp32 = mybir.dt.float32
f32r = mybir.dt.float32r
bf16 = mybir.dt.bfloat16
i32 = mybir.dt.int32
u32 = mybir.dt.uint32
ALU = mybir.AluOpType
ACT = mybir.ActivationFunctionType
AX = mybir.AxisListType

P = 128
NB, T, D = 32, 256, 128
H, DH, PD = 16, 8, 4
NT = T // P
E, HF = 8, 256
NF = 4
NV = DH + 6 + 6
GR = 64
SCALE = float(DH) ** -0.5
EPS = 1e-5
MASK = -1e30


class Signal:

    def __init__(self, sem, per):
        self.sem, self.per = sem, per


def wait(eng, signal, batch, k=None):
    value = batch * signal.per + (signal.per if k is None else k)
    if not isinstance(value, int) or value > 0:
        eng.wait_ge(signal.sem, value)


def settle(eng, settled):
    eng.sem_inc(settled, 1)


JOBS = [
    (0, "k3", 0, 0), (0, "q3", 0, 1), (0, "route", -2, 0),
    (1, "norm", 2, 1), (1, "head1", -1, 0), (1, "line0", 2, 1),
    (2, "k0", 1, 0), (2, "q0", 1, 1), (2, "line1", 2, 0),
    (3, "max1", 0, 1), (3, "attnT", -1, 0), (3, "qkv0", 2, 1),
    (4, "k1", 1, 0), (4, "q1", 1, 1), (4, "out", -1, 0),
    (5, "head0", 0, 1), (5, "qkv1", 2, 0), (5, "res", -1, 1),
    (6, "k2", 1, 0), (6, "q2", 1, 1),
    (7, "max0", 1, 0), (7, "norm2", -1, 1),
]
SPLITS = (1, 3, 5, 7)
BANK = {name: bank for _, name, _, bank in JOBS}


def span(start, count):
    return slice(start, start + count) if isinstance(start, int) else bass.ds(start, count)


def one(batch):
    return span(batch, 1)


def live(batch):
    return not isinstance(batch, int) or 0 <= batch < NB


def before(n, b):
    bank, m = JOBS[n][3], n
    while True:
        m -= 1
        if m < 0:
            m, b = len(JOBS) - 1, b - 1
        if JOBS[m][3] == bank and live(b + JOBS[m][2]):
            return JOBS[m][1], b + JOBS[m][2]
        if isinstance(b, int) and b < -3:
            return None


def iterations(engine, body):
    for b in (-2, -1, 0, 1):
        body(b, b % 2)
    with engine.Fori(1, NB // 2 - 1) as i:
        body(i * 2, 0)
        body(i * 2 + 1, 1)
    for b in (NB - 2, NB - 1, NB, NB + 1):
        body(b, b % 2)


def pair_heads(p):
    g = p % 2
    return g, [(4 * (p // 2) + g + 2 * n, 2 * (p // 2) + n) for n in range(2)]


def build(nc, x, w_qkv, b_qkv, w1_write, w2_write, w1_read, w2_read, w_out, b_out,
          decay_logits, bias_scale, Wg, W1, W2, W3, c, wmod, out):
    with ExitStack() as whole:
        def sb(stack, name, shape, dt=fp32):
            return stack.enter_context(nc.sbuf_tensor(name, shape, dt))

        def sem(name):
            return whole.enter_context(nc.semaphore(name))

        def signal(name, per=1):
            return Signal(sem(name), per)

        x_all = sb(whole, "x_all", [P, NB * NT * D])
        h2_all = sb(whole, "h2_all", [P, NB * T])
        route_w = sb(whole, "route_w", [P, NB * NT * E])
        mod = sb(whole, "mod", [P, 6, NB])
        ident = sb(whole, "ident", [P, P])
        ones = sb(whole, "ones", [P, P])

        attention = whole.enter_context(ExitStack())
        a = lambda name, shape, dt=fp32: sb(attention, name, shape, dt)
        w_proj = a("w_proj", [P, 640])
        w_outT = a("w_outT", [P, P])
        bias_qkv = a("bias_qkv", [P, 3 * D])
        gate_bias = a("gate_bias", [P, NB])
        wg_sb = a("wg_sb", [P, E])
        identb = a("identb", [P, P], bf16)
        identr = a("identr", [P, P], f32r)
        causal = a("causal", [P, P], bf16)
        decay = a("decay", [P, H, P])
        decay_q = a("decay_q", [P, H])
        decay_k = a("decay_k", [P, H])
        bscale = a("bscale", [P, H])
        pick = a("pick", [P, 8, P], f32r)
        keep_f = a("keep_f", [P, 1])
        keep_i = a("keep_i", [P, 1])
        iota8 = a("iota8", [P, E])
        neg_half = a("neg_half", [P, 2 * NT * H])

        setup(nc, ExitStack(), sem, sb, locals())
        attend(nc, whole, attention, sb, sem, signal, locals())
        attention.close()
        experts(nc, whole, sb, sem, signal, locals())


def setup(nc, stack, sem, sb, v):
    x, mod, ident, ones = v["x"], v["mod"], v["ident"], v["ones"]
    w_proj, decay = v["w_proj"], v["decay"]
    with stack:
        s = lambda name, shape, dt=fp32: sb(stack, name, shape, dt)
        wq_raw = s("wq_raw", [P, 3, D])
        wl_raw = s("wl_raw", [PD * H, 4, D])
        wo_raw = s("wo_raw", [P, D])
        c_raw = s("c_raw", [NB, D])
        wmod_sb = s("wmod_sb", [P, 6 * D])
        bout = s("bout", [P, 1])
        logit = s("logit", [P, H])
        az = s("az", [P, H]); ez = s("ez", [P, H]); lz = s("lz", [P, H]); lam = s("lam", [P, H]); lam2 = s("lam2", [P, H])
        silu_c = s("silu_c", [P, NB])
        dist_i = s("dist_i", [P, P], i32); dist = s("dist", [P, P])
        col_i = s("col_i", [P, 1], i32); col = s("col", [P, 1]); rcol = s("rcol", [P, 1])
        e_i = s("e_i", [P, E], i32)
        mask0 = s("mask0", [P, P]); mask1 = s("mask1", [P, P])
        pick0 = s("pick0", [P, 8, P]); pick1 = s("pick1", [P, 8, P])
        kf = [s(f"kf{n}", [P, 1]) for n in range(7)]
        ga_abs = s("ga_abs", [P, 2, NB]); ga_sign = s("ga_sign", [P, 2, NB]); ga_two = s("ga_two", [P, 2, NB])
        tA = stack.enter_context(nc.psum_tensor("tA", [P, 512], fp32))
        tB = stack.enter_context(nc.psum_tensor("tB", [P, 512], fp32))
        tC = stack.enter_context(nc.psum_tensor("tC", [P, 512], fp32))

        ld_w, ld_c, ld_v, ld_x, ld_d = (sem(n) for n in ("ld_w", "ld_c", "ld_v", "ld_x", "ld_d"))
        pool_step, ident_ok, dist_ok, cols_ok = (sem(n) for n in ("pool_step", "ident_ok", "dist_ok", "cols_ok"))
        wT_ok, cT_ok, silu_ok, mod_ok, modded = (sem(n) for n in ("wT_ok", "cT_ok", "silu_ok", "mod_ok", "modded"))
        az_ok, ln_ok, lam_ok, arg_ok, exp_ok = (sem(n) for n in ("az_ok", "ln_ok", "lam_ok", "arg_ok", "exp_ok"))
        dve_step, act_step, setup_done = sem("dve_step"), sem("act_step"), sem("setup_done")
        xd = x.rearrange("b (t p) d -> p (b t) d", p=P)

        with nc.Block() as block:
            @block.sync
            def _(sp):
                sp.dma_start(wq_raw[:], v["w_qkv"].rearrange("(m p) d -> p m d", p=P)).then_inc(ld_w, 16)
                for n, w in enumerate(("w2_write", "w1_read", "w2_read", "w1_write")):
                    sp.dma_start(wl_raw[:, n, :], v[w]).then_inc(ld_w, 16)
                sp.dma_start(wo_raw[:], v["w_out"]).then_inc(ld_w, 16)
                for n in range(8):
                    k = NB * NT // 8
                    sp.dma_start(v["x_all"][:, n * k * D:(n + 1) * k * D].rearrange("p (n d) -> p n d", d=D), xd[:, n * k:(n + 1) * k, :]).then_inc(ld_x, 16)
                sp.wait_ge(ld_x, 128)

            @block.gpsimd
            def _(pool):
                n = [0]

                def step(ins):
                    ins.then_inc(pool_step, 1)
                    n[0] += 1
                    pool.wait_ge(pool_step, n[0])

                step(nc.gpsimd.memset(ident[:], 0.0))
                nc.gpsimd.affine_select(out=ident[:], in_=ident[:], compare_op=ALU.not_equal, fill=1.0, base=0,
                                        pattern=[[-1, P]], channel_multiplier=1).then_inc(ident_ok, 1)
                step(nc.gpsimd.iota(dist_i[:], pattern=[[1, P]], base=0, channel_multiplier=-1))
                nc.gpsimd.tensor_scalar(dist[:], dist_i[:], 0.0, None, ALU.max).then_inc(dist_ok, 1)
                step(nc.gpsimd.iota(col_i[:], pattern=[[0, 1]], base=0, channel_multiplier=1))
                step(nc.gpsimd.tensor_copy(col[:], col_i[:]))
                nc.gpsimd.tensor_scalar(rcol[:], col[:], -1.0, float(P), ALU.mult, ALU.add).then_inc(cols_ok, 1)
                step(nc.gpsimd.iota(e_i[:], pattern=[[1, E]], base=0, channel_multiplier=0))
                nc.gpsimd.tensor_copy(v["iota8"][:], e_i[:])
                nc.gpsimd.memset(v["neg_half"][:], -0.5)
                nc.gpsimd.memset(ones[:], 1.0)
                step(nc.gpsimd.memset(mask0[:], 0.0))
                step(nc.gpsimd.affine_select(out=mask1[:], in_=mask0[:], compare_op=ALU.is_ge, fill=MASK, base=0,
                                             pattern=[[-1, P]], channel_multiplier=1))
                nc.gpsimd.tensor_copy(v["causal"][:], mask1[:])
                step(nc.gpsimd.memset(pick0[:], 0.0))
                step(nc.gpsimd.affine_select(out=pick1[:], in_=pick0[:], compare_op=ALU.not_equal, fill=1.0, base=0,
                                             pattern=[[-1, 8], [0, P]], channel_multiplier=1))
                step(nc.gpsimd.affine_select(out=pick0[:], in_=pick1[:], compare_op=ALU.not_equal, fill=1.0, base=-GR,
                                             pattern=[[-1, 8], [0, P]], channel_multiplier=1))
                nc.gpsimd.tensor_copy(v["pick"][:], pick0[:])
                step(nc.gpsimd.tensor_scalar(kf[0][:], col[:], float(GR), float(-GR), ALU.is_ge, ALU.mult))
                step(nc.gpsimd.tensor_tensor(kf[1][:], col[:], kf[0][:], ALU.add))
                for k in range(3):
                    src = kf[1 + k]
                    step(nc.gpsimd.tensor_scalar(kf[5][:], src[:], float(NV), float(-NV), ALU.is_ge, ALU.mult))
                    step(nc.gpsimd.tensor_tensor(kf[2 + k][:], src[:], kf[5][:], ALU.add))
                nc.gpsimd.tensor_scalar(v["keep_f"][:], kf[4][:], float(DH + 6), None, ALU.is_lt)
                nc.gpsimd.tensor_scalar(v["keep_i"][:], kf[4][:], float(DH + 6), None, ALU.is_ge)
                nc.gpsimd.wait_ge(ident_ok, 1)
                nc.gpsimd.tensor_copy(v["identb"][:], ident[:]).then_inc(pool_step, 1)
                nc.gpsimd.tensor_copy(v["identr"][:], ident[:]).then_inc(pool_step, 1)
                pool.wait_ge(exp_ok, 1)
                nc.gpsimd.affine_select(out=decay[:], in_=decay[:], compare_op=ALU.is_gt, fill=0.0, base=0,
                                        pattern=[[0, H], [1, P]], channel_multiplier=-1).then_inc(setup_done, 1)
                pool.wait_ge(setup_done, 1)

            @block.tensor
            def _(pe):
                pe.wait_ge(ident_ok, 1)
                pe.wait_ge(ld_c, 16 * 2)
                nc.tensor.transpose(tC[:, 256:256 + NB], c_raw[:], ident[0:NB, 0:NB]).then_inc(cT_ok, 1)
                pe.wait_ge(ld_w, 16 * 6)
                for m in range(3):
                    nc.tensor.transpose(tA[:, m * P:(m + 1) * P], wq_raw[:, m, :], ident[:])
                nc.tensor.transpose(tA[:, 3 * P:4 * P], wo_raw[:], ident[:])
                for n in range(4):
                    last = nc.tensor.transpose(tB[:, n * 64:(n + 1) * 64], wl_raw[:, n, :], ident[0:64, 0:64])
                last.then_inc(wT_ok, 1)
                pe.wait_ge(silu_ok, 1)
                for m in range(6):
                    last = nc.tensor.matmul(tC[:, m * NB:(m + 1) * NB], wmod_sb[:, m * D:(m + 1) * D], silu_c[:],
                                            start=True, stop=True)
                last.then_inc(mod_ok, 1)

            @block.scalar
            def _(act):
                act.dma_start(c_raw[:], v["c"]).then_inc(ld_c, 16)
                act.dma_start(wmod_sb[:], v["wmod"]).then_inc(ld_c, 16)
                act.dma_start(logit[:], v["decay_logits"].rearrange("(a n) -> a n", a=1).broadcast_to([P, H])).then_inc(ld_d, 16)
                act.dma_start(v["bscale"][:], v["bias_scale"].rearrange("(a n) -> a n", a=1).broadcast_to([P, H])).then_inc(ld_v, 16)
                act.dma_start(v["bias_qkv"][:], v["b_qkv"].rearrange("(a n) -> a n", a=1).broadcast_to([P, 3 * D])).then_inc(ld_v, 16)
                act.dma_start(bout[:], v["b_out"].rearrange("(p a) -> p a", a=1)).then_inc(ld_v, 16)
                act.dma_start(v["wg_sb"][:], v["Wg"]).then_inc(ld_v, 16)
                act.wait_ge(cT_ok, 1)
                nc.scalar.activation(silu_c[:], tC[:, 256:256 + NB], ACT.Silu).then_inc(silu_ok, 1)
                act.wait_ge(az_ok, 1)
                nc.scalar.activation(ez[:], az[:], ACT.Exp, scale=-1.0).then_inc(act_step, 1)
                act.wait_ge(act_step, 1)
                nc.scalar.activation(lz[:], ez[:], ACT.Ln, bias=1.0).then_inc(ln_ok, 1)
                act.wait_ge(arg_ok, 1)
                nc.scalar.activation(v["decay_q"][:], v["decay_q"][:], ACT.Exp).then_inc(act_step, 1)
                nc.scalar.activation(v["decay_k"][:], v["decay_k"][:], ACT.Exp).then_inc(act_step, 1)
                nc.scalar.activation(decay[:], decay[:], ACT.Exp).then_inc(exp_ok, 1)
                act.wait_ge(ld_v, 64)

            @block.vector
            def _(dve):
                n = [0]

                def step(ins):
                    ins.then_inc(dve_step, 1)
                    n[0] += 1
                    dve.wait_ge(dve_step, n[0])

                dve.wait_ge(ld_d, 16)
                step(nc.vector.tensor_scalar(lam2[:], logit[:], -1.0, None, ALU.mult))
                nc.vector.tensor_tensor(az[:], logit[:], lam2[:], ALU.max).then_inc(az_ok, 1)
                dve.wait_ge(wT_ok, 1)
                nc.vector.tensor_scalar(w_proj[:, 0:P], tA[:, 0:P], SCALE, None, ALU.mult)
                nc.vector.tensor_copy(w_proj[:, P:3 * P], tA[:, P:3 * P])
                nc.vector.tensor_copy(v["w_outT"][:], tA[:, 3 * P:4 * P])
                for n4, rev in enumerate((True, False, False, True)):
                    dst = w_proj[:, 384 + 64 * n4:448 + 64 * n4].rearrange("p (h i) -> p h i", i=PD)
                    src = tB[:, 64 * n4:64 * n4 + 64].rearrange("p (h i) -> p h i", i=PD)
                    for i in range(PD):
                        nc.vector.tensor_copy(dst[:, :, i], src[:, :, PD - 1 - i if rev else i])
                dve.wait_ge(ld_v, 64)
                nc.vector.tensor_scalar(v["bias_qkv"][:, 0:D], v["bias_qkv"][:, 0:D], SCALE, None, ALU.mult)
                dve.wait_ge(ln_ok, 1)
                step(nc.vector.scalar_tensor_tensor(out=lam[:], in0=lam2[:], scalar=0.0, in1=lz[:], op0=ALU.max, op1=ALU.add))
                step(nc.vector.tensor_scalar(ez[:], lam[:], -1.0, None, ALU.mult))
                dve.wait_ge(dist_ok, 1)
                dve.wait_ge(cols_ok, 1)
                nc.vector.tensor_scalar(v["decay_q"][:], ez[:], col[:], None, ALU.mult)
                nc.vector.tensor_scalar(v["decay_k"][:], ez[:], rcol[:], None, ALU.mult)
                for h in range(H):
                    last = nc.vector.tensor_scalar(decay[:, h, :], dist[:], ez[:, h:h + 1], None, ALU.mult)
                last.then_inc(arg_ok, 1)
                dve.wait_ge(mod_ok, 1)
                step(nc.vector.tensor_copy(mod[:], tC[:, 0:6 * NB].rearrange("p (m b) -> p m b", b=NB)))
                for m in (1, 4):
                    nc.vector.tensor_scalar(mod[:, m, :], mod[:, m, :], 1.0, None, ALU.add)
                gates = mod[:, 2:6:3, :]
                nc.vector.tensor_scalar(ga_sign[:], gates, 0.0, 2.0, ALU.is_ge, ALU.mult)
                step(nc.vector.tensor_scalar(ga_two[:], gates, -1.0, None, ALU.mult))
                step(nc.vector.tensor_tensor(ga_abs[:], ga_two[:], gates, ALU.max))
                step(nc.vector.tensor_scalar(ga_two[:], ga_abs[:], 0.25, None, ALU.max))
                step(nc.vector.tensor_scalar(ga_abs[:], ga_sign[:], 1.0, None, ALU.subtract))
                step(nc.vector.tensor_tensor(gates, ga_abs[:], ga_two[:], ALU.mult))
                step(nc.vector.tensor_scalar(v["gate_bias"][:], mod[:, 2, :], bout[:], None, ALU.mult))


def attend(nc, whole, stack, sb, sem, signal, v):
    x_all, h2_all, mod, ident = v["x_all"], v["h2_all"], v["mod"], v["ident"]
    w_proj, w_outT, bias_qkv, decay = v["w_proj"], v["w_outT"], v["bias_qkv"], v["decay"]
    pick, causal, identb, identr, route_w = v["pick"], v["causal"], v["identb"], v["identr"], v["route_w"]
    with stack.enter_context(ExitStack()):
        a = lambda name, shape, dt=fp32: sb(stack, name, shape, dt)
        KT = [a(f"KT{n}", [P, 8, T], f32r) for n in range(2)]
        QF = [a(f"QF{n}", [P, 8, T], f32r) for n in range(2)]
        QI = [a(f"QI{n}", [P, 8, T], f32r) for n in range(2)]
        VP = [a(f"VP{n}", [P, NT, H, 32]) for n in range(2)]
        packs = {k: a("pack_" + k, [P, NF, NT, 4, GR], f32r) for k in "kq"}
        vals = {k: [a(f"val_{k}{n}", [P, NF, NT, 4, NV]) for n in range(2)] for k in "kq"}
        v_stage = a("v_stage", [P, NT, D])
        lines = a("lines", [P, NT, 256])
        prod = [a(f"prod{n}", [P, 2, NT * H, 6]) for n in range(2)]
        cross = a("cross", [P, 2, NT * H, 6])
        square = a("square", [P, 2, NT * H, 6])
        norm_sq = a("norm_sq", [P, 2 * NT * H])
        norm_cl = a("norm_cl", [P, 2 * NT * H])
        norm_half = a("norm_half", [P, 2 * NT * H])
        newton = [a(f"newton{n}", [P, 2 * NT * H]) for n in range(2)]
        three_halves = a("three_halves", [P, 2 * NT * H])
        bits = a("bits", [P, 2 * NT * H], i32)
        guess = a("guess", [P, 2 * NT * H], i32)
        rnorm = a("rnorm", [P, 2, NT, H])
        rscale = a("rscale", [P, NT, H])
        st1 = a("st1", [P, NT, 6]); mv1 = a("mv1", [P, NT, 2]); ve1 = a("ve1", [P, NT]); rs1 = a("rs1", [P, NT])
        st2 = a("st2", [P, NT, 6]); mv2 = a("mv2", [P, NT, 2]); ve2 = a("ve2", [P, NT]); rs2 = a("rs2", [P, NT])
        xhat = a("xhat", [P, NT, D])
        xhat2 = a("xhat2", [P, NT, D])
        hT = a("hT", [P, T + 1])
        h2T = a("h2T", [P, T])
        mtok = [a(f"mtok{n}", [P, NT, P], f32r) for n in range(2)]
        MT = [a(f"MT{n}", [P, T], f32r) for n in range(2)]
        tt = [a(f"tt{n}", [P, 2, NT, P]) for n in range(2)]
        PT = [a(f"PT{n}", [P, 2, 3 * P]) for n in range(2)]
        headT = a("headT", [P, 2 * T])
        rden = a("rden", [P, NT, 8])
        attn = a("attn", [P, NT, D])
        attnT = a("attnT", [P, T])
        yT = a("yT", [P, T])
        lg = a("lg", [P, NT, E]); top = a("top", [P, NT, 8]); topi = a("topi", [P, NT, 8], u32)
        topf = a("topf", [P, NT, 8]); gap = a("gap", [P, NT]); egap = a("egap", [P, NT]); eg1 = a("eg1", [P, NT])
        p12 = a("p12", [P, NT, 2]); hot = a("hot", [P, 2, NT, E])
        ps = lambda name, shape: stack.enter_context(nc.psum_tensor(name, shape, fp32))
        pre = ps("pre", [P, 2, 512])
        sc = ps("sc", [P, 2, 512])
        inc = ps("inc", [P, 2, NT, P])
        pv = ps("pv", [P, 2, T])
        bank = [ps(f"bank{n}", [P, 512]) for n in range(2)]

        ready = {j: signal("ready_" + j) for _, j, _, _ in JOBS}
        used = {j: signal("used_" + j) for _, j, _, _ in JOBS}
        zeroed, dve_settled, pool_settled = sem("zeroed"), sem("dve_settled"), sem("pool_settled")
        init = sem("init")
        stats, var, rstd, normed = signal("stats", 2), signal("var"), signal("rstd"), signal("normed")
        stats2, var2, rstd2, normed2 = signal("stats2", 2), signal("var2"), signal("rstd2"), signal("normed2")
        eps1, eps2 = signal("eps1"), signal("eps2")
        prods, crossed, squares, sums = signal("prods"), signal("crossed"), signal("squares"), signal("sums")
        clamped, halved, guessed = signal("clamped"), signal("halved"), signal("guessed")
        newton_step, rscaled = signal("newton_step", 12), signal("rscaled")
        values, decayed = signal("values"), signal("decayed")
        packed = signal("packed", 2 * NF)
        v_done = signal("v_done")
        hi_done = signal("hi_done", 2 * NF)
        pre_ready, maxed = signal("pre_ready", 8), signal("maxed", 8)
        inc_ready, weighed = signal("inc_ready", 8), signal("weighed", 8)
        sc_ready, added, exped, pv_ready = (signal(n, 8) for n in ("sc_ready", "added", "exped", "pv_ready"))
        head_out = signal("head_out", 2)
        recip = signal("recip", 2)
        route_step, hot_done = signal("route_step", 3), signal("hot_done")
        gapped, gap_exp, probs, chosen, routed = (signal(n) for n in ("gapped", "gap_exp", "probs", "chosen", "routed"))

        def split_views(k, par, f):
            return (vals[k][par][:, f, :, :, :].rearrange("p t h c -> p (t h) c"),
                    packs[k][:, f, :, :, 0:3 * NV].rearrange("p t h (c v) -> p (t h) c v", c=3))

        with nc.Block() as block:
            @block.tensor
            def _(pe):
                def incidences(b, par, p):
                    g, heads = pair_heads(p)
                    rows = slice(GR * g, GR * g + GR)
                    if p % 2 == 0:
                        wait(pe, used[f"q{p // 2}"], b)
                    wait(pe, weighed, b, p)
                    for n, (h, j) in enumerate(heads):
                        for t in range(NT):
                            blk = slice(t * P, (t + 1) * P)
                            last = nc.tensor.matmul(inc[:, n, t, :], KT[par][rows, j, blk], QI[par][rows, j, blk],
                                                    start=True, stop=True)
                    last.then_inc(inc_ready.sem, 1)

                def scores(b, par, p):
                    g, heads = pair_heads(p)
                    rows = slice(GR * g, GR * g + GR)
                    wait(pe, exped, b, p)
                    if p % 4 == 0:
                        wait(pe, used["max0" if p < 4 else "max1"], b)
                    for n, (h, j) in enumerate(heads):
                        for keys, cols, queries in ((slice(0, P), slice(0, T), slice(0, T)),
                                                    (slice(P, T), slice(T, T + P), slice(P, T))):
                            nc.tensor.matmul(sc[:, n, cols], KT[par][rows, j, keys], QF[par][rows, j, queries],
                                             start=True, stop=False)
                            nc.tensor.matmul(sc[:, n, cols], pick[rows, h % 8, :], MT[p // 4][rows, queries],
                                             start=False, stop=False)
                            last = nc.tensor.matmul(sc[:, n, cols.start:cols.start + P], causal[:], identb[:],
                                                    start=False, stop=True)
                    last.then_inc(sc_ready.sem, 1)

                def prescores(b, par, p):
                    g, heads = pair_heads(p)
                    rows = slice(GR * g, GR * g + GR)
                    if p % 2 == 0:
                        wait(pe, used[f"k{p // 2}"], b)
                        wait(pe, used[f"q{p // 2}"], b)
                    wait(pe, maxed, b, p)
                    for n, (h, j) in enumerate(heads):
                        for queries, cols, keys in ((slice(0, P), slice(0, P), slice(0, P)),
                                                    (slice(P, T), slice(P, P + T), slice(0, T))):
                            nc.tensor.matmul(pre[:, n, cols], QF[par][rows, j, queries], KT[par][rows, j, keys],
                                             start=True, stop=False)
                            last = nc.tensor.matmul(pre[:, n, cols.stop - P:cols.stop], identb[:], causal[:],
                                                    start=False, stop=True)
                    last.then_inc(pre_ready.sem, 1)

                def values_out(b, par, p):
                    g, heads = pair_heads(p)
                    if p == 0:
                        wait(pe, v_done, b)
                    if p % 4 == 0:
                        wait(pe, head_out, b, p // 4)
                    wait(pe, exped, b, p + 1)
                    for n, (h, j) in enumerate(heads):
                        rows = slice(32 * (h % 4), 32 * (h % 4) + 32)
                        quad = (p % 4) // 2
                        nc.tensor.matmul(pv[rows, quad, :], VP[par][:, 0, h, :], PT[p % 2][:, n, 0:T],
                                         start=True, stop=False)
                        last = nc.tensor.matmul(pv[rows, quad, P:T], VP[par][:, 1, h, :], PT[p % 2][:, n, T:T + P],
                                                start=False, stop=True)
                    last.then_inc(pv_ready.sem, 1)

                def job(n, b, par):
                    _, name, off, bk = JOBS[n]
                    jb = b + off
                    if (was := before(n, b)) is not None:
                        wait(pe, used[was[0]], was[1])
                    B = bank[bk]
                    if name == "norm":
                        wait(pe, normed, jb)
                        for t in range(NT):
                            last = nc.tensor.transpose(B[:, t * P:(t + 1) * P], xhat[:, t, :], ident[:])
                    elif name[:-1] == "qkv":
                        t = int(name[-1])
                        wait(pe, used["norm"], jb)
                        last = nc.tensor.matmul(B[:, 0:384], hT[:, 1 + t * P:1 + (t + 1) * P], w_proj[:, 0:384],
                                                start=True, stop=True)
                    elif name[:-1] == "line":
                        t = int(name[-1])
                        nc.tensor.matmul(B[:, 0:192], hT[:, 1 + t * P:1 + (t + 1) * P], w_proj[:, 384:576],
                                         start=True, stop=True)
                        last = nc.tensor.matmul(B[:, 192:256], hT[:, t * P:(t + 1) * P], w_proj[:, 576:640],
                                                start=True, stop=True)
                    elif name[:-1] in ("k", "q"):
                        f = int(name[-1])
                        wait(pe, packed, jb, 2 * f + (1 if name[0] == "k" else 2))
                        for j in range(2):
                            for t in range(NT):
                                src = packs[name[0]][:, f, t, 2 * j:2 * j + 2, :].rearrange("p h r -> p (h r)")
                                last = nc.tensor.matmul(B[:, (2 * j + t) * P:(2 * j + t + 1) * P], src, identr[:],
                                                        start=True, stop=True)
                    elif name[:-1] == "max":
                        half = int(name[-1])
                        wait(pe, maxed, jb, 4 * half + 4)
                        for t in range(NT):
                            last = nc.tensor.matmul(B[:, t * P:(t + 1) * P], mtok[half][:, t, :], identr[:],
                                                    start=True, stop=True)
                    elif name[:-1] == "head":
                        wait(pe, head_out, jb, int(name[-1]) + 1)
                        for t in range(NT):
                            for quad in range(2):
                                last = nc.tensor.transpose(B[:, (2 * t + quad) * P:(2 * t + quad + 1) * P],
                                                           headT[:, quad * T + t * P:quad * T + (t + 1) * P], ident[:])
                    elif name == "attnT":
                        wait(pe, used["head1"], jb)
                        for t in range(NT):
                            last = nc.tensor.transpose(B[:, t * P:(t + 1) * P], attn[:, t, :], ident[:])
                    elif name == "out":
                        wait(pe, used["attnT"], jb)
                        last = nc.tensor.matmul(B[:, 0:T], w_outT[:], attnT[:], start=True, stop=True)
                    elif name == "res":
                        wait(pe, used["out"], jb)
                        for t in range(NT):
                            last = nc.tensor.transpose(B[:, t * P:(t + 1) * P], yT[:, t * P:(t + 1) * P], ident[:])
                    elif name == "norm2":
                        wait(pe, normed2, jb)
                        for t in range(NT):
                            last = nc.tensor.transpose(B[:, t * P:(t + 1) * P], xhat2[:, t, :], ident[:])
                    elif name == "route":
                        wait(pe, used["norm2"], jb)
                        for t in range(NT):
                            last = nc.tensor.matmul(B[:, t * E:(t + 1) * E], h2T[:, t * P:(t + 1) * P], v["wg_sb"][:],
                                                    start=True, stop=True)
                    last.then_inc(ready[name].sem, 1)

                def body(b, par):
                    for p in range(8):
                        if p == 0 and live(b) and not live(b - 1):
                            incidences(b, par, 0)
                        if live(b):
                            scores(b, par, p)
                        small = [n for n, (slot, name, off, bk) in enumerate(JOBS) if slot == p and live(b + off)]
                        for n in small[:1]:
                            job(n, b, par)
                        if p < 3 and live(b):
                            prescores(b, par, p + 5)
                        if p >= 3 and live(b + 1):
                            prescores(b + 1, 1 - par, p - 3)
                        for n in small[1:2]:
                            job(n, b, par)
                        if p > 0 and live(b):
                            values_out(b, par, p - 1)
                        if p == 0 and live(b - 1):
                            values_out(b - 1, 1 - par, 7)
                        for n in small[2:]:
                            job(n, b, par)
                        if p < 7 and live(b):
                            incidences(b, par, p + 1)
                        if p == 7 and live(b) and live(b + 1):
                            incidences(b + 1, 1 - par, 0)

                pe.wait_ge(init, 1)
                iterations(pe, body)

            @block.vector
            def _(dve):
                def body(b, par):
                    for p in range(8):
                        if p == 0 and live(b) and not live(b - 1):
                            weigh(b, 0)
                        if live(b):
                            wait(dve, sc_ready, b, p + 1)
                            wait(dve, weighed, b, p + 1)
                            diag = sc[:, :, 0:512].rearrange("p n (t k) -> p n t k", t=2)[:, :, :, 0:P]
                            nc.vector.tensor_tensor(diag, diag, tt[p % 2][:], ALU.add).then_inc(added.sem, 1)
                        if p == 0 and live(b + 2):
                            first_stats(b + 2)
                        pb, pp = (b, p + 5) if p < 3 else (b + 1, p - 3)
                        if live(pb):
                            half, i = pp // 4, 4 * ((pp % 4) // 2) + pp % 2
                            g = pp % 2
                            wait(dve, pre_ready, pb, pp + 1)
                            if pp % 4 == 0:
                                wait(dve, ready[f"max{half}"], pb - 1)
                            at = GR * g + i
                            nc.vector.reduce_max(mtok[half][:, 0, at:at + 3:2], pre[:, :, 0:P], AX.X)
                            nc.vector.reduce_max(mtok[half][:, 1, at:at + 3:2], pre[:, :, P:3 * P], AX.X)\
                              .then_inc(maxed.sem, 1)
                        extras(b, par, p)
                        if p < 7 and live(b):
                            weigh(b, p + 1)
                        if p == 7 and live(b) and live(b + 1):
                            weigh(b + 1, 0)

                def weigh(b, p):
                    h0 = pair_heads(p)[1][0][0]
                    wait(dve, inc_ready, b, p + 1)
                    wait(dve, added, b, p - 1)
                    nc.vector.tensor_tensor(
                        tt[p % 2][:], inc[:], decay[:, h0:h0 + 3:2, :].unsqueeze(2).broadcast_to([P, 2, NT, P]),
                        ALU.mult).then_inc(weighed.sem, 1)

                def first_stats(jb):
                    wait(dve, normed, jb - 1)
                    settle(dve, dve_settled)
                    for t in range(NT):
                        nc.vector.bn_stats(st1[:, t, :], x_all[:, span(jb * T + t * D, D)]).then_inc(stats.sem, 1)
                    wait(dve, stats, jb, 2)
                    wait(dve, rstd, jb - 1)
                    settle(dve, dve_settled)
                    for t in range(NT):
                        last = nc.vector.bn_aggr(mv1[:, t, :], st1[:, t, :])
                    last.then_inc(var.sem, 1)

                def extras(b, par, p):
                    if p == 0 and live(b + 2):
                        jb = b + 2
                        wait(dve, rstd, jb)
                        wait(dve, ready["norm"], jb - 1)
                        for t in range(NT):
                            last = nc.vector.tensor_scalar(xhat[:, t, :], x_all[:, span(jb * T + t * D, D)], mv1[:, t, 0:1],
                                                           rs1[:, t:t + 1], ALU.subtract, ALU.mult)
                        last.then_inc(normed.sem, 1)
                    if p == 0 and live(b - 2):
                        jb = b - 2
                        wait(dve, ready["route"], jb)
                        B = bank[BANK["route"]]
                        nc.vector.tensor_copy(lg[:], B[:, 0:NT * E].rearrange("p (t e) -> p t e", t=NT))\
                          .then_inc(used["route"].sem, 1)
                        wait(dve, used["route"], jb)
                        settle(dve, dve_settled)
                        for t in range(NT):
                            last = nc.vector.max(top[:, t, :], lg[:, t, :])
                        last.then_inc(route_step.sem, 1)
                        wait(dve, route_step, jb, 1)
                        settle(dve, dve_settled)
                        for t in range(NT):
                            nc.vector.max_index(topi[:, t, :], top[:, t, :], lg[:, t, :])
                        wait(dve, gap_exp, jb - 1)
                        nc.vector.tensor_tensor(gap[:], top[:, :, 1], top[:, :, 0], ALU.subtract).then_inc(gapped.sem, 1)
                        wait(dve, gapped, jb)
                    if p == 1 and live(b - 1):
                        heads_norm(b - 1, 1)
                    if p == 2 and live(b - 2):
                        jb = b - 2
                        nc.vector.tensor_copy(topf[:], topi[:]).then_inc(chosen.sem, 1)
                        wait(dve, gap_exp, jb)
                        nc.vector.tensor_scalar(eg1[:], egap[:], 1.0, None, ALU.add).then_inc(route_step.sem, 1)
                        wait(dve, route_step, jb, 2)
                        nc.vector.reciprocal(p12[:, :, 0], eg1[:]).then_inc(route_step.sem, 1)
                        wait(dve, route_step, jb, 3)
                        nc.vector.tensor_tensor(p12[:, :, 1], p12[:, :, 0], egap[:], ALU.mult).then_inc(probs.sem, 1)
                        wait(dve, chosen, jb)
                        wait(dve, probs, jb)
                        for n in range(2):
                            for t in range(NT):
                                last = nc.vector.tensor_scalar(hot[:, n, t, :], v["iota8"][:], topf[:, t, n:n + 1],
                                                               p12[:, t, n:n + 1], ALU.is_equal, ALU.mult)
                        last.then_inc(hot_done.sem, 1)
                        wait(dve, hot_done, jb)
                        nc.vector.tensor_tensor(route_w[:, span(jb * (NT * E), NT * E)],
                                                hot[:, 0].rearrange("p t e -> p (t e)"),
                                                hot[:, 1].rearrange("p t e -> p (t e)"), ALU.add).then_inc(routed.sem, 1)
                    if p == 5 and live(b):
                        heads_norm(b, 0)
                    if p in (3, 5) and live(b + 2):
                        jb, t = b + 2, (p - 3) // 2
                        wait(dve, ready[f"qkv{t}"], jb)
                        if t == 0:
                            wait(dve, packed, jb - 2)
                            wait(dve, v_done, jb - 1)
                        B = bank[BANK[f"qkv{t}"]]
                        for n, k in enumerate("qk"):
                            nc.vector.tensor_tensor(
                                vals[k][par][:, :, t, :, 0:DH],
                                B[:, n * D:(n + 1) * D].rearrange("p (f h d) -> p f h d", f=NF, d=DH),
                                bias_qkv[:, n * D:(n + 1) * D].rearrange("p (f h d) -> p f h d", f=NF, d=DH), ALU.add)
                        nc.vector.tensor_tensor(v_stage[:, t, :], B[:, 2 * D:3 * D], bias_qkv[:, 2 * D:3 * D],
                                                ALU.add).then_inc(used[f"qkv{t}"].sem, 1)
                    if p == 5 and live(b - 1):
                        jb = b - 1
                        wait(dve, ready["res"], jb)
                        xs = x_all[:, span(jb * T, T)]
                        B = bank[BANK["res"]]
                        nc.vector.tensor_tensor(xs, B[:, 0:T], xs,
                                                ALU.add).then_inc(used["res"].sem, 1)
                        wait(dve, used["res"], jb)
                        wait(dve, normed2, jb - 1)
                        settle(dve, dve_settled)
                        for t in range(NT):
                            nc.vector.bn_stats(st2[:, t, :], x_all[:, span(jb * T + t * D, D)]).then_inc(stats2.sem, 1)
                        wait(dve, stats2, jb, 2)
                        wait(dve, rstd2, jb - 1)
                        settle(dve, dve_settled)
                        for t in range(NT):
                            last = nc.vector.bn_aggr(mv2[:, t, :], st2[:, t, :])
                        last.then_inc(var2.sem, 1)
                    if p == 6 and live(b - 1):
                        jb = b - 1
                        wait(dve, rstd2, jb)
                        wait(dve, ready["norm2"], jb - 1)
                        for t in range(NT):
                            last = nc.vector.tensor_scalar(xhat2[:, t, :], x_all[:, span(jb * T + t * D, D)], mv2[:, t, 0:1],
                                                           rs2[:, t:t + 1], ALU.subtract, ALU.mult)
                        last.then_inc(normed2.sem, 1)
                    if p == 6 and live(b + 2):
                        jb = b + 2
                        wait(dve, squares, jb)
                        wait(dve, clamped, jb - 1)
                        nc.vector.reduce_sum(norm_sq[:], square[:].rearrange("p k n c -> p (k n) c"), AX.X)\
                          .then_inc(sums.sem, 1)
                        wait(dve, sums, jb)
                        wait(dve, newton_step, jb - 1)
                        nc.vector.tensor_scalar(norm_cl[:], norm_sq[:], 1e-24, None, ALU.max).then_inc(clamped.sem, 1)
                        wait(dve, clamped, jb)
                        nc.vector.tensor_scalar(norm_half[:], norm_cl[:], -0.5, None, ALU.mult)
                        nc.vector.tensor_scalar(bits[:], norm_cl[:].bitcast(i32), 1, None, ALU.logical_shift_right)\
                          .then_inc(halved.sem, 1)
                        wait(dve, halved, jb)
                        nc.vector.tensor_scalar(guess[:], bits[:], -1.0, float(0x5F3759DF), ALU.mult, ALU.add)\
                          .then_inc(guessed.sem, 1)

                def heads_norm(jb, half):
                    wait(dve, ready[f"head{half}"], jb)
                    wait(dve, used[f"head{1 - half}"], jb if half else jb - 1)
                    B = bank[BANK[f"head{half}"]][:, :].rearrange("p (t q r) -> p t q r", t=NT, r=32)
                    nc.vector.reciprocal(rden[:], B[:, :, :, DH]).then_inc(recip.sem, 1)
                    wait(dve, recip, jb, half + 1)
                    if half == 0:
                        wait(dve, ready["attnT"], jb - 1)
                    nc.vector.tensor_tensor(
                        attn[:, :, 64 * half:64 * half + 64].rearrange("p t (q d) -> p t q d", d=DH), B[:, :, :, 0:DH],
                        rden[:].unsqueeze(3).broadcast_to([P, NT, 8, DH]), ALU.mult).then_inc(used[f"head{half}"].sem, 1)

                nc.vector.memset(three_halves[:], 1.5)
                for n in range(2):
                    nc.vector.memset(mtok[n][:].bitcast(fp32), 0.0)
                    nc.vector.memset(VP[n][:], 0.0)
                    nc.vector.memset(vals["k"][n][:, :, 1, :, DH:DH + 6], 0.0)
                    nc.vector.memset(vals["q"][n][:, :, 0, :, DH:DH + 6], 0.0)
                for k in "kq":
                    nc.vector.memset(packs[k][:, :, :, :, 3 * NV:GR].bitcast(fp32), 0.0)
                nc.vector.memset(hT[:, 0:1], 0.0).then_inc(zeroed, 1)
                dve.wait_ge(zeroed, 1)
                for n in range(2):
                    last = nc.vector.memset(VP[n][:, :, :, DH:DH + 1], 1.0)
                last.then_inc(init, 1)
                dve.wait_ge(init, 1)
                iterations(dve, body)

            @block.scalar
            def _(act):
                def evacuate(name, b, par):
                    B = bank[BANK[name]]
                    wait(act, ready[name], b)
                    done = used[name].sem
                    if name == "norm":
                        nc.scalar.activation(hT[:, 1:T + 1], B[:, 0:T], ACT.Identity, bias=mod[:, 0, one(b)],
                                             scale=mod[:, 1, one(b)]).then_inc(done, 1)
                    elif name[:-1] == "line":
                        t = int(name[-1])
                        if t == 0:
                            wait(act, prods, b - 1)
                        nc.scalar.activation(lines[:, t, :], B[:, 0:256], ACT.Copy).then_inc(done, 1)
                    elif name[:-1] == "k":
                        f = int(name[-1])
                        nc.scalar.activation(KT[par][:, 2 * f:2 * f + 2, :],
                                             B[:, :].rearrange("p (j t) -> p j t", j=2), ACT.Copy).then_inc(done, 1)
                    elif name[:-1] == "q":
                        f = int(name[-1])
                        src = B[:, :].rearrange("p (j t) -> p j t", j=2)
                        nc.scalar.activation(QF[par][:, 2 * f:2 * f + 2, :], src, ACT.Copy, scale=v["keep_f"][:])
                        nc.scalar.activation(QI[par][:, 2 * f:2 * f + 2, :], src, ACT.Copy,
                                             scale=v["keep_i"][:]).then_inc(done, 1)
                    elif name[:-1] == "max":
                        half = int(name[-1])
                        wait(act, sc_ready, b - 1, 4 * half + 4)
                        nc.scalar.activation(MT[half][:], B[:, 0:T], ACT.Copy, scale=-1.0).then_inc(done, 1)
                    elif name == "attnT":
                        nc.scalar.activation(attnT[:], B[:, 0:T], ACT.Copy).then_inc(done, 1)
                    elif name == "out":
                        wait(act, ready["res"], b - 1)
                        nc.scalar.activation(yT[:], B[:, 0:T], ACT.Identity, bias=v["gate_bias"][:, one(b)],
                                             scale=mod[:, 2, one(b)]).then_inc(done, 1)
                    elif name == "norm2":
                        wait(act, ready["route"], b - 1)
                        nc.scalar.activation(h2T[:], B[:, 0:T], ACT.Identity, bias=mod[:, 3, one(b)],
                                             scale=mod[:, 4, one(b)])
                        nc.scalar.activation(h2_all[:, span(b * T, T)], B[:, 0:T], ACT.Identity, bias=mod[:, 3, one(b)],
                                             scale=mod[:, 4, one(b)]).then_inc(done, 1)

                def split_high(jb, par, f):
                    if f == 0:
                        wait(act, decayed, jb)
                        wait(act, used["qkv1"], jb)
                    for n, k in enumerate("kq"):
                        wait(act, ready[f"{k}{f}"], jb - 1)
                        src, dst = split_views(k, par, f)
                        high = slice(0, 2) if k == "k" else slice(0, 3, 2)
                        nc.scalar.activation(dst[:, :, high, :], src.unsqueeze(2).broadcast_to([P, NT * 4, 2, NV]),
                                             ACT.Copy).then_inc(hi_done.sem, 1)

                def heads_out(jb, half):
                    wait(act, pv_ready, jb, 4 * half + 4)
                    wait(act, ready[f"head{1 - half}"], jb if half else jb - 1)
                    nc.scalar.activation(headT[:], pv[:, :, :].rearrange("p q t -> p (q t)"),
                                         ACT.Copy).then_inc(head_out.sem, 1)

                def body(b, par):
                    for p in range(8):
                        if live(b):
                            wait(act, added, b, p + 1)
                            wait(act, pv_ready, b, p - 1)
                            nc.scalar.activation(PT[p % 2][:], sc[:, :, 0:3 * P], ACT.Exp).then_inc(exped.sem, 1)
                        small = [(name, off) for slot, name, off, bk in JOBS if slot == p and live(b + off)]
                        for n, (name, off) in enumerate(small):
                            if name[:-1] not in ("qkv", "head") and name not in ("res", "route"):
                                evacuate(name, b + off, (par + off) % 2)
                        if p == 0 and live(b - 1):
                            heads_out(b - 1, 1)
                        if p == 4 and live(b):
                            heads_out(b, 0)
                        if p in SPLITS and live(b + 1):
                            split_high(b + 1, 1 - par, SPLITS.index(p))
                        if p == 1 and live(b + 1):
                            wait(act, used["qkv1"], b + 1)
                            wait(act, pv_ready, b - 1)
                            nc.scalar.activation(VP[1 - par][:, :, :, 0:DH].rearrange("p t h d -> p (t h) d"),
                                                 v_stage[:].rearrange("p t (h d) -> p (t h) d", d=DH),
                                                 ACT.Copy).then_inc(v_done.sem, 1)
                        if p == 5 and live(b + 2):
                            wait(act, crossed, b + 2)
                            wait(act, sums, b + 1)
                            nc.scalar.activation(square[:], cross[:], ACT.Square).then_inc(squares.sem, 1)
                        if p == 1 and live(b - 2):
                            wait(act, gapped, b - 2)
                            wait(act, probs, b - 3)
                            nc.scalar.activation(egap[:], gap[:], ACT.Exp).then_inc(gap_exp.sem, 1)

                act.wait_ge(init, 1)
                iterations(act, body)

            @block.gpsimd
            def _(pool):
                def body(b, par):
                    for p in range(8):
                        if p == 0 and live(b + 2):
                            inverse_std(b + 2, var, mv1, ve1, eps1, rs1, rstd)
                        if p == 6 and live(b - 1):
                            inverse_std(b - 1, var2, mv2, ve2, eps2, rs2, rstd2)
                        if p in SPLITS and live(b + 1):
                            split_rest(b + 1, 1 - par, SPLITS.index(p))
                        if p == 3 and live(b + 2):
                            products(b + 2)
                        if p == 4 and live(b + 2):
                            cross_products(b + 2)
                        if p == 7 and live(b + 2):
                            line_values(b + 2, par)

                def inverse_std(jb, var, mv, ve, eps_done, rs, done):
                    wait(pool, var, jb)
                    settle(pool, pool_settled)
                    nc.gpsimd.tensor_scalar(ve[:], mv[:, :, 1], EPS, None, ALU.add).then_inc(eps_done.sem, 1)
                    wait(pool, eps_done, jb)
                    wait(pool, normed if done is rstd else normed2, jb - 1)
                    nc.gpsimd.tensor_tensor(rs[:], ve[:], v["neg_half"][:, 0:NT], ALU.pow).then_inc(done.sem, 1)

                def products(jb):
                    wait(pool, used["line1"], jb)
                    wait(pool, crossed, jb - 1)
                    col = {k: lines[:, :, 64 * k:64 * k + 64].rearrange("p t (h i) -> p t h i", i=PD) for k in range(4)}
                    for kind, p1, p2 in ((0, col[3], col[0]), (1, col[1], col[2])):
                        runs = [(0, 1, 3, slice(0, 2)), (0, 3, 4, slice(3, 4)), (1, 2, 4, slice(2, 5, 2)), (2, 3, 4, slice(5, 6))] \
                            if kind == 0 else [(0, 1, 4, slice(0, 3)), (1, 2, 4, slice(3, 5)), (2, 3, 4, slice(5, 6))]
                        for i, j0, j1, to in runs:
                            for n, (one_p, many_p) in enumerate(((p1, p2), (p2, p1))):
                                dst = prod[n][:, kind, :, :].rearrange("p (t h) c -> p t h c", t=NT)[:, :, :, to]
                                last = nc.gpsimd.tensor_tensor(
                                    dst, many_p[:, :, :, j0:j1],
                                    one_p[:, :, :, i:i + 1].broadcast_to([P, NT, H, j1 - j0]), ALU.mult)
                    last.then_inc(prods.sem, 1)

                def cross_products(jb):
                    wait(pool, prods, jb)
                    wait(pool, squares, jb - 1)
                    wait(pool, values, jb - 1)
                    nc.gpsimd.tensor_tensor(cross[:, 0], prod[0][:, 0], prod[1][:, 0], ALU.subtract)
                    parts = [t[:, 1, :, :].rearrange("p n (a c) -> p n a c", a=2) for t in (*prod, cross)]
                    nc.gpsimd.tensor_tensor(parts[2][:, :, :, 0:3:2], parts[1][:, :, :, 0:3:2], parts[0][:, :, :, 0:3:2],
                                            ALU.subtract)
                    nc.gpsimd.tensor_tensor(parts[2][:, :, :, 1], parts[0][:, :, :, 1], parts[1][:, :, :, 1],
                                            ALU.subtract).then_inc(crossed.sem, 1)

                def line_values(jb, par):
                    wait(pool, guessed, jb)
                    y = guess[:].bitcast(fp32)
                    flat = rnorm[:].rearrange("p k t h -> p (k t h)")
                    for n in range(3):
                        for k, (dst, one_in, two_in, op) in enumerate((
                                (newton[0][:], y, y, ALU.mult), (newton[1][:], newton[0][:], norm_half[:], ALU.mult),
                                (newton[0][:], newton[1][:], three_halves[:], ALU.add), (flat, newton[0][:], y, ALU.mult))):
                            nc.gpsimd.tensor_tensor(dst, one_in, two_in, op).then_inc(newton_step.sem, 1)
                            wait(pool, newton_step, jb, 4 * n + k + 1)
                        y = flat
                    nc.gpsimd.tensor_tensor(rscale[:], rnorm[:, 1], v["bscale"][:].unsqueeze(1).broadcast_to([P, NT, H]),
                                            ALU.mult).then_inc(rscaled.sem, 1)
                    wait(pool, rscaled, jb)
                    wait(pool, packed, jb - 2)
                    for n, (k, by) in enumerate((("k", rnorm[:, 0]), ("q", rscale[:]))):
                        for t in range(NT):
                            last = nc.gpsimd.tensor_tensor(
                                vals[k][par][:, :, t, :, DH + 6:NV],
                                cross[:, n, t * H:(t + 1) * H, :].rearrange("p (f h) c -> p f h c", f=NF),
                                by[:, t, :].rearrange("p (f h) -> p f h", f=NF).unsqueeze(3).broadcast_to([P, NF, 4, 6]),
                                ALU.mult)
                    last.then_inc(values.sem, 1)
                    wait(pool, values, jb)
                    for k, t, by in (("k", 0, v["decay_k"]), ("q", 1, v["decay_q"])):
                        last = nc.gpsimd.tensor_tensor(
                            vals[k][par][:, :, t, :, DH:DH + 6], vals[k][par][:, :, t, :, DH + 6:NV],
                            by[:].rearrange("p (f h) -> p f h", f=NF).unsqueeze(3).broadcast_to([P, NF, 4, 6]), ALU.mult)
                    last.then_inc(decayed.sem, 1)

                def split_rest(jb, par, f):
                    for n, k in enumerate("kq"):
                        src, dst = split_views(k, par, f)
                        wait(pool, hi_done, jb, 2 * f + n + 1)
                        nc.gpsimd.tensor_tensor(dst[:, :, 2 if k == "k" else 1, :], src, dst[:, :, 0, :].bitcast(fp32),
                                                ALU.subtract).then_inc(packed.sem, 1)

                pool.wait_ge(init, 1)
                iterations(pool, body)


def experts(nc, whole, sb, sem, signal, v):
    C, NC, TC = 512, NB * T // 512, 4
    x_all, h2_all, route_w, mod, ident = v["x_all"], v["h2_all"], v["route_w"], v["mod"], v["ident"]
    with whole.enter_context(ExitStack()) as stack:
        a = lambda name, shape, dt=fp32: sb(stack, name, shape, dt)
        raw = [a(f"raw{n}", [P, E * HF]) for n in range(2)]
        w_hi = [a(f"w_hi{n}", [P, E * HF], f32r) for n in range(2)]
        w_lo = [a(f"w_lo{n}", [P, E * HF], f32r) for n in range(2)]
        w3 = a("w3", [P, E * 2, D])
        x_hi = [a(f"x_hi{n}", [P, C], f32r) for n in range(2)]
        x_lo = [a(f"x_lo{n}", [P, C], f32r) for n in range(2)]
        act_u = [a(f"act_u{n}", [P, C]) for n in range(2)]
        hid = [[a(f"hid{n}{m}", [P, C]) for m in range(2)] for n in range(2)]
        acc = [a(f"acc{n}", [P, TC, D]) for n in range(2)]
        gated = a("gated", [P, C])
        result = [a(f"result{n}", [P, C]) for n in range(2)]
        diag = [a(f"diag{n}", [P, 2, D]) for n in range(2)]
        gate = [a(f"gate{n}", [P, 2, D]) for n in range(2)]
        ps = lambda name, shape: stack.enter_context(nc.psum_tensor(name, shape, fp32))
        up = [[ps(f"up{n}{m}", [P, C]) for m in range(2)] for n in range(2)]
        y = [ps(f"y{n}", [P, TC, D]) for n in range(2)]
        gate_ps = ps("gate_ps", [P, C])

        w_loaded, w3_loaded = sem("w_loaded"), sem("w3_loaded")
        w_high, w_low = sem("w_high"), sem("w_low")
        x_high, x_low = signal("x_high"), signal("x_low")
        up_ready, silued, hidden = signal("up_ready", 2 * E), signal("silued", 2 * E), signal("hidden", 2 * E)
        y_ready, y_added = signal("y_ready", E), signal("y_added", E)
        diag_ready, gate_ready, gate_done = signal("diag_ready"), signal("gate_ready"), signal("gate_done")
        scaled, summed, stored = signal("scaled"), signal("summed"), signal("stored", 16)

        def chunks(engine, body):
            for n in (0, 1):
                body(n, n)
            with engine.Fori(1, NC // 2 - 1) as i:
                body(i * 2, 0)
                body(i * 2 + 1, 1)
            for n in (NC - 2, NC - 1):
                body(n, n % 2)

        def last_chunk(ch):
            return isinstance(ch, int) and ch == NC - 1

        def first_chunk(ch):
            return isinstance(ch, int) and ch == 0

        outd = v["out"].rearrange("b (t p) d -> p (b t) d", p=P)

        with nc.Block() as block:
            @block.sync
            def _(sp):
                for n, w in enumerate(("W1", "W2")):
                    sp.dma_start(raw[n][:].rearrange("p (e h) -> p e h", e=E), v[w].rearrange("e d h -> d e h"))\
                      .then_inc(w_loaded, 16)
                sp.dma_start(w3[:], v["W3"].rearrange("e (m p) d -> p (e m) d", p=P)).then_inc(w3_loaded, 16)

                def body(ch, par):
                    wait(sp, summed, ch)
                    wait(sp, stored, ch - 1)
                    sp.dma_start(outd[:, span(ch * TC, TC), :], result[par][:].rearrange("p (t d) -> p t d", t=TC))\
                      .then_inc(stored.sem, 16)

                chunks(sp, body)
                wait(sp, stored, NC - 1)

            @block.tensor
            def _(pe):
                def down(ch, e):
                    wait(pe, hidden, ch, 2 * e + 2)
                    wait(pe, y_added, ch, e - 1)
                    for t in range(TC):
                        for m in range(2):
                            last = nc.tensor.matmul(y[e % 2][:, t, :], hid[e % 2][m][:, t * P:(t + 1) * P],
                                                    w3[:, 2 * e + m, :], start=(m == 0), stop=(m == 1))
                    last.then_inc(y_ready.sem, 1)

                def body(ch, par):
                    wait(pe, x_low, ch)
                    for e in range(E):
                        for m in range(2):
                            n = 2 * e + m
                            wait(pe, hidden, ch, n - 1)
                            cols = slice(n * P, (n + 1) * P)
                            for k in range(2):
                                for q, (w, xx) in enumerate(((w_hi, x_hi), (w_hi, x_lo), (w_lo, x_hi))):
                                    last = nc.tensor.matmul(up[m][k][:], w[k][:, cols], xx[par][:],
                                                            start=(q == 0), stop=(q == 2))
                            last.then_inc(up_ready.sem, 1)
                            if m == 0:
                                if e > 0:
                                    down(ch, e - 1)
                                elif not first_chunk(ch):
                                    down(ch - 1, E - 1)
                        if e == 2:
                            wait(pe, diag_ready, ch)
                            wait(pe, gate_done, ch - 1)
                            nc.tensor.matmul(gate_ps[:, 0:2 * D], v["ones"][:],
                                             diag[par][:].rearrange("p b d -> p (b d)"), start=True, stop=True)\
                              .then_inc(gate_ready.sem, 1)

                pe.wait_ge(w_low, 2)
                pe.wait_ge(w3_loaded, 16)
                chunks(pe, body)
                down(NC - 1, E - 1)

            @block.scalar
            def _(act):
                def split(ch, par):
                    wait(act, up_ready, ch - 2)
                    nc.scalar.activation(x_hi[par][:], h2_all[:, span(ch * C, C)], ACT.Copy).then_inc(x_high.sem, 1)

                def body(ch, par):
                    for e in range(E):
                        for m in range(2):
                            n = 2 * e + m
                            wait(act, up_ready, ch, n + 1)
                            wait(act, hidden, ch, n - 1)
                            nc.scalar.activation(act_u[m][:], up[m][0][:], ACT.Silu).then_inc(silued.sem, 1)
                        if e == 2:
                            wait(act, gate_ready, ch)
                            wait(act, scaled, ch - 2)
                            nc.scalar.activation(gate[par][:].rearrange("p b d -> p (b d)"), gate_ps[:, 0:2 * D],
                                                 ACT.Copy).then_inc(gate_done.sem, 1)
                        if e == 3 and not last_chunk(ch):
                            split(ch + 1, 1 - par)

                act.wait_ge(w_loaded, 32)
                for n in range(2):
                    nc.scalar.activation(w_hi[n][:], raw[n][:], ACT.Copy).then_inc(w_high, 1)
                split(0, 0)
                chunks(act, body)

            @block.vector
            def _(dve):
                def split(ch, par):
                    wait(dve, x_high, ch)
                    nc.vector.tensor_tensor(x_lo[par][:], h2_all[:, span(ch * C, C)], x_hi[par][:].bitcast(fp32),
                                            ALU.subtract).then_inc(x_low.sem, 1)

                def accumulate(ch, par, e):
                    wait(dve, y_ready, ch, e + 1)
                    if e == 0:
                        wait(dve, scaled, ch - 2)
                    else:
                        wait(dve, y_added, ch, e)
                    for t in range(TC):
                        weight = route_w[:, span(ch * (TC * E) + (t * E + e), 1)]
                        if e == 0:
                            last = nc.vector.tensor_scalar(acc[par][:, t, :], y[e % 2][:, t, :], weight, None, ALU.mult)
                        else:
                            last = nc.vector.scalar_tensor_tensor(
                                out=acc[par][:, t, :], in0=y[e % 2][:, t, :], scalar=weight, in1=acc[par][:, t, :],
                                op0=ALU.mult, op1=ALU.add)
                    last.then_inc(y_added.sem, 1)

                def body(ch, par):
                    for e in range(E):
                        for m in range(2):
                            n = 2 * e + m
                            wait(dve, silued, ch, n + 1)
                            wait(dve, y_ready, ch, e - 1)
                            nc.vector.tensor_tensor(hid[e % 2][m][:], act_u[m][:], up[m][1][:], ALU.mult)\
                              .then_inc(hidden.sem, 1)
                        if e > 0:
                            accumulate(ch, par, e - 1)
                        elif not first_chunk(ch):
                            accumulate(ch - 1, 1 - par, E - 1)
                        if e == 3 and not last_chunk(ch):
                            split(ch + 1, 1 - par)

                for n in range(2):
                    dve.wait_ge(w_high, n + 1)
                    nc.vector.tensor_tensor(w_lo[n][:], raw[n][:], w_hi[n][:].bitcast(fp32), ALU.subtract)\
                      .then_inc(w_low, 1)
                split(0, 0)
                chunks(dve, body)
                accumulate(NC - 1, (NC - 1) % 2, E - 1)

            @block.gpsimd
            def _(pool):
                def finish(ch, par):
                    wait(pool, y_added, ch)
                    wait(pool, gate_done, ch)
                    wait(pool, summed, ch - 1)
                    nc.gpsimd.tensor_tensor(
                        gated[:].rearrange("p (b t d) -> p b t d", b=2, t=NT),
                        acc[par][:].rearrange("p (b t) d -> p b t d", b=2),
                        gate[par][:].unsqueeze(2).broadcast_to([P, 2, NT, D]), ALU.mult).then_inc(scaled.sem, 1)
                    wait(pool, scaled, ch)
                    wait(pool, stored, ch - 2)
                    nc.gpsimd.tensor_tensor(result[par][:], gated[:], x_all[:, span(ch * C, C)], ALU.add)\
                      .then_inc(summed.sem, 1)

                def body(ch, par):
                    wait(pool, gate_ready, ch - 2)
                    for n in range(2):
                        last = nc.gpsimd.tensor_tensor(diag[par][:, n, :], ident[:], mod[:, 5, one(ch * 2 + n)].broadcast_to([P, D]), ALU.mult)
                    last.then_inc(diag_ready.sem, 1)
                    if not first_chunk(ch):
                        finish(ch - 1, 1 - par)

                chunks(pool, body)
                finish(NC - 1, (NC - 1) % 2)


_INS = ["x", "w_qkv", "b_qkv", "w1_write", "w2_write", "w1_read", "w2_read", "w_out", "b_out", "decay_logits", "bias_scale"]
_INS = ["L0_attn_" + n for n in _INS] + ["L0_ffn_Wg", "L0_ffn_W1", "L0_ffn_W2", "L0_ffn_W3", "L0_c", "L0_wmod"]


def kernel(**inputs):
    import numpy as _np
    import concourse.bacc as _bacc
    from concourse import mybir as _mybir
    from concourse.bass_utils import run_bass_kernel_spmd as _run

    nc = _bacc.Bacc("TRN2", target_bir_lowering=False, num_devices=1)
    arrays, args = {}, []
    for name in _INS:
        arr = _np.ascontiguousarray(inputs[name])
        arrays[f"in_{name}"] = arr
        args.append(nc.dram_tensor(f"in_{name}", arr.shape, _mybir.dt.from_np(arr.dtype), kind="ExternalInput").ap())
    out = nc.dram_tensor("out", (NB, T, D), _mybir.dt.float32, kind="ExternalOutput").ap()
    build(nc, *args, out)
    return _run(nc, [arrays], core_ids=[0]).results[0]["out"]
```

```python
import concourse.bass as bass
from concourse import mybir
from contextlib import ExitStack

fp32 = mybir.dt.float32
f32r = mybir.dt.float32r
bf16 = mybir.dt.bfloat16
i32 = mybir.dt.int32
u32 = mybir.dt.uint32
ALU = mybir.AluOpType
ACT = mybir.ActivationFunctionType
AX = mybir.AxisListType

P = 128
NB, T, D = 32, 256, 128
H, DH, PD = 16, 8, 4
NT = T // P
E, HF = 8, 256
NF = 4
PIECES, PX = 4, E // 4
NV = DH + 6 + 6
GR = 64
SCALE = float(DH) ** -0.5
EPS = 1e-5
MASK = -1e30


class Signal:

    def __init__(self, sem, per):
        self.sem, self.per = sem, per


def wait(eng, signal, batch, k=None):
    value = batch * signal.per + (signal.per if k is None else k)
    if not isinstance(value, int) or value > 0:
        eng.wait_ge(signal.sem, value)


def settle(eng, settled):
    eng.sem_inc(settled, 1)


JOBS = [
    (0, "k3", 0, 0), (0, "q3", 0, 1),
    (1, "norm", 2, 0), (1, "head1", -1, 1),
    (2, "k0", 1, 0), (2, "q0", 1, 1), (2, "line0", 2, 0),
    (3, "line1", 2, 1), (3, "max1", 0, 0), (3, "attnT", -1, 1),
    (4, "k1", 1, 0), (4, "q1", 1, 1), (4, "norm2", -2, 0),
    (5, "out", -1, 1), (5, "head0", 0, 0), (5, "qkv0", 2, 1),
    (6, "k2", 1, 0), (6, "q2", 1, 1), (6, "res", -1, 0),
    (7, "max0", 1, 1), (7, "qkv1", 2, 0), (7, "route", -2, 1),
]
SPLITS = (1, 2, 5, 6)
BANK = {name: bank for _, name, _, bank in JOBS}


def span(start, count):
    return slice(start, start + count) if isinstance(start, int) else bass.ds(start, count)


def one(batch):
    return span(batch, 1)


def live(batch):
    return not isinstance(batch, int) or 0 <= batch < NB


def before(n, b):
    bank, m = JOBS[n][3], n
    while True:
        m -= 1
        if m < 0:
            m, b = len(JOBS) - 1, b - 1
        if JOBS[m][3] == bank and live(b + JOBS[m][2]):
            return JOBS[m][1], b + JOBS[m][2]
        if isinstance(b, int) and b < -3:
            return None


def iterations(engine, body):
    for b in range(-2, 4):
        body(b, b % 2)
    with engine.Fori(2, NB // 2 - 1) as i:
        body(i * 2, 0)
        body(i * 2 + 1, 1)
    for b in range(NB - 2, NB + 3):
        body(b, b % 2)


def pair_heads(p):
    g = p % 2
    return g, [(4 * (p // 2) + g + 2 * n, 2 * (p // 2) + n) for n in range(2)]


def build(nc, x, w_qkv, b_qkv, w1_write, w2_write, w1_read, w2_read, w_out, b_out,
          decay_logits, bias_scale, Wg, W1, W2, W3, c, wmod, out):
    with ExitStack() as whole:
        def sb(stack, name, shape, dt=fp32):
            return stack.enter_context(nc.sbuf_tensor(name, shape, dt))

        def sem(name):
            return whole.enter_context(nc.semaphore(name))

        def signal(name, per=1):
            return Signal(sem(name), per)

        x_all = sb(whole, "x_all", [P, NB * NT * D])
        h2_all = sb(whole, "h2_all", [P, NB * T])
        route_w = sb(whole, "route_w", [P, NB * NT * E])
        mod = sb(whole, "mod", [P, 6, NB])
        ident = sb(whole, "ident", [P, P])
        ones = sb(whole, "ones", [P, P])
        w_first = [sb(whole, f"w_first{n}", [P, PX * HF]) for n in range(2)]
        first_loaded = sem("first_loaded")

        attention = whole.enter_context(ExitStack())
        a = lambda name, shape, dt=fp32: sb(attention, name, shape, dt)
        w_proj = a("w_proj", [P, 640])
        w_outT = a("w_outT", [P, P])
        bias_qkv = a("bias_qkv", [P, 3 * D])
        gate_bias = a("gate_bias", [P, NB])
        wg_sb = a("wg_sb", [P, E])
        identb = a("identb", [P, P], bf16)
        identr = a("identr", [P, P], f32r)
        causal = a("causal", [P, P], bf16)
        decay = a("decay", [P, H, P])
        decay_q = a("decay_q", [P, H])
        decay_k = a("decay_k", [P, H])
        bscale = a("bscale", [P, H])
        pick = a("pick", [P, 8, P], f32r)
        keep_f = a("keep_f", [P, 1])
        keep_i = a("keep_i", [P, 1])
        iota8 = a("iota8", [P, E])
        neg_half = a("neg_half", [P, NT])

        setup(nc, ExitStack(), sem, sb, locals())
        attend(nc, whole, attention, sb, sem, signal, locals())
        attention.close()
        experts(nc, whole, sb, sem, signal, locals())


def setup(nc, stack, sem, sb, v):
    x, mod, ident, ones = v["x"], v["mod"], v["ident"], v["ones"]
    w_proj, decay = v["w_proj"], v["decay"]
    with stack:
        s = lambda name, shape, dt=fp32: sb(stack, name, shape, dt)
        wq_raw = s("wq_raw", [P, 3, D])
        wl_raw = s("wl_raw", [PD * H, 4, D])
        wo_raw = s("wo_raw", [P, D])
        c_raw = s("c_raw", [NB, D])
        wmod_sb = s("wmod_sb", [P, 6 * D])
        bout = s("bout", [P, 1])
        logit = s("logit", [P, H])
        az = s("az", [P, H]); ez = s("ez", [P, H]); lz = s("lz", [P, H]); lam = s("lam", [P, H]); lam2 = s("lam2", [P, H])
        silu_c = s("silu_c", [P, NB])
        dist_i = s("dist_i", [P, P], i32); dist = s("dist", [P, P])
        col_i = s("col_i", [P, 1], i32); col = s("col", [P, 1]); rcol = s("rcol", [P, 1])
        e_i = s("e_i", [P, E], i32)
        mask0 = s("mask0", [P, P]); mask1 = s("mask1", [P, P])
        pick0 = s("pick0", [P, 8, P]); pick1 = s("pick1", [P, 8, P])
        kf = [s(f"kf{n}", [P, 1]) for n in range(7)]
        ga_abs = s("ga_abs", [P, 2, NB]); ga_sign = s("ga_sign", [P, 2, NB]); ga_two = s("ga_two", [P, 2, NB])
        tA = stack.enter_context(nc.psum_tensor("tA", [P, 512], fp32))
        tB = stack.enter_context(nc.psum_tensor("tB", [P, 512], fp32))
        tC = stack.enter_context(nc.psum_tensor("tC", [P, 512], fp32))

        ld_w, ld_c, ld_v, ld_x, ld_d = (sem(n) for n in ("ld_w", "ld_c", "ld_v", "ld_x", "ld_d"))
        pool_step, ident_ok, dist_ok, cols_ok = (sem(n) for n in ("pool_step", "ident_ok", "dist_ok", "cols_ok"))
        wT_ok, cT_ok, silu_ok, mod_ok, modded = (sem(n) for n in ("wT_ok", "cT_ok", "silu_ok", "mod_ok", "modded"))
        az_ok, ln_ok, lam_ok, arg_ok, exp_ok = (sem(n) for n in ("az_ok", "ln_ok", "lam_ok", "arg_ok", "exp_ok"))
        dve_step, act_step, setup_done = sem("dve_step"), sem("act_step"), sem("setup_done")
        xd = x.rearrange("b (t p) d -> p (b t) d", p=P)

        with nc.Block() as block:
            @block.sync
            def _(sp):
                sp.dma_start(wq_raw[:], v["w_qkv"].rearrange("(m p) d -> p m d", p=P)).then_inc(ld_w, 16)
                for n, w in enumerate(("w2_write", "w1_read", "w2_read", "w1_write")):
                    sp.dma_start(wl_raw[:, n, :], v[w]).then_inc(ld_w, 16)
                sp.dma_start(wo_raw[:], v["w_out"]).then_inc(ld_w, 16)
                for n in range(8):
                    k = NB * NT // 8
                    sp.dma_start(v["x_all"][:, n * k * D:(n + 1) * k * D].rearrange("p (n d) -> p n d", d=D), xd[:, n * k:(n + 1) * k, :]).then_inc(ld_x, 16)
                sp.wait_ge(ld_x, 128)

            @block.gpsimd
            def _(pool):
                n = [0]

                def step(ins):
                    ins.then_inc(pool_step, 1)
                    n[0] += 1
                    pool.wait_ge(pool_step, n[0])

                step(nc.gpsimd.memset(ident[:], 0.0))
                nc.gpsimd.affine_select(out=ident[:], in_=ident[:], compare_op=ALU.not_equal, fill=1.0, base=0,
                                        pattern=[[-1, P]], channel_multiplier=1).then_inc(ident_ok, 1)
                step(nc.gpsimd.iota(dist_i[:], pattern=[[1, P]], base=0, channel_multiplier=-1))
                nc.gpsimd.tensor_scalar(dist[:], dist_i[:], 0.0, None, ALU.max).then_inc(dist_ok, 1)
                step(nc.gpsimd.iota(col_i[:], pattern=[[0, 1]], base=0, channel_multiplier=1))
                step(nc.gpsimd.tensor_copy(col[:], col_i[:]))
                nc.gpsimd.tensor_scalar(rcol[:], col[:], -1.0, float(P), ALU.mult, ALU.add).then_inc(cols_ok, 1)
                step(nc.gpsimd.iota(e_i[:], pattern=[[1, E]], base=0, channel_multiplier=0))
                nc.gpsimd.tensor_copy(v["iota8"][:], e_i[:])
                nc.gpsimd.memset(v["neg_half"][:], -0.5)
                nc.gpsimd.memset(ones[:], 1.0)
                step(nc.gpsimd.memset(mask0[:], 0.0))
                step(nc.gpsimd.affine_select(out=mask1[:], in_=mask0[:], compare_op=ALU.is_ge, fill=MASK, base=0,
                                             pattern=[[-1, P]], channel_multiplier=1))
                nc.gpsimd.tensor_copy(v["causal"][:], mask1[:])
                step(nc.gpsimd.memset(pick0[:], 0.0))
                step(nc.gpsimd.affine_select(out=pick1[:], in_=pick0[:], compare_op=ALU.not_equal, fill=1.0, base=0,
                                             pattern=[[-1, 8], [0, P]], channel_multiplier=1))
                step(nc.gpsimd.affine_select(out=pick0[:], in_=pick1[:], compare_op=ALU.not_equal, fill=1.0, base=-GR,
                                             pattern=[[-1, 8], [0, P]], channel_multiplier=1))
                nc.gpsimd.tensor_copy(v["pick"][:], pick0[:])
                step(nc.gpsimd.tensor_scalar(kf[0][:], col[:], float(GR), float(-GR), ALU.is_ge, ALU.mult))
                step(nc.gpsimd.tensor_tensor(kf[1][:], col[:], kf[0][:], ALU.add))
                for k in range(3):
                    src = kf[1 + k]
                    step(nc.gpsimd.tensor_scalar(kf[5][:], src[:], float(NV), float(-NV), ALU.is_ge, ALU.mult))
                    step(nc.gpsimd.tensor_tensor(kf[2 + k][:], src[:], kf[5][:], ALU.add))
                nc.gpsimd.tensor_scalar(v["keep_f"][:], kf[4][:], float(DH + 6), None, ALU.is_lt)
                nc.gpsimd.tensor_scalar(v["keep_i"][:], kf[4][:], float(DH + 6), None, ALU.is_ge)
                nc.gpsimd.wait_ge(ident_ok, 1)
                nc.gpsimd.tensor_copy(v["identb"][:], ident[:]).then_inc(pool_step, 1)
                nc.gpsimd.tensor_copy(v["identr"][:], ident[:]).then_inc(pool_step, 1)
                pool.wait_ge(exp_ok, 1)
                nc.gpsimd.affine_select(out=decay[:], in_=decay[:], compare_op=ALU.is_gt, fill=0.0, base=0,
                                        pattern=[[0, H], [1, P]], channel_multiplier=-1).then_inc(setup_done, 1)
                pool.wait_ge(setup_done, 1)

            @block.tensor
            def _(pe):
                pe.wait_ge(ident_ok, 1)
                pe.wait_ge(ld_c, 16 * 2)
                nc.tensor.transpose(tC[:, 256:256 + NB], c_raw[:], ident[0:NB, 0:NB]).then_inc(cT_ok, 1)
                pe.wait_ge(ld_w, 16 * 6)
                for m in range(3):
                    nc.tensor.transpose(tA[:, m * P:(m + 1) * P], wq_raw[:, m, :], ident[:])
                nc.tensor.transpose(tA[:, 3 * P:4 * P], wo_raw[:], ident[:])
                for n in range(4):
                    last = nc.tensor.transpose(tB[:, n * 64:(n + 1) * 64], wl_raw[:, n, :], ident[0:64, 0:64])
                last.then_inc(wT_ok, 1)
                pe.wait_ge(silu_ok, 1)
                for m in range(6):
                    last = nc.tensor.matmul(tC[:, m * NB:(m + 1) * NB], wmod_sb[:, m * D:(m + 1) * D], silu_c[:],
                                            start=True, stop=True)
                last.then_inc(mod_ok, 1)

            @block.scalar
            def _(act):
                act.dma_start(c_raw[:], v["c"]).then_inc(ld_c, 16)
                act.dma_start(wmod_sb[:], v["wmod"]).then_inc(ld_c, 16)
                act.dma_start(logit[:], v["decay_logits"].rearrange("(a n) -> a n", a=1).broadcast_to([P, H])).then_inc(ld_d, 16)
                act.dma_start(v["bscale"][:], v["bias_scale"].rearrange("(a n) -> a n", a=1).broadcast_to([P, H])).then_inc(ld_v, 16)
                act.dma_start(v["bias_qkv"][:], v["b_qkv"].rearrange("(a n) -> a n", a=1).broadcast_to([P, 3 * D])).then_inc(ld_v, 16)
                act.dma_start(bout[:], v["b_out"].rearrange("(p a) -> p a", a=1)).then_inc(ld_v, 16)
                act.dma_start(v["wg_sb"][:], v["Wg"]).then_inc(ld_v, 16)
                act.wait_ge(cT_ok, 1)
                nc.scalar.activation(silu_c[:], tC[:, 256:256 + NB], ACT.Silu).then_inc(silu_ok, 1)
                act.wait_ge(az_ok, 1)
                nc.scalar.activation(ez[:], az[:], ACT.Exp, scale=-1.0).then_inc(act_step, 1)
                act.wait_ge(act_step, 1)
                nc.scalar.activation(lz[:], ez[:], ACT.Ln, bias=1.0).then_inc(ln_ok, 1)
                act.wait_ge(arg_ok, 1)
                nc.scalar.activation(v["decay_q"][:], v["decay_q"][:], ACT.Exp).then_inc(act_step, 1)
                nc.scalar.activation(v["decay_k"][:], v["decay_k"][:], ACT.Exp).then_inc(act_step, 1)
                nc.scalar.activation(decay[:], decay[:], ACT.Exp).then_inc(exp_ok, 1)
                act.wait_ge(ld_v, 64)

            @block.vector
            def _(dve):
                n = [0]

                def step(ins):
                    ins.then_inc(dve_step, 1)
                    n[0] += 1
                    dve.wait_ge(dve_step, n[0])

                dve.wait_ge(ld_d, 16)
                step(nc.vector.tensor_scalar(lam2[:], logit[:], -1.0, None, ALU.mult))
                nc.vector.tensor_tensor(az[:], logit[:], lam2[:], ALU.max).then_inc(az_ok, 1)
                dve.wait_ge(wT_ok, 1)
                nc.vector.tensor_scalar(w_proj[:, 0:P], tA[:, 0:P], SCALE, None, ALU.mult)
                nc.vector.tensor_copy(w_proj[:, P:3 * P], tA[:, P:3 * P])
                nc.vector.tensor_copy(v["w_outT"][:], tA[:, 3 * P:4 * P])
                for n4, rev in enumerate((True, False, False, True)):
                    dst = w_proj[:, 384 + 64 * n4:448 + 64 * n4].rearrange("p (h i) -> p h i", i=PD)
                    src = tB[:, 64 * n4:64 * n4 + 64].rearrange("p (h i) -> p h i", i=PD)
                    for i in range(PD):
                        nc.vector.tensor_copy(dst[:, :, i], src[:, :, PD - 1 - i if rev else i])
                dve.wait_ge(ld_v, 64)
                nc.vector.tensor_scalar(v["bias_qkv"][:, 0:D], v["bias_qkv"][:, 0:D], SCALE, None, ALU.mult)
                dve.wait_ge(ln_ok, 1)
                step(nc.vector.scalar_tensor_tensor(out=lam[:], in0=lam2[:], scalar=0.0, in1=lz[:], op0=ALU.max, op1=ALU.add))
                step(nc.vector.tensor_scalar(ez[:], lam[:], -1.0, None, ALU.mult))
                dve.wait_ge(dist_ok, 1)
                dve.wait_ge(cols_ok, 1)
                nc.vector.tensor_scalar(v["decay_q"][:], ez[:], col[:], None, ALU.mult)
                nc.vector.tensor_scalar(v["decay_k"][:], ez[:], rcol[:], None, ALU.mult)
                for h in range(H):
                    last = nc.vector.tensor_scalar(decay[:, h, :], dist[:], ez[:, h:h + 1], None, ALU.mult)
                last.then_inc(arg_ok, 1)
                dve.wait_ge(mod_ok, 1)
                step(nc.vector.tensor_copy(mod[:], tC[:, 0:6 * NB].rearrange("p (m b) -> p m b", b=NB)))
                for m in (1, 4):
                    nc.vector.tensor_scalar(mod[:, m, :], mod[:, m, :], 1.0, None, ALU.add)
                gates = mod[:, 2:6:3, :]
                nc.vector.tensor_scalar(ga_sign[:], gates, 0.0, 2.0, ALU.is_ge, ALU.mult)
                step(nc.vector.tensor_scalar(ga_two[:], gates, -1.0, None, ALU.mult))
                step(nc.vector.tensor_tensor(ga_abs[:], ga_two[:], gates, ALU.max))
                step(nc.vector.tensor_scalar(ga_two[:], ga_abs[:], 0.25, None, ALU.max))
                step(nc.vector.tensor_scalar(ga_abs[:], ga_sign[:], 1.0, None, ALU.subtract))
                step(nc.vector.tensor_tensor(gates, ga_abs[:], ga_two[:], ALU.mult))
                step(nc.vector.tensor_scalar(v["gate_bias"][:], mod[:, 2, :], bout[:], None, ALU.mult))


def attend(nc, whole, stack, sb, sem, signal, v):
    x_all, h2_all, mod, ident = v["x_all"], v["h2_all"], v["mod"], v["ident"]
    w_proj, w_outT, bias_qkv, decay = v["w_proj"], v["w_outT"], v["bias_qkv"], v["decay"]
    pick, causal, identb, identr, route_w = v["pick"], v["causal"], v["identb"], v["identr"], v["route_w"]
    with stack.enter_context(ExitStack()):
        a = lambda name, shape, dt=fp32: sb(stack, name, shape, dt)
        KT = [a(f"KT{n}", [P, 8, T], f32r) for n in range(2)]
        QF = [a(f"QF{n}", [P, 8, T], f32r) for n in range(2)]
        QI = [a(f"QI{n}", [P, 8, T], f32r) for n in range(2)]
        VP = [a(f"VP{n}", [P, NT, H, 32]) for n in range(2)]
        packs = {k: a("pack_" + k, [P, NF, NT, 4, GR], f32r) for k in "kq"}
        vals = {k: [a(f"val_{k}{n}", [P, NF, NT, 4, NV]) for n in range(2)] for k in "kq"}
        v_stage = a("v_stage", [P, NT, D])
        lines = a("lines", [P, NT, 256])
        prod = [a(f"prod{n}", [P, 2, NT * H, 6]) for n in range(2)]
        cross = a("cross", [P, 2, NT * H, 6])
        square = a("square", [P, 2, NT * H, 6])
        norm_sq = a("norm_sq", [P, 2 * NT * H])
        norm_cl = a("norm_cl", [P, 2 * NT * H])
        norm_half = a("norm_half", [P, 2 * NT * H])
        newton = [a(f"newton{n}", [P, 2 * NT * H]) for n in range(2)]
        three_halves = a("three_halves", [P, 1])
        bits = a("bits", [P, 2 * NT * H], i32)
        guess = a("guess", [P, 2 * NT * H], i32)
        rnorm = a("rnorm", [P, 2, NT, H])
        rscale = a("rscale", [P, NT, H])
        st1 = a("st1", [P, NT, 6]); mv1 = a("mv1", [P, NT, 2]); ve1 = a("ve1", [P, NT]); rs1 = a("rs1", [P, NT])
        st2 = a("st2", [P, NT, 6]); mv2 = a("mv2", [P, NT, 2]); ve2 = a("ve2", [P, NT]); rs2 = a("rs2", [P, NT])
        xhat = a("xhat", [P, NT, D])
        xhat2 = a("xhat2", [P, NT, D])
        hT = a("hT", [P, T + 1])
        mtok = [a(f"mtok{n}", [P, NT, P], f32r) for n in range(2)]
        MT = [a(f"MT{n}", [P, 3 * P], f32r) for n in range(2)]
        tt = [a(f"tt{n}", [P, 2, NT, P]) for n in range(2)]
        PT = [a(f"PT{n}", [P, 2, 3 * P]) for n in range(2)]
        headT = a("headT", [P, 2 * T])
        rden = a("rden", [P, NT, 8])
        attn = a("attn", [P, NT, D])
        attnT = a("attnT", [P, T])
        yT = a("yT", [P, T])
        h2T = a("h2T", [P, T])
        lg = a("lg", [P, NT, E]); top = a("top", [P, NT, 8]); topi = a("topi", [P, NT, 8], u32)
        topf = a("topf", [P, NT, 8]); gap = a("gap", [P, NT]); egap = a("egap", [P, NT]); eg1 = a("eg1", [P, NT])
        p12 = a("p12", [P, NT, 2]); hot = a("hot", [P, 2, NT, E])
        ps = lambda name, shape: stack.enter_context(nc.psum_tensor(name, shape, fp32))
        pre = ps("pre", [P, 2, 512])
        sc = ps("sc", [P, 2, 512])
        inc = ps("inc", [P, 2, NT, P])
        pv = ps("pv", [P, 2, T])
        bank = [ps(f"bank{n}", [P, 512]) for n in range(2)]

        ready = {j: signal("ready_" + j) for _, j, _, _ in JOBS}
        used = {j: signal("used_" + j) for _, j, _, _ in JOBS}
        zeroed, dve_settled, pool_settled = sem("zeroed"), sem("dve_settled"), sem("pool_settled")
        init = sem("init")
        stats, var, rstd, normed = signal("stats", 2), signal("var"), signal("rstd"), signal("normed")
        stats2, var2, rstd2, normed2 = signal("stats2", 2), signal("var2"), signal("rstd2"), signal("normed2")
        eps1, eps2, centred, centred2 = (signal(n) for n in ("eps1", "eps2", "centred", "centred2"))
        prods, crossed, squares, sums = signal("prods"), signal("crossed"), signal("squares"), signal("sums")
        clamped, halved, guessed = signal("clamped"), signal("halved"), signal("guessed")
        newton_step, rscaled = signal("newton_step", 12), signal("rscaled")
        values, decayed = signal("values"), signal("decayed")
        packed = signal("packed", 2 * NF)
        v_done, h2_kept = signal("v_done"), signal("h2_kept")
        hi_done = signal("hi_done", 2 * NF)
        pre_ready, maxed = signal("pre_ready", 8), signal("maxed", 8)
        inc_ready, weighed = signal("inc_ready", 8), signal("weighed", 8)
        sc_ready, added, exped, pv_ready = (signal(n, 8) for n in ("sc_ready", "added", "exped", "pv_ready"))
        head_out = signal("head_out", 2)
        recip = signal("recip", 2)
        route_step, hot_done = signal("route_step", 4), signal("hot_done")
        gapped, gap_exp, probs, chosen, routed = (signal(n) for n in ("gapped", "gap_exp", "probs", "chosen", "routed"))

        def split_views(k, par, f):
            return (vals[k][par][:, f, :, :, :].rearrange("p t h c -> p (t h) c"),
                    packs[k][:, f, :, :, 0:3 * NV].rearrange("p t h (c v) -> p (t h) c v", c=3))

        with nc.Block() as block:
            @block.sync
            def _(sp):
                for n, w in enumerate(("W1", "W2")):
                    sp.dma_start(v["w_first"][n][:].rearrange("p (e h) -> p e h", e=PX),
                                 v[w][0:PX].rearrange("e d h -> d e h")).then_inc(v["first_loaded"], 16)

            @block.tensor
            def _(pe):
                def diagonal(bank_pair, n):
                    return bank_pair[:, n, :].rearrange("p (t k) -> p t k", t=2)[:, :, 0:P]

                def incidences(b, par, p):
                    g, heads = pair_heads(p)
                    rows = slice(GR * g, GR * g + GR)
                    if p % 2 == 0:
                        wait(pe, used[f"q{p // 2}"], b)
                    wait(pe, weighed, b, p)
                    for n, (h, j) in enumerate(heads):
                        for t in range(NT):
                            blk = slice(t * P, (t + 1) * P)
                            last = nc.tensor.matmul(inc[:, n, t, :], KT[par][rows, j, blk], QI[par][rows, j, blk],
                                                    start=True, stop=True)
                    last.then_inc(inc_ready.sem, 1)

                def scores(b, par, p):
                    g, heads = pair_heads(p)
                    rows = slice(GR * g, GR * g + GR)
                    wait(pe, exped, b, p)
                    if p % 4 == 0:
                        wait(pe, used["max0" if p < 4 else "max1"], b)
                    for n, (h, j) in enumerate(heads):
                        nc.tensor.matmul(sc[:, n, 0:T], KT[par][rows, j, 0:P], QF[par][rows, j, :],
                                         start=True, stop=False)
                        nc.tensor.matmul(sc[:, n, T:3 * P], KT[par][rows, j, P:T], QF[par][rows, j, P:T],
                                         start=False, stop=False)
                        nc.tensor.matmul(diagonal(sc, n), causal[:], identb[:].unsqueeze(1).broadcast_to([P, 2, P]),
                                         start=False, stop=False)
                        last = nc.tensor.matmul(sc[:, n, 0:3 * P], pick[rows, h % 8, :], MT[p // 4][rows, :],
                                                start=False, stop=True)
                    last.then_inc(sc_ready.sem, 1)

                def prescores(b, par, p):
                    g, heads = pair_heads(p)
                    rows = slice(GR * g, GR * g + GR)
                    if p % 2 == 0:
                        wait(pe, used[f"k{p // 2}"], b)
                        wait(pe, used[f"q{p // 2}"], b)
                    wait(pe, maxed, b, p)
                    for n, (h, j) in enumerate(heads):
                        nc.tensor.matmul(pre[:, n, 0:P], QF[par][rows, j, 0:P], KT[par][rows, j, 0:P],
                                         start=True, stop=False)
                        nc.tensor.matmul(pre[:, n, P:3 * P], QF[par][rows, j, P:T], KT[par][rows, j, :],
                                         start=False, stop=False)
                        last = nc.tensor.matmul(diagonal(pre, n), identb[:],
                                                causal[:].unsqueeze(1).broadcast_to([P, 2, P]), start=False, stop=True)
                    last.then_inc(pre_ready.sem, 1)

                def values_out(b, par, p):
                    g, heads = pair_heads(p)
                    if p == 0:
                        wait(pe, v_done, b)
                    if p % 4 == 0:
                        wait(pe, head_out, b, p // 4)
                    wait(pe, exped, b, p + 1)
                    for n, (h, j) in enumerate(heads):
                        rows = slice(32 * (h % 4), 32 * (h % 4) + 32)
                        quad = (p % 4) // 2
                        nc.tensor.matmul(pv[rows, quad, :], VP[par][:, 0, h, :], PT[p % 2][:, n, 0:T],
                                         start=True, stop=False)
                        last = nc.tensor.matmul(pv[rows, quad, P:T], VP[par][:, 1, h, :], PT[p % 2][:, n, T:T + P],
                                                start=False, stop=True)
                    last.then_inc(pv_ready.sem, 1)

                def job(n, b, par):
                    _, name, off, bk = JOBS[n]
                    jb = b + off
                    if (was := before(n, b)) is not None:
                        wait(pe, used[was[0]], was[1])
                    B = bank[bk]
                    if name == "norm":
                        wait(pe, normed, jb)
                        for t in range(NT):
                            last = nc.tensor.transpose(B[:, t * P:(t + 1) * P], xhat[:, t, :], ident[:])
                    elif name[:-1] == "qkv":
                        t = int(name[-1])
                        wait(pe, used["norm"], jb)
                        last = nc.tensor.matmul(B[:, 0:384], hT[:, 1 + t * P:1 + (t + 1) * P], w_proj[:, 0:384],
                                                start=True, stop=True)
                    elif name[:-1] == "line":
                        t = int(name[-1])
                        wait(pe, used["norm"], jb)
                        nc.tensor.matmul(B[:, 0:192], hT[:, 1 + t * P:1 + (t + 1) * P], w_proj[:, 384:576],
                                         start=True, stop=True)
                        last = nc.tensor.matmul(B[:, 192:256], hT[:, t * P:(t + 1) * P], w_proj[:, 576:640],
                                                start=True, stop=True)
                    elif name[:-1] in ("k", "q"):
                        f = int(name[-1])
                        wait(pe, packed, jb, 2 * f + (1 if name[0] == "k" else 2))
                        for j in range(2):
                            for t in range(NT):
                                src = packs[name[0]][:, f, t, 2 * j:2 * j + 2, :].rearrange("p h r -> p (h r)")
                                last = nc.tensor.matmul(B[:, (2 * j + t) * P:(2 * j + t + 1) * P], src, identr[:],
                                                        start=True, stop=True)
                    elif name[:-1] == "max":
                        half = int(name[-1])
                        wait(pe, maxed, jb, 4 * half + 4)
                        for n3, t in enumerate((0, 1, 1)):
                            last = nc.tensor.matmul(B[:, n3 * P:(n3 + 1) * P], mtok[half][:, t, :], identr[:],
                                                    start=True, stop=True)
                    elif name[:-1] == "head":
                        wait(pe, head_out, jb, int(name[-1]) + 1)
                        for t in range(NT):
                            for quad in range(2):
                                last = nc.tensor.transpose(B[:, (2 * t + quad) * P:(2 * t + quad + 1) * P],
                                                           headT[:, quad * T + t * P:quad * T + (t + 1) * P], ident[:])
                    elif name == "attnT":
                        wait(pe, used["head1"], jb)
                        for t in range(NT):
                            last = nc.tensor.transpose(B[:, t * P:(t + 1) * P], attn[:, t, :], ident[:])
                    elif name == "out":
                        wait(pe, used["attnT"], jb)
                        last = nc.tensor.matmul(B[:, 0:T], w_outT[:], attnT[:], start=True, stop=True)
                    elif name == "res":
                        wait(pe, used["out"], jb)
                        for t in range(NT):
                            last = nc.tensor.transpose(B[:, t * P:(t + 1) * P], yT[:, t * P:(t + 1) * P], ident[:])
                    elif name == "norm2":
                        wait(pe, normed2, jb)
                        for t in range(NT):
                            last = nc.tensor.transpose(B[:, t * P:(t + 1) * P], xhat2[:, t, :], ident[:])
                    elif name == "route":
                        wait(pe, used["norm2"], jb)
                        for t in range(NT):
                            last = nc.tensor.matmul(B[:, t * E:(t + 1) * E], h2T[:, t * P:(t + 1) * P], v["wg_sb"][:],
                                                    start=True, stop=True)
                    last.then_inc(ready[name].sem, 1)

                def body(b, par):
                    for p in range(8):
                        if p == 0 and live(b) and not live(b - 1):
                            incidences(b, par, 0)
                        if live(b):
                            scores(b, par, p)
                        if p < 7 and live(b):
                            incidences(b, par, p + 1)
                        if p == 7 and live(b) and live(b + 1):
                            incidences(b + 1, 1 - par, 0)
                        small = [n for n, (slot, name, off, bk) in enumerate(JOBS) if slot == p and live(b + off)]
                        late = 1 if p == 1 else 0
                        for n in small[:1 - late]:
                            job(n, b, par)
                        if p < 3 and live(b):
                            prescores(b, par, p + 5)
                        if p >= 3 and live(b + 1):
                            prescores(b + 1, 1 - par, p - 3)
                        for n in small[1 - late:2 - late]:
                            job(n, b, par)
                        if p > 0 and live(b):
                            values_out(b, par, p - 1)
                        if p == 0 and live(b - 1):
                            values_out(b - 1, 1 - par, 7)
                        for n in small[2 - late:]:
                            job(n, b, par)

                pe.wait_ge(init, 1)
                iterations(pe, body)

            @block.vector
            def _(dve):
                def body(b, par):
                    for p in range(8):
                        if p == 0 and live(b) and not live(b - 1):
                            weigh(b, 0)
                        if live(b):
                            wait(dve, sc_ready, b, p + 1)
                            wait(dve, weighed, b, p + 1)
                            diag = sc[:, :, 0:512].rearrange("p n (t k) -> p n t k", t=2)[:, :, :, 0:P]
                            nc.vector.tensor_tensor(diag, diag, tt[p % 2][:], ALU.add).then_inc(added.sem, 1)
                        if p < 7 and live(b):
                            weigh(b, p + 1)
                        if p == 7 and live(b) and live(b + 1):
                            weigh(b + 1, 0)
                        if p == 0 and live(b + 2):
                            first_stats(b + 2)
                        pb, pp = (b, p + 5) if p < 3 else (b + 1, p - 3)
                        if live(pb):
                            half, i = pp // 4, 4 * ((pp % 4) // 2) + pp % 2
                            g = pp % 2
                            wait(dve, pre_ready, pb, pp + 1)
                            if pp % 4 == 0:
                                wait(dve, ready[f"max{half}"], pb - 1)
                            at = GR * g + i
                            nc.vector.reduce_max(mtok[half][:, 0, at:at + 3:2], pre[:, :, 0:P], AX.X)
                            nc.vector.reduce_max(mtok[half][:, 1, at:at + 3:2], pre[:, :, P:3 * P], AX.X)\
                              .then_inc(maxed.sem, 1)
                        extras(b, par, p)

                def weigh(b, p):
                    h0 = pair_heads(p)[1][0][0]
                    wait(dve, inc_ready, b, p + 1)
                    wait(dve, added, b, p - 1)
                    nc.vector.tensor_tensor(
                        tt[p % 2][:], inc[:], decay[:, h0:h0 + 3:2, :].unsqueeze(2).broadcast_to([P, 2, NT, P]),
                        ALU.mult).then_inc(weighed.sem, 1)

                def first_stats(jb):
                    wait(dve, normed, jb - 1)
                    settle(dve, dve_settled)
                    for t in range(NT):
                        nc.vector.bn_stats(st1[:, t, :], x_all[:, span(jb * T + t * D, D)]).then_inc(stats.sem, 1)
                    wait(dve, stats, jb, 2)
                    wait(dve, rstd, jb - 1)
                    settle(dve, dve_settled)
                    for t in range(NT):
                        last = nc.vector.bn_aggr(mv1[:, t, :], st1[:, t, :])
                    last.then_inc(var.sem, 1)

                def project(jb, par, t):
                    wait(dve, ready[f"qkv{t}"], jb)
                    if t == 0:
                        wait(dve, packed, jb - 2)
                        wait(dve, v_done, jb - 1)
                    B = bank[BANK[f"qkv{t}"]]
                    for n, k in enumerate("qk"):
                        nc.vector.tensor_tensor(
                            vals[k][par][:, :, t, :, 0:DH],
                            B[:, n * D:(n + 1) * D].rearrange("p (f h d) -> p f h d", f=NF, d=DH),
                            bias_qkv[:, n * D:(n + 1) * D].rearrange("p (f h d) -> p f h d", f=NF, d=DH), ALU.add)
                    nc.vector.tensor_tensor(v_stage[:, t, :], B[:, 2 * D:3 * D], bias_qkv[:, 2 * D:3 * D],
                                            ALU.add).then_inc(used[f"qkv{t}"].sem, 1)

                def extras(b, par, p):
                    if p == 1 and live(b - 1):
                        heads_norm(b - 1, 1)
                    if p == 1 and live(b - 3):
                        jb = b - 3
                        wait(dve, used["route"], jb)
                        settle(dve, dve_settled)
                        for t in range(NT):
                            last = nc.vector.max(top[:, t, :], lg[:, t, :])
                        last.then_inc(route_step.sem, 1)
                        wait(dve, route_step, jb, 1)
                        settle(dve, dve_settled)
                        for t in range(NT):
                            nc.vector.max_index(topi[:, t, :], top[:, t, :], lg[:, t, :])
                        wait(dve, gap_exp, jb - 1)
                        nc.vector.tensor_tensor(gap[:], top[:, :, 1], top[:, :, 0], ALU.subtract).then_inc(gapped.sem, 1)
                        wait(dve, gapped, jb)
                    if p == 3 and live(b - 3):
                        nc.vector.tensor_copy(topf[:], topi[:]).then_inc(chosen.sem, 1)
                        wait(dve, gap_exp, b - 3)
                        nc.vector.tensor_scalar(eg1[:], egap[:], 1.0, None, ALU.add).then_inc(route_step.sem, 1)
                    if p == 3 and live(b - 3):
                        jb = b - 3
                        wait(dve, route_step, jb, 2)
                        nc.vector.reciprocal(p12[:, :, 0], eg1[:]).then_inc(route_step.sem, 1)
                        wait(dve, route_step, jb, 3)
                        nc.vector.tensor_tensor(p12[:, :, 1], p12[:, :, 0], egap[:], ALU.mult).then_inc(probs.sem, 1)
                        wait(dve, chosen, jb)
                        wait(dve, probs, jb)
                        nc.vector.tensor_tensor(
                            hot[:], v["iota8"][:].unsqueeze(1).unsqueeze(1).broadcast_to([P, 2, NT, E]),
                            topf[:, :, 0:2].rearrange("p t n -> p n t").unsqueeze(3).broadcast_to([P, 2, NT, E]),
                            ALU.is_equal).then_inc(route_step.sem, 1)
                        wait(dve, route_step, jb, 4)
                        nc.vector.tensor_tensor(
                            hot[:], hot[:], p12[:].rearrange("p t n -> p n t").unsqueeze(3).broadcast_to([P, 2, NT, E]),
                            ALU.mult).then_inc(hot_done.sem, 1)
                        wait(dve, hot_done, jb)
                        nc.vector.tensor_tensor(route_w[:, span(jb * (NT * E), NT * E)],
                                                hot[:, 0].rearrange("p t e -> p (t e)"),
                                                hot[:, 1].rearrange("p t e -> p (t e)"), ALU.add).then_inc(routed.sem, 1)
                    if p == 5:
                        if live(b):
                            heads_norm(b, 0)
                        if live(b + 2):
                            wait(dve, squares, b + 2)
                            wait(dve, clamped, b + 1)
                            nc.vector.reduce_sum(norm_sq[:], square[:].rearrange("p k n c -> p (k n) c"), AX.X)\
                              .then_inc(sums.sem, 1)
                            wait(dve, sums, b + 2)
                            wait(dve, newton_step, b + 1)
                            nc.vector.tensor_scalar(norm_cl[:], norm_sq[:], 1e-24, None, ALU.max)
                            nc.vector.tensor_scalar(norm_half[:], norm_sq[:], 1e-24, -0.5, ALU.max, ALU.mult)\
                              .then_inc(clamped.sem, 1)
                            wait(dve, clamped, b + 2)
                            nc.vector.tensor_scalar(bits[:], norm_cl[:].bitcast(i32), 1, None, ALU.logical_shift_right)\
                              .then_inc(halved.sem, 1)
                            project(b + 2, par, 0)
                            wait(dve, halved, b + 2)
                            nc.vector.tensor_scalar(guess[:], bits[:], -1.0, float(0x5F3759DF), ALU.mult, ALU.add)\
                              .then_inc(guessed.sem, 1)
                    if p == 6 and live(b - 1):
                        jb = b - 1
                        wait(dve, ready["res"], jb)
                        xs = x_all[:, span(jb * T, T)]
                        nc.vector.tensor_tensor(xs, bank[BANK["res"]][:, 0:T], xs, ALU.add).then_inc(used["res"].sem, 1)
                        wait(dve, used["res"], jb)
                        wait(dve, normed2, jb - 1)
                        settle(dve, dve_settled)
                        for t in range(NT):
                            nc.vector.bn_stats(st2[:, t, :], x_all[:, span(jb * T + t * D, D)]).then_inc(stats2.sem, 1)
                        wait(dve, stats2, jb, 2)
                        wait(dve, rstd2, jb - 1)
                        settle(dve, dve_settled)
                        for t in range(NT):
                            last = nc.vector.bn_aggr(mv2[:, t, :], st2[:, t, :])
                        last.then_inc(var2.sem, 1)
                    if p == 7 and live(b + 2):
                        project(b + 2, par, 1)
                    if p == 7 and live(b - 2):
                        jb = b - 2
                        wait(dve, ready["route"], jb)
                        B = bank[BANK["route"]]
                        nc.vector.tensor_copy(lg[:], B[:, 0:NT * E].rearrange("p (t e) -> p t e", t=NT))\
                          .then_inc(used["route"].sem, 1)

                def heads_norm(jb, half):
                    wait(dve, ready[f"head{half}"], jb)
                    wait(dve, used[f"head{1 - half}"], jb if half else jb - 1)
                    B = bank[BANK[f"head{half}"]][:, :].rearrange("p (t q r) -> p t q r", t=NT, r=32)
                    nc.vector.reciprocal(rden[:], B[:, :, :, DH]).then_inc(recip.sem, 1)
                    wait(dve, recip, jb, half + 1)
                    if half == 0:
                        wait(dve, ready["attnT"], jb - 1)
                    nc.vector.tensor_tensor(
                        attn[:, :, 64 * half:64 * half + 64].rearrange("p t (q d) -> p t q d", d=DH), B[:, :, :, 0:DH],
                        rden[:].unsqueeze(3).broadcast_to([P, NT, 8, DH]), ALU.mult).then_inc(used[f"head{half}"].sem, 1)

                nc.vector.memset(three_halves[:], 1.5)
                for n in range(2):
                    nc.vector.memset(mtok[n][:].bitcast(fp32), 0.0)
                    nc.vector.memset(VP[n][:], 0.0)
                    nc.vector.memset(vals["k"][n][:, :, 1, :, DH:DH + 6], 0.0)
                    nc.vector.memset(vals["q"][n][:, :, 0, :, DH:DH + 6], 0.0)
                for k in "kq":
                    nc.vector.memset(packs[k][:, :, :, :, 3 * NV:GR].bitcast(fp32), 0.0)
                nc.vector.memset(hT[:, 0:1], 0.0).then_inc(zeroed, 1)
                dve.wait_ge(zeroed, 1)
                for n in range(2):
                    last = nc.vector.memset(VP[n][:, :, :, DH:DH + 1], 1.0)
                last.then_inc(init, 1)
                dve.wait_ge(init, 1)
                iterations(dve, body)

            @block.scalar
            def _(act):
                def evacuate(name, b, par):
                    B = bank[BANK[name]]
                    wait(act, ready[name], b)
                    done = used[name].sem
                    if name == "norm":
                        nc.scalar.activation(hT[:, 1:T + 1], B[:, 0:T], ACT.Identity, bias=mod[:, 0, one(b)],
                                             scale=mod[:, 1, one(b)]).then_inc(done, 1)
                    elif name[:-1] == "line":
                        t = int(name[-1])
                        if t == 0:
                            wait(act, prods, b - 1)
                        nc.scalar.activation(lines[:, t, :], B[:, 0:256], ACT.Copy).then_inc(done, 1)
                    elif name[:-1] == "k":
                        f = int(name[-1])
                        nc.scalar.activation(KT[par][:, 2 * f:2 * f + 2, :],
                                             B[:, :].rearrange("p (j t) -> p j t", j=2), ACT.Copy).then_inc(done, 1)
                    elif name[:-1] == "q":
                        f = int(name[-1])
                        src = B[:, :].rearrange("p (j t) -> p j t", j=2)
                        nc.scalar.activation(QF[par][:, 2 * f:2 * f + 2, :], src, ACT.Copy, scale=v["keep_f"][:])
                        nc.scalar.activation(QI[par][:, 2 * f:2 * f + 2, :], src, ACT.Copy,
                                             scale=v["keep_i"][:]).then_inc(done, 1)
                    elif name[:-1] == "max":
                        half = int(name[-1])
                        wait(act, sc_ready, b - 1, 4 * half + 4)
                        nc.scalar.activation(MT[half][:], B[:, 0:3 * P], ACT.Copy, scale=-1.0).then_inc(done, 1)
                    elif name == "attnT":
                        nc.scalar.activation(attnT[:], B[:, 0:T], ACT.Copy).then_inc(done, 1)
                    elif name == "out":
                        wait(act, ready["res"], b - 1)
                        nc.scalar.activation(yT[:], B[:, 0:T], ACT.Identity, bias=v["gate_bias"][:, one(b)],
                                             scale=mod[:, 2, one(b)]).then_inc(done, 1)
                    elif name == "norm2":
                        wait(act, ready["route"], b - 1)
                        wait(act, h2_kept, b - 1)
                        nc.scalar.activation(h2T[:], B[:, 0:T], ACT.Identity, bias=mod[:, 3, one(b)],
                                             scale=mod[:, 4, one(b)]).then_inc(done, 1)

                def split_high(jb, par, f):
                    if f == 0:
                        wait(act, decayed, jb)
                        wait(act, used["qkv1"], jb)
                    for n, k in enumerate("kq"):
                        wait(act, ready[f"{k}{f}"], jb - 1)
                        src, dst = split_views(k, par, f)
                        high = slice(0, 2) if k == "k" else slice(0, 3, 2)
                        nc.scalar.activation(dst[:, :, high, :], src.unsqueeze(2).broadcast_to([P, NT * 4, 2, NV]),
                                             ACT.Copy).then_inc(hi_done.sem, 1)

                def exponentials(b, p):
                    wait(act, added, b, p + 1)
                    wait(act, pv_ready, b, p - 1)
                    nc.scalar.activation(PT[p % 2][:], sc[:, :, 0:3 * P], ACT.Exp).then_inc(exped.sem, 1)

                def heads_out(jb, half):
                    wait(act, pv_ready, jb, 4 * half + 4)
                    wait(act, ready[f"head{1 - half}"], jb if half else jb - 1)
                    nc.scalar.activation(headT[:], pv[:, :, :].rearrange("p q t -> p (q t)"),
                                         ACT.Copy).then_inc(head_out.sem, 1)

                def body(b, par):
                    for p in range(8):
                        small = [(name, off) for slot, name, off, bk in JOBS if slot == p and live(b + off)]
                        for n in range(3):
                            if n == 2 and p == 0 and live(b - 1):
                                heads_out(b - 1, 1)
                            if n == 2 and p == 4 and live(b):
                                heads_out(b, 0)
                            if n == 0 and p in (1, 5) and live(b):
                                exponentials(b, p)
                            if n < len(small):
                                name, off = small[n]
                                if name[:-1] not in ("qkv", "head") and name not in ("res", "route"):
                                    evacuate(name, b + off, (par + off) % 2)
                            if n == 0 and p not in (1, 5) and live(b):
                                exponentials(b, p)
                        if p == 5 and live(b + 2):
                            wait(act, crossed, b + 2)
                            wait(act, sums, b + 1)
                            nc.scalar.activation(square[:], cross[:], ACT.Square).then_inc(squares.sem, 1)
                        if p in SPLITS and live(b + 1):
                            split_high(b + 1, 1 - par, SPLITS.index(p))
                        if p == 1 and live(b + 1):
                            wait(act, used["qkv1"], b + 1)
                            wait(act, pv_ready, b - 1)
                            nc.scalar.activation(VP[1 - par][:, :, :, 0:DH].rearrange("p t h d -> p (t h) d"),
                                                 v_stage[:].rearrange("p t (h d) -> p (t h) d", d=DH),
                                                 ACT.Copy).then_inc(v_done.sem, 1)
                        if p == 2 and live(b - 3):
                            wait(act, gapped, b - 3)
                            wait(act, probs, b - 4)
                            nc.scalar.activation(egap[:], gap[:], ACT.Exp).then_inc(gap_exp.sem, 1)

                act.wait_ge(init, 1)
                iterations(act, body)

            @block.gpsimd
            def _(pool):
                def body(b, par):
                    for p in range(8):
                        if p == 0 and live(b + 2):
                            inverse_std(b + 2, var, mv1, ve1, eps1, rs1, rstd)
                            normalise(b + 2, rstd, mv1, rs1, xhat, centred, normed, ready["norm"])
                        if p == 0 and live(b - 2):
                            inverse_std(b - 2, var2, mv2, ve2, eps2, rs2, rstd2)
                            normalise(b - 2, rstd2, mv2, rs2, xhat2, centred2, normed2, ready["norm2"])
                        if p == 4 and live(b + 2):
                            cross_products(b + 2)
                        if p in SPLITS[:3] and live(b + 1):
                            split_rest(b + 1, 1 - par, SPLITS.index(p))
                        if p == 5 and live(b - 2):
                            wait(pool, used["norm2"], b - 2)
                            nc.gpsimd.tensor_copy(h2_all[:, span((b - 2) * T, T)], h2T[:]).then_inc(h2_kept.sem, 1)
                        if p == 3 and live(b + 2):
                            products(b + 2)
                        if p == 6 and live(b + 2):
                            inverse_norms(b + 2)
                        if p == 6 and live(b + 1):
                            split_rest(b + 1, 1 - par, 3)
                        if p == 6 and live(b + 2):
                            line_values(b + 2, par)

                def inverse_std(jb, var, mv, ve, eps_done, rs, done):
                    wait(pool, var, jb)
                    settle(pool, pool_settled)
                    nc.gpsimd.tensor_scalar(ve[:], mv[:, :, 1], EPS, None, ALU.add).then_inc(eps_done.sem, 1)
                    wait(pool, eps_done, jb)
                    wait(pool, normed if done is rstd else normed2, jb - 1)
                    nc.gpsimd.tensor_tensor(rs[:], ve[:], v["neg_half"][:], ALU.pow).then_inc(done.sem, 1)

                def normalise(jb, rstd, mv, rs, xhat, centred, done, read):
                    each = [P, NT, D]
                    wait(pool, read, jb - 1)
                    nc.gpsimd.tensor_tensor(xhat[:], x_all[:, span(jb * T, T)].rearrange("p (t d) -> p t d", t=NT),
                                            mv[:, :, 0:1].broadcast_to(each), ALU.subtract).then_inc(centred.sem, 1)
                    wait(pool, rstd, jb)
                    wait(pool, centred, jb)
                    nc.gpsimd.tensor_tensor(xhat[:], xhat[:], rs[:].unsqueeze(2).broadcast_to(each), ALU.mult)\
                      .then_inc(done.sem, 1)

                def products(jb):
                    wait(pool, used["line1"], jb)
                    wait(pool, crossed, jb - 1)
                    col = {k: lines[:, :, 64 * k:64 * k + 64].rearrange("p t (h i) -> p t h i", i=PD) for k in range(4)}
                    for kind, p1, p2 in ((0, col[3], col[0]), (1, col[1], col[2])):
                        runs = [(0, 1, 3, slice(0, 2)), (0, 3, 4, slice(3, 4)), (1, 2, 4, slice(2, 5, 2)), (2, 3, 4, slice(5, 6))] \
                            if kind == 0 else [(0, 1, 4, slice(0, 3)), (1, 2, 4, slice(3, 5)), (2, 3, 4, slice(5, 6))]
                        for i, j0, j1, to in runs:
                            for n, (one_p, many_p) in enumerate(((p1, p2), (p2, p1))):
                                dst = prod[n][:, kind, :, :].rearrange("p (t h) c -> p t h c", t=NT)[:, :, :, to]
                                last = nc.gpsimd.tensor_tensor(
                                    dst, many_p[:, :, :, j0:j1],
                                    one_p[:, :, :, i:i + 1].broadcast_to([P, NT, H, j1 - j0]), ALU.mult)
                    last.then_inc(prods.sem, 1)

                def cross_products(jb):
                    wait(pool, prods, jb)
                    wait(pool, squares, jb - 1)
                    wait(pool, values, jb - 1)
                    nc.gpsimd.tensor_tensor(cross[:, 0], prod[0][:, 0], prod[1][:, 0], ALU.subtract)
                    parts = [t[:, 1, :, :].rearrange("p n (a c) -> p n a c", a=2) for t in (*prod, cross)]
                    nc.gpsimd.tensor_tensor(parts[2][:, :, :, 0:3:2], parts[1][:, :, :, 0:3:2], parts[0][:, :, :, 0:3:2],
                                            ALU.subtract)
                    nc.gpsimd.tensor_tensor(parts[2][:, :, :, 1], parts[0][:, :, :, 1], parts[1][:, :, :, 1],
                                            ALU.subtract).then_inc(crossed.sem, 1)

                def inverse_norms(jb):
                    wait(pool, guessed, jb)
                    y = guess[:].bitcast(fp32)
                    flat = rnorm[:].rearrange("p k t h -> p (k t h)")
                    for n in range(3):
                        for k, (dst, one_in, two_in, op) in enumerate((
                                (newton[0][:], y, y, ALU.mult), (newton[1][:], newton[0][:], norm_half[:], ALU.mult),
                                (newton[0][:], newton[1][:], three_halves[:].broadcast_to([P, 2 * NT * H]), ALU.add), (flat, newton[0][:], y, ALU.mult))):
                            nc.gpsimd.tensor_tensor(dst, one_in, two_in, op).then_inc(newton_step.sem, 1)
                            wait(pool, newton_step, jb, 4 * n + k + 1)
                        y = flat
                    nc.gpsimd.tensor_tensor(rscale[:], rnorm[:, 1], v["bscale"][:].unsqueeze(1).broadcast_to([P, NT, H]),
                                            ALU.mult).then_inc(rscaled.sem, 1)

                def line_values(jb, par):
                    wait(pool, rscaled, jb)
                    wait(pool, packed, jb - 2)
                    for n, (k, by) in enumerate((("k", rnorm[:, 0]), ("q", rscale[:]))):
                        for t in range(NT):
                            last = nc.gpsimd.tensor_tensor(
                                vals[k][par][:, :, t, :, DH + 6:NV],
                                cross[:, n, t * H:(t + 1) * H, :].rearrange("p (f h) c -> p f h c", f=NF),
                                by[:, t, :].rearrange("p (f h) -> p f h", f=NF).unsqueeze(3).broadcast_to([P, NF, 4, 6]),
                                ALU.mult)
                    last.then_inc(values.sem, 1)
                    wait(pool, values, jb)
                    for k, t, by in (("k", 0, v["decay_k"]), ("q", 1, v["decay_q"])):
                        last = nc.gpsimd.tensor_tensor(
                            vals[k][par][:, :, t, :, DH:DH + 6], vals[k][par][:, :, t, :, DH + 6:NV],
                            by[:].rearrange("p (f h) -> p f h", f=NF).unsqueeze(3).broadcast_to([P, NF, 4, 6]), ALU.mult)
                    last.then_inc(decayed.sem, 1)

                def split_rest(jb, par, f):
                    for n, k in enumerate("kq"):
                        src, dst = split_views(k, par, f)
                        wait(pool, hi_done, jb, 2 * f + n + 1)
                        nc.gpsimd.tensor_tensor(dst[:, :, 2 if k == "k" else 1, :], src, dst[:, :, 0, :].bitcast(fp32),
                                                ALU.subtract).then_inc(packed.sem, 1)

                pool.wait_ge(init, 1)
                iterations(pool, body)


def experts(nc, whole, sb, sem, signal, v):
    C, NC, TC = 512, NB * T // 512, 4
    x_all, h2_all, route_w, mod, ident = v["x_all"], v["h2_all"], v["route_w"], v["mod"], v["ident"]
    with whole.enter_context(ExitStack()) as stack:
        a = lambda name, shape, dt=fp32: sb(stack, name, shape, dt)
        raw = [a(f"raw{n}", [P, E * HF]) for n in range(2)]
        w_hi = [a(f"w_hi{n}", [P, E * HF], f32r) for n in range(2)]
        w_lo = [a(f"w_lo{n}", [P, E * HF], f32r) for n in range(2)]
        w3 = a("w3", [P, E * 2, D])
        x_hi = [a(f"x_hi{n}", [P, C], f32r) for n in range(2)]
        x_lo = [a(f"x_lo{n}", [P, C], f32r) for n in range(2)]
        act_u = [a(f"act_u{n}", [P, C]) for n in range(2)]
        hid = [[a(f"hid{n}{m}", [P, C]) for m in range(2)] for n in range(2)]
        acc = [a(f"acc{n}", [P, TC, D]) for n in range(2)]
        gated = a("gated", [P, C])
        result = [a(f"result{n}", [P, C]) for n in range(2)]
        diag = [a(f"diag{n}", [P, 2, D]) for n in range(2)]
        gate = [a(f"gate{n}", [P, 2, D]) for n in range(2)]
        ps = lambda name, shape: stack.enter_context(nc.psum_tensor(name, shape, fp32))
        up = [[ps(f"up{n}{m}", [P, C]) for m in range(2)] for n in range(2)]
        y = [ps(f"y{n}", [P, TC, D]) for n in range(2)]
        gate_ps = ps("gate_ps", [P, C])

        PC = PX * HF
        w_loaded = [v["first_loaded"]] + [sem(f"w_loaded{k}") for k in range(1, PIECES)]
        w3_loaded = sem("w3_loaded")
        w_high, w_low = sem("w_high"), sem("w_low")
        x_high, x_low = signal("x_high"), signal("x_low")
        up_ready, silued, hidden = signal("up_ready", 2 * E), signal("silued", 2 * E), signal("hidden", 2 * E)
        y_ready, y_added = signal("y_ready", E), signal("y_added", E)
        diag_ready, gate_ready, gate_done = signal("diag_ready"), signal("gate_ready"), signal("gate_done")
        scaled, summed, stored = signal("scaled"), signal("summed"), signal("stored", 16)

        def chunks(engine, body):
            for n in (0, 1):
                body(n, n)
            with engine.Fori(1, NC // 2 - 1) as i:
                body(i * 2, 0)
                body(i * 2 + 1, 1)
            for n in (NC - 2, NC - 1):
                body(n, n % 2)

        def piece(n, k):
            return v["w_first"][n][:] if k == 0 else raw[n][:, k * PC:(k + 1) * PC]

        def last_chunk(ch):
            return isinstance(ch, int) and ch == NC - 1

        def first_chunk(ch):
            return isinstance(ch, int) and ch == 0

        outd = v["out"].rearrange("b (t p) d -> p (b t) d", p=P)

        with nc.Block() as block:
            @block.sync
            def _(sp):
                for k in range(1, PIECES):
                    for n, w in enumerate(("W1", "W2")):
                        sp.dma_start(raw[n][:, k * PC:(k + 1) * PC].rearrange("p (e h) -> p e h", e=PX),
                                     v[w][k * PX:(k + 1) * PX].rearrange("e d h -> d e h")).then_inc(w_loaded[k], 16)

                def body(ch, par):
                    wait(sp, summed, ch)
                    wait(sp, stored, ch - 1)
                    sp.dma_start(outd[:, span(ch * TC, TC), :], result[par][:].rearrange("p (t d) -> p t d", t=TC))\
                      .then_inc(stored.sem, 16)

                chunks(sp, body)
                wait(sp, stored, NC - 1)

            @block.tensor
            def _(pe):
                def down(ch, e):
                    wait(pe, y_added, ch, e - 1)
                    for m in range(2):
                        wait(pe, hidden, ch, 2 * e + m + 1)
                        for t in range(TC):
                            last = nc.tensor.matmul(y[e % 2][:, t, :], hid[e % 2][m][:, t * P:(t + 1) * P],
                                                    w3[:, 2 * e + m, :], start=(m == 0 and t == 0),
                                                    stop=(m == 1 and t == TC - 1))
                    last.then_inc(y_ready.sem, 1)

                def body(ch, par):
                    wait(pe, x_low, ch)
                    for e in range(E):
                        if first_chunk(ch) and e % PX == 0:
                            pe.wait_ge(w_low, 2 * (e // PX) + 2)
                        if first_chunk(ch) and e == 1:
                            pe.wait_ge(w3_loaded, 16)
                        for m in range(2):
                            n = 2 * e + m
                            wait(pe, hidden, ch, n - 1)
                            cols = slice(n * P, (n + 1) * P)
                            for k in range(2):
                                for q, (w, xx) in enumerate(((w_hi, x_hi), (w_hi, x_lo), (w_lo, x_hi))):
                                    last = nc.tensor.matmul(up[m][k][:], w[k][:, cols], xx[par][:],
                                                            start=(q == 0), stop=(q == 2))
                            last.then_inc(up_ready.sem, 1)
                            if m == 0:
                                if e > 0:
                                    down(ch, e - 1)
                                elif not first_chunk(ch):
                                    down(ch - 1, E - 1)
                        if e == 2:
                            wait(pe, diag_ready, ch)
                            wait(pe, gate_done, ch - 1)
                            nc.tensor.matmul(gate_ps[:, 0:2 * D], v["ones"][:],
                                             diag[par][:].rearrange("p b d -> p (b d)"), start=True, stop=True)\
                              .then_inc(gate_ready.sem, 1)

                chunks(pe, body)
                down(NC - 1, E - 1)

            @block.scalar
            def _(act):
                def split(ch, par):
                    wait(act, up_ready, ch - 2)
                    nc.scalar.activation(x_hi[par][:], h2_all[:, span(ch * C, C)], ACT.Copy).then_inc(x_high.sem, 1)

                def body(ch, par):
                    for e in range(E):
                        for m in range(2):
                            n = 2 * e + m
                            wait(act, up_ready, ch, n + 1)
                            wait(act, hidden, ch, n - 1)
                            nc.scalar.activation(act_u[m][:], up[m][0][:], ACT.Silu).then_inc(silued.sem, 1)
                        if e == 2:
                            wait(act, gate_ready, ch)
                            wait(act, scaled, ch - 2)
                            nc.scalar.activation(gate[par][:].rearrange("p b d -> p (b d)"), gate_ps[:, 0:2 * D],
                                                 ACT.Copy).then_inc(gate_done.sem, 1)
                        if e == 3 and not last_chunk(ch):
                            split(ch + 1, 1 - par)
                        if first_chunk(ch) and e % PX == 0 and e // PX + 1 < PIECES:
                            weights_high(e // PX + 1)

                def weights_high(k):
                    act.wait_ge(w_loaded[k], 32)
                    for n in range(2):
                        nc.scalar.activation(w_hi[n][:, k * PC:(k + 1) * PC], piece(n, k), ACT.Copy).then_inc(w_high, 1)

                act.dma_start(w3[:], v["W3"].rearrange("e (m p) d -> p (e m) d", p=P)).then_inc(w3_loaded, 16)
                split(0, 0)
                weights_high(0)
                chunks(act, body)

            @block.vector
            def _(dve):
                def split(ch, par):
                    wait(dve, x_high, ch)
                    nc.vector.tensor_tensor(x_lo[par][:], h2_all[:, span(ch * C, C)], x_hi[par][:].bitcast(fp32),
                                            ALU.subtract).then_inc(x_low.sem, 1)

                def accumulate(ch, par, e):
                    wait(dve, y_ready, ch, e + 1)
                    if e == 0:
                        wait(dve, scaled, ch - 2)
                    else:
                        wait(dve, y_added, ch, e)
                    for t in range(TC):
                        weight = route_w[:, span(ch * (TC * E) + (t * E + e), 1)]
                        if e == 0:
                            last = nc.vector.tensor_scalar(acc[par][:, t, :], y[e % 2][:, t, :], weight, None, ALU.mult)
                        else:
                            last = nc.vector.scalar_tensor_tensor(
                                out=acc[par][:, t, :], in0=y[e % 2][:, t, :], scalar=weight, in1=acc[par][:, t, :],
                                op0=ALU.mult, op1=ALU.add)
                    last.then_inc(y_added.sem, 1)

                def body(ch, par):
                    for e in range(E):
                        for m in range(2):
                            n = 2 * e + m
                            wait(dve, silued, ch, n + 1)
                            wait(dve, y_ready, ch, e - 1)
                            nc.vector.tensor_tensor(hid[e % 2][m][:], act_u[m][:], up[m][1][:], ALU.mult)\
                              .then_inc(hidden.sem, 1)
                        if e > 0:
                            accumulate(ch, par, e - 1)
                        elif not first_chunk(ch):
                            accumulate(ch - 1, 1 - par, E - 1)
                        if e == 3 and not last_chunk(ch):
                            split(ch + 1, 1 - par)
                        if first_chunk(ch) and e % PX == 0 and e // PX + 1 < PIECES:
                            weights_low(e // PX + 1)

                def weights_low(k):
                    for n in range(2):
                        cols = slice(k * PC, (k + 1) * PC)
                        dve.wait_ge(w_high, 2 * k + n + 1)
                        nc.vector.tensor_tensor(w_lo[n][:, cols], piece(n, k), w_hi[n][:, cols].bitcast(fp32),
                                                ALU.subtract).then_inc(w_low, 1)

                split(0, 0)
                weights_low(0)
                chunks(dve, body)
                accumulate(NC - 1, (NC - 1) % 2, E - 1)

            @block.gpsimd
            def _(pool):
                def finish(ch, par):
                    wait(pool, y_added, ch)
                    wait(pool, gate_done, ch)
                    wait(pool, summed, ch - 1)
                    nc.gpsimd.tensor_tensor(
                        gated[:].rearrange("p (b t d) -> p b t d", b=2, t=NT),
                        acc[par][:].rearrange("p (b t) d -> p b t d", b=2),
                        gate[par][:].unsqueeze(2).broadcast_to([P, 2, NT, D]), ALU.mult).then_inc(scaled.sem, 1)
                    wait(pool, scaled, ch)
                    wait(pool, stored, ch - 2)
                    nc.gpsimd.tensor_tensor(result[par][:], gated[:], x_all[:, span(ch * C, C)], ALU.add)\
                      .then_inc(summed.sem, 1)

                def body(ch, par):
                    wait(pool, gate_ready, ch - 2)
                    for n in range(2):
                        last = nc.gpsimd.tensor_tensor(diag[par][:, n, :], ident[:], mod[:, 5, one(ch * 2 + n)].broadcast_to([P, D]), ALU.mult)
                    last.then_inc(diag_ready.sem, 1)
                    if not first_chunk(ch):
                        finish(ch - 1, 1 - par)

                chunks(pool, body)
                finish(NC - 1, (NC - 1) % 2)


_INS = ["x", "w_qkv", "b_qkv", "w1_write", "w2_write", "w1_read", "w2_read", "w_out", "b_out", "decay_logits", "bias_scale"]
_INS = ["L0_attn_" + n for n in _INS] + ["L0_ffn_Wg", "L0_ffn_W1", "L0_ffn_W2", "L0_ffn_W3", "L0_c", "L0_wmod"]


def kernel(**inputs):
    import numpy as _np
    import concourse.bacc as _bacc
    from concourse import mybir as _mybir
    from concourse.bass_utils import run_bass_kernel_spmd as _run

    nc = _bacc.Bacc("TRN2", target_bir_lowering=False, num_devices=1)
    arrays, args = {}, []
    for name in _INS:
        arr = _np.ascontiguousarray(inputs[name])
        arrays[f"in_{name}"] = arr
        args.append(nc.dram_tensor(f"in_{name}", arr.shape, _mybir.dt.from_np(arr.dtype), kind="ExternalInput").ap())
    out = nc.dram_tensor("out", (NB, T, D), _mybir.dt.float32, kind="ExternalOutput").ap()
    build(nc, *args, out)
    return _run(nc, [arrays], core_ids=[0]).results[0]["out"]
```
